# Optimizing a Trainium2 kernel written in Bass

```python
import numpy as np
import jax
import jax.numpy as jnp

def _softmax(x, axis=-1):
    return jax.nn.softmax(x, axis=axis)

def _gelu(x):
    return jax.nn.gelu(x, approximate=True)

def _silu(x):
    return jax.nn.silu(x)

def _sigmoid(x):
    return jax.nn.sigmoid(x)

def _layernorm(x, axis=-1, eps=1e-05):
    m = jnp.mean(x, axis=axis, keepdims=True)
    v = jnp.var(x, axis=axis, keepdims=True)
    return (x - m) / jnp.sqrt(v + eps)

def _scatter_add(tgt, idx, src, axis=0):
    return tgt.at[idx].add(src)

def _segment_sum(src, seg, n):
    return jax.ops.segment_sum(src, seg, n)
kernel_name = 'mk_decoder_preln_d1_seqx_r8_33bf95'

def setup_inputs(seed: int=0):
    np.random.seed(seed)
    _w = jnp.asarray

    def _rec_inputs():
        import jax
        import jax.numpy as jnp
        _rk = jax.random.key(seed)
        x = -4.161e-06 + 1 * jax.random.normal(jax.random.fold_in(_rk, 1), (16, 56, 256), jnp.float32)
        _lenS = 56 - jax.random.randint(jax.random.fold_in(_rk, 7), (16,), 0, max(1, 56 // 4) + 1, jnp.int32)
        _lenS2 = 1500 - jax.random.randint(jax.random.fold_in(_rk, 8), (16,), 0, max(1, 1500 // 4) + 1, jnp.int32)
        _ctx_2048P = jax.random.normal(jax.random.fold_in(_rk, 11), (16, 16, 256), jnp.float32)
        _ctx_2048c = jax.random.dirichlet(jax.random.fold_in(_rk, 511), 0.3 * jnp.ones((16,), jnp.float32), (16, 1500))
        _ctx_2048t = jnp.einsum('bsk,bkd->bsd', _ctx_2048c, _ctx_2048P)
        _ctx_2048t = _ctx_2048t * jax.lax.rsqrt(jnp.mean(jnp.square(_ctx_2048t)) + 1e-12) * 0.953939
        ctx_2048 = -0.000192764 + 0.999654 * (_ctx_2048t + 0.3 * jax.random.normal(jax.random.fold_in(_rk, 611), (16, 1500, 256), jnp.float32))
        return (x, ctx_2048)
    x, ctx_2048 = _rec_inputs()

    def _L0_attn_setup():
        import jax, jax.numpy as jnp
        import numpy as np
        N_HEADS, D_MODEL, D_HEAD, SEQ, BATCH = (16, 256, 128, 256, 1)
        ATTN_SCALE = float(np.sqrt(D_HEAD))
        ROPE_BASE = 10000.0

        def _rope_cos_sin(seq_len, d_head, dtype):
            inv_freq = 1.0 / ROPE_BASE ** (jnp.arange(0, d_head, 2, dtype=jnp.float32) / d_head)
            t = jnp.arange(seq_len, dtype=jnp.float32)
            freqs = t[:, None] * inv_freq[None, :]
            return (jnp.cos(freqs).astype(dtype), jnp.sin(freqs).astype(dtype))

        def _apply_rotary(x, cos, sin):
            B, S, H, D = x.shape
            x2 = x.reshape(B, S, H, D // 2, 2)
            xr, xi = (x2[..., 0], x2[..., 1])
            c = cos[None, :, None, :]
            s = sin[None, :, None, :]
            outr = xr * c - xi * s
            outi = xr * s + xi * c
            return jnp.stack([outr, outi], axis=-1).reshape(B, S, H, D)
        key = jax.random.key(seed)
        ks = jax.random.split(key, 9)
        std = 0.02
        return {'resid_pre': jax.random.normal(ks[0], (BATCH, SEQ, D_MODEL), dtype=jnp.float32), 'W_Q': jax.random.normal(ks[1], (N_HEADS, D_MODEL, D_HEAD), dtype=jnp.float32) * std, 'W_K': jax.random.normal(ks[2], (N_HEADS, D_MODEL, D_HEAD), dtype=jnp.float32) * std, 'W_V': jax.random.normal(ks[3], (N_HEADS, D_MODEL, D_HEAD), dtype=jnp.float32) * std, 'W_O': jax.random.normal(ks[4], (N_HEADS, D_HEAD, D_MODEL), dtype=jnp.float32) * std, 'b_Q': jnp.zeros((N_HEADS, D_HEAD), dtype=jnp.float32), 'b_K': jnp.zeros((N_HEADS, D_HEAD), dtype=jnp.float32), 'b_V': jnp.zeros((N_HEADS, D_HEAD), dtype=jnp.float32), 'b_O': jnp.zeros((D_MODEL,), dtype=jnp.float32)}
    _L0_attn_all = _L0_attn_setup()
    _L0_attn_in = {k: v for k, v in _L0_attn_all.items() if k in ('W_Q', 'W_K', 'W_V', 'W_O', 'b_Q', 'b_K', 'b_V', 'b_O')}
    del _L0_attn_all

    def _L0_xattn_setup():
        import jax, jax.numpy as jnp
        import numpy as np
        FP8_MAX = 448.0
        EPS = 1e-05

        def _fp8_roundtrip(x):
            return x.astype(jnp.float8_e4m3fn).astype(jnp.float32)

        def _div_clamp_fp8(x, scale):
            y = jnp.clip(x.astype(jnp.float32) / scale, -FP8_MAX, FP8_MAX)
            y = y.astype(jnp.bfloat16).astype(jnp.float32)
            return _fp8_roundtrip(y)

        def _ln(x, w, b):
            mu = jnp.mean(x, axis=-1, keepdims=True)
            var = jnp.mean(jnp.square(x - mu), axis=-1, keepdims=True)
            return (x - mu) * jax.lax.rsqrt(var + EPS) * w + b

        def _fp8_linear_pertensor(x, wq, w_scale, in_scale):
            xq = _div_clamp_fp8(x, in_scale)
            return jnp.einsum('bsi,oi->bso', xq * in_scale, wq) * w_scale

        def _gqa(q, k, v):
            scale = 1.0 / np.sqrt(q.shape[-1])
            scores = jnp.einsum('bsghd,btgd->bghst', q, k) * scale
            p = jax.nn.softmax(scores, axis=-1)
            return jnp.einsum('bghst,btgd->bsghd', p, v)
        key = jax.random.key(seed)
        ks = jax.random.split(key, 8)
        B, S, SC, H, NH, G, D = (2, 256, 64, 256, 16, 8, 128)

        def qw(k, out_f, in_f):
            w = jax.random.normal(k, (out_f, in_f), jnp.float32) * 0.02
            sc = jnp.max(jnp.abs(w)) / FP8_MAX
            return (_fp8_roundtrip(w / sc), sc.astype(jnp.float32))
        wq, wq_s = qw(ks[0], NH * D, H)
        wqx, wqx_s = qw(ks[1], NH * D, H)
        wk, wk_s = qw(ks[2], G * D, H)
        wv, wv_s = qw(ks[3], G * D, H)
        wproj, wp_s = qw(ks[4], H, 2 * NH * D)
        return {'hidden_states': jax.random.normal(ks[5], (B, S, H), jnp.float32), 'cond': jax.random.normal(ks[6], (B, SC, H), jnp.float32), 'ln_w': jnp.ones((H,), jnp.float32), 'ln_b': jnp.zeros((H,), jnp.float32), 'wq': wq, 'wq_scale': wq_s, 'q_in_scale': jnp.full((H,), 0.05, jnp.float32), 'wqx': wqx, 'wqx_scale': wqx_s, 'qx_in_scale': jnp.full((H,), 0.05, jnp.float32), 'wk': wk, 'wk_scale': wk_s, 'k_in_scale': jnp.full((H,), 0.05, jnp.float32), 'wv': wv, 'wv_scale': wv_s, 'v_in_scale': jnp.full((H,), 0.05, jnp.float32), 'w_kv_x': jax.random.normal(ks[7], (2 * G * D, H), jnp.float32) * 0.02, 'qln_w': jnp.ones((D,), jnp.float32), 'qln_b': jnp.zeros((D,), jnp.float32), 'kln_w': jnp.ones((D,), jnp.float32), 'kln_b': jnp.zeros((D,), jnp.float32), 'qxln_w': jnp.ones((D,), jnp.float32), 'qxln_b': jnp.zeros((D,), jnp.float32), 'kxln_w': jnp.ones((D,), jnp.float32), 'kxln_b': jnp.zeros((D,), jnp.float32), 'wproj': wproj, 'proj_w_scale': wp_s, 'proj_in_scale': jnp.asarray(0.05, jnp.float32), 'proj_smooth': jnp.full((2 * NH * D,), 0.05, jnp.float32)}
    _L0_xattn_all = _L0_xattn_setup()
    _L0_xattn_in = {k: v for k, v in _L0_xattn_all.items() if k in ('ln_w', 'ln_b', 'wq', 'wq_scale', 'q_in_scale', 'wqx', 'wqx_scale', 'qx_in_scale', 'wk', 'wk_scale', 'k_in_scale', 'wv', 'wv_scale', 'v_in_scale', 'w_kv_x', 'qln_w', 'qln_b', 'kln_w', 'kln_b', 'qxln_w', 'qxln_b', 'kxln_w', 'kxln_b', 'wproj', 'proj_w_scale', 'proj_in_scale', 'proj_smooth')}
    del _L0_xattn_all

    def _L0_ffn_setup():
        import jax, jax.numpy as jnp
        import numpy as np
        ALPHA = 1.702
        LIMIT = 7.0
        EPS = 1e-05
        TOP_K = 4
        key = jax.random.key(seed)
        ks = jax.random.split(key, 8)
        B, S, H, I, E = (2, 64, 256, 256, 16)
        return {'x': jax.random.normal(ks[0], (B, S, H), jnp.float32), 'norm_w': jnp.ones((H,), jnp.float32), 'gate_w': jax.random.normal(ks[1], (E, H), jnp.float32) * 0.02, 'gate_b': jax.random.normal(ks[2], (E,), jnp.float32) * 0.02, 'w1': jax.random.normal(ks[3], (E, 2 * I, H), jnp.float32) * 0.02, 'b1': jax.random.normal(ks[4], (E, 2 * I), jnp.float32) * 0.02, 'w2': jax.random.normal(ks[5], (E, H, I), jnp.float32) * 0.02, 'b2': jax.random.normal(ks[6], (E, H), jnp.float32) * 0.02}
    _L0_ffn_all = _L0_ffn_setup()
    _L0_ffn_in = {k: v for k, v in _L0_ffn_all.items() if k in ('norm_w', 'gate_w', 'gate_b', 'w1', 'b1', 'w2', 'b2')}
    del _L0_ffn_all
    return {'x': x, 'ctx_2048': ctx_2048, 'L0_attn_W_Q': _L0_attn_in['W_Q'], 'L0_attn_W_K': _L0_attn_in['W_K'], 'L0_attn_W_V': _L0_attn_in['W_V'], 'L0_attn_W_O': _L0_attn_in['W_O'], 'L0_attn_b_Q': _L0_attn_in['b_Q'], 'L0_attn_b_K': _L0_attn_in['b_K'], 'L0_attn_b_V': _L0_attn_in['b_V'], 'L0_attn_b_O': _L0_attn_in['b_O'], 'L0_xattn_ln_w': _L0_xattn_in['ln_w'], 'L0_xattn_ln_b': _L0_xattn_in['ln_b'], 'L0_xattn_wq': _L0_xattn_in['wq'], 'L0_xattn_wq_scale': _L0_xattn_in['wq_scale'], 'L0_xattn_q_in_scale': _L0_xattn_in['q_in_scale'], 'L0_xattn_wqx': _L0_xattn_in['wqx'], 'L0_xattn_wqx_scale': _L0_xattn_in['wqx_scale'], 'L0_xattn_qx_in_scale': _L0_xattn_in['qx_in_scale'], 'L0_xattn_wk': _L0_xattn_in['wk'], 'L0_xattn_wk_scale': _L0_xattn_in['wk_scale'], 'L0_xattn_k_in_scale': _L0_xattn_in['k_in_scale'], 'L0_xattn_wv': _L0_xattn_in['wv'], 'L0_xattn_wv_scale': _L0_xattn_in['wv_scale'], 'L0_xattn_v_in_scale': _L0_xattn_in['v_in_scale'], 'L0_xattn_w_kv_x': _L0_xattn_in['w_kv_x'], 'L0_xattn_qln_w': _L0_xattn_in['qln_w'], 'L0_xattn_qln_b': _L0_xattn_in['qln_b'], 'L0_xattn_kln_w': _L0_xattn_in['kln_w'], 'L0_xattn_kln_b': _L0_xattn_in['kln_b'], 'L0_xattn_qxln_w': _L0_xattn_in['qxln_w'], 'L0_xattn_qxln_b': _L0_xattn_in['qxln_b'], 'L0_xattn_kxln_w': _L0_xattn_in['kxln_w'], 'L0_xattn_kxln_b': _L0_xattn_in['kxln_b'], 'L0_xattn_wproj': _L0_xattn_in['wproj'], 'L0_xattn_proj_w_scale': _L0_xattn_in['proj_w_scale'], 'L0_xattn_proj_in_scale': _L0_xattn_in['proj_in_scale'], 'L0_xattn_proj_smooth': _L0_xattn_in['proj_smooth'], 'L0_ffn_norm_w': _L0_ffn_in['norm_w'], 'L0_ffn_gate_w': _L0_ffn_in['gate_w'], 'L0_ffn_gate_b': _L0_ffn_in['gate_b'], 'L0_ffn_w1': _L0_ffn_in['w1'], 'L0_ffn_b1': _L0_ffn_in['b1'], 'L0_ffn_w2': _L0_ffn_in['w2'], 'L0_ffn_b2': _L0_ffn_in['b2']}

def reference(x, ctx_2048, L0_attn_W_Q, L0_attn_W_K, L0_attn_W_V, L0_attn_W_O, L0_attn_b_Q, L0_attn_b_K, L0_attn_b_V, L0_attn_b_O, L0_xattn_ln_w, L0_xattn_ln_b, L0_xattn_wq, L0_xattn_wq_scale, L0_xattn_q_in_scale, L0_xattn_wqx, L0_xattn_wqx_scale, L0_xattn_qx_in_scale, L0_xattn_wk, L0_xattn_wk_scale, L0_xattn_k_in_scale, L0_xattn_wv, L0_xattn_wv_scale, L0_xattn_v_in_scale, L0_xattn_w_kv_x, L0_xattn_qln_w, L0_xattn_qln_b, L0_xattn_kln_w, L0_xattn_kln_b, L0_xattn_qxln_w, L0_xattn_qxln_b, L0_xattn_kxln_w, L0_xattn_kxln_b, L0_xattn_wproj, L0_xattn_proj_w_scale, L0_xattn_proj_in_scale, L0_xattn_proj_smooth, L0_ffn_norm_w, L0_ffn_gate_w, L0_ffn_gate_b, L0_ffn_w1, L0_ffn_b1, L0_ffn_w2, L0_ffn_b2):
    import jax
    import jax.numpy as jnp

    def _L0_attn_ref(resid_pre, W_Q, W_K, W_V, W_O, b_Q, b_K, b_V, b_O):
        import jax, jax.numpy as jnp
        import numpy as np
        N_HEADS, D_MODEL, D_HEAD, SEQ, BATCH = (16, 256, 128, 256, 1)
        ATTN_SCALE = float(np.sqrt(D_HEAD))
        ROPE_BASE = 10000.0

        def _rope_cos_sin(seq_len, d_head, dtype):
            inv_freq = 1.0 / ROPE_BASE ** (jnp.arange(0, d_head, 2, dtype=jnp.float32) / d_head)
            t = jnp.arange(seq_len, dtype=jnp.float32)
            freqs = t[:, None] * inv_freq[None, :]
            return (jnp.cos(freqs).astype(dtype), jnp.sin(freqs).astype(dtype))

        def _apply_rotary(x, cos, sin):
            B, S, H, D = x.shape
            x2 = x.reshape(B, S, H, D // 2, 2)
            xr, xi = (x2[..., 0], x2[..., 1])
            c = cos[None, :, None, :]
            s = sin[None, :, None, :]
            outr = xr * c - xi * s
            outi = xr * s + xi * c
            return jnp.stack([outr, outi], axis=-1).reshape(B, S, H, D)
        B, S, _ = resid_pre.shape
        q = jnp.einsum('bpd,hde->bphe', resid_pre, W_Q) + b_Q
        k = jnp.einsum('bpd,hde->bphe', resid_pre, W_K) + b_K
        v = jnp.einsum('bpd,hde->bphe', resid_pre, W_V) + b_V
        cos, sin = _rope_cos_sin(S, D_HEAD, q.dtype)
        q = _apply_rotary(q, cos, sin)
        k = _apply_rotary(k, cos, sin)
        scores = jnp.einsum('bqhd,bkhd->bhqk', q, k) / ATTN_SCALE
        causal = jnp.tril(jnp.ones((S, S), dtype=bool))
        scores = jnp.where(causal[None, None], scores, jnp.zeros((), dtype=scores.dtype))
        max_v = jnp.max(jnp.abs(scores), axis=-1, keepdims=True)
        sgn = jnp.sign(scores)
        attn_w = sgn * jnp.exp(sgn * scores - max_v)
        attn = attn_w / (jnp.sum(jnp.abs(attn_w), axis=-1, keepdims=True) + 1e-06)
        z = jnp.einsum('bkhd,bhqk->bqhd', v, attn)
        out = jnp.einsum('bqhd,hdm->bqm', z, W_O) + b_O
        return out

    def _L0_xattn_ref(hidden_states, cond, ln_w, ln_b, wq, wq_scale, q_in_scale, wqx, wqx_scale, qx_in_scale, wk, wk_scale, k_in_scale, wv, wv_scale, v_in_scale, w_kv_x, qln_w, qln_b, kln_w, kln_b, qxln_w, qxln_b, kxln_w, kxln_b, wproj, proj_w_scale, proj_in_scale, proj_smooth):
        import jax, jax.numpy as jnp
        import numpy as np
        FP8_MAX = 448.0
        EPS = 1e-05

        def _fp8_roundtrip(x):
            return x.astype(jnp.float8_e4m3fn).astype(jnp.float32)

        def _div_clamp_fp8(x, scale):
            y = jnp.clip(x.astype(jnp.float32) / scale, -FP8_MAX, FP8_MAX)
            y = y.astype(jnp.bfloat16).astype(jnp.float32)
            return _fp8_roundtrip(y)

        def _ln(x, w, b):
            mu = jnp.mean(x, axis=-1, keepdims=True)
            var = jnp.mean(jnp.square(x - mu), axis=-1, keepdims=True)
            return (x - mu) * jax.lax.rsqrt(var + EPS) * w + b

        def _fp8_linear_pertensor(x, wq, w_scale, in_scale):
            xq = _div_clamp_fp8(x, in_scale)
            return jnp.einsum('bsi,oi->bso', xq * in_scale, wq) * w_scale

        def _gqa(q, k, v):
            scale = 1.0 / np.sqrt(q.shape[-1])
            scores = jnp.einsum('bsghd,btgd->bghst', q, k) * scale
            p = jax.nn.softmax(scores, axis=-1)
            return jnp.einsum('bghst,btgd->bsghd', p, v)
        b, s, _ = hidden_states.shape
        sc = cond.shape[1]
        d = qln_w.shape[0]
        nh = wq.shape[0] // d
        g = wk.shape[0] // d
        hpg = nh // g
        ln_out = _ln(hidden_states, ln_w, ln_b)
        q = _fp8_linear_pertensor(ln_out, wq, wq_scale, q_in_scale).reshape(b, s, g, hpg, d)
        q = _ln(q, qln_w, qln_b)
        k = _fp8_linear_pertensor(ln_out, wk, wk_scale, k_in_scale).reshape(b, s, g, d)
        k = _ln(k, kln_w, kln_b)
        v = _fp8_linear_pertensor(ln_out, wv, wv_scale, v_in_scale).reshape(b, s, g, d)
        core = _gqa(q, k, v).reshape(b, s, nh * d)
        qx = _fp8_linear_pertensor(ln_out, wqx, wqx_scale, qx_in_scale).reshape(b, s, g, hpg, d)
        qx = _ln(qx, qxln_w, qxln_b)
        kvx = jnp.einsum('bsi,oi->bso', cond, w_kv_x)
        kx, vx = jnp.split(kvx, 2, axis=-1)
        kx = _ln(kx.reshape(b, sc, g, d), kxln_w, kxln_b)
        vx = vx.reshape(b, sc, g, d)
        xout = _gqa(qx, kx, vx).reshape(b, s, nh * d)
        cat = jnp.concatenate([core, xout], axis=-1)
        catq = _div_clamp_fp8(cat, proj_smooth)
        return jnp.einsum('bsi,oi->bso', catq, wproj) * (proj_in_scale * proj_w_scale)

    def _L0_ffn_ref(x, norm_w, gate_w, gate_b, w1, b1, w2, b2):
        import jax, jax.numpy as jnp
        import numpy as np
        ALPHA = 1.702
        LIMIT = 7.0
        EPS = 1e-05
        TOP_K = 4
        B, S, H = x.shape
        M = B * S
        E = gate_w.shape[0]
        xf = x.reshape(M, H)
        t = xf * jax.lax.rsqrt(jnp.mean(xf * xf, axis=-1, keepdims=True) + EPS) * norm_w
        logits = t @ gate_w.T + gate_b
        vals, idx = jax.lax.top_k(logits, TOP_K)
        gates_k = jax.nn.softmax(vals, axis=-1)
        G = jnp.zeros((M, E), x.dtype).at[jnp.arange(M)[:, None], idx].set(gates_k)
        h = jnp.einsum('mh,eoh->emo', t, w1) + b1[:, None, :]
        a = jnp.minimum(h[..., ::2], LIMIT)
        b = jnp.clip(h[..., 1::2], -LIMIT, LIMIT)
        act = a * jax.nn.sigmoid(ALPHA * a) * (b + 1.0)
        y = jnp.einsum('emi,edi->emd', act, w2) + b2[:, None, :]
        delta = jnp.einsum('me,emd->md', G, y)
        return x + delta.reshape(B, S, H)
    x = x + _L0_attn_ref(_layernorm(x, axis=-1), L0_attn_W_Q, L0_attn_W_K, L0_attn_W_V, L0_attn_W_O, L0_attn_b_Q, L0_attn_b_K, L0_attn_b_V, L0_attn_b_O)
    x = x + _L0_xattn_ref(_layernorm(x, axis=-1), ctx_2048, L0_xattn_ln_w, L0_xattn_ln_b, L0_xattn_wq, L0_xattn_wq_scale, L0_xattn_q_in_scale, L0_xattn_wqx, L0_xattn_wqx_scale, L0_xattn_qx_in_scale, L0_xattn_wk, L0_xattn_wk_scale, L0_xattn_k_in_scale, L0_xattn_wv, L0_xattn_wv_scale, L0_xattn_v_in_scale, L0_xattn_w_kv_x, L0_xattn_qln_w, L0_xattn_qln_b, L0_xattn_kln_w, L0_xattn_kln_b, L0_xattn_qxln_w, L0_xattn_qxln_b, L0_xattn_kxln_w, L0_xattn_kxln_b, L0_xattn_wproj, L0_xattn_proj_w_scale, L0_xattn_proj_in_scale, L0_xattn_proj_smooth)
    x = x + _L0_ffn_ref(_layernorm(x, axis=-1), L0_ffn_norm_w, L0_ffn_gate_w, L0_ffn_gate_b, L0_ffn_w1, L0_ffn_b1, L0_ffn_w2, L0_ffn_b2)
    return x

_drawn_inputs = setup_inputs


def setup_inputs(seed=0):
    import zlib

    import numpy as np

    out = dict(_drawn_inputs(seed))
    spreads = {'L0_attn_b_Q': (0.0, 0.1),
     'L0_attn_b_K': (0.0, 0.1),
     'L0_attn_b_V': (0.0, 0.1),
     'L0_attn_b_O': (0.0, 0.1),
     'L0_xattn_ln_w': (1.0, 0.555),
     'L0_xattn_ln_b': (0.0, 0.1),
     'L0_xattn_q_in_scale': (0.05000000074505806, 0.6),
     'L0_xattn_qx_in_scale': (0.05000000074505806, 0.6),
     'L0_xattn_k_in_scale': (0.05000000074505806, 0.6),
     'L0_xattn_v_in_scale': (0.05000000074505806, 0.6),
     'L0_xattn_qln_w': (1.0, 0.6),
     'L0_xattn_qln_b': (0.0, 0.8),
     'L0_xattn_kln_w': (1.0, 0.6),
     'L0_xattn_kln_b': (0.0, 0.8),
     'L0_xattn_qxln_w': (1.0, 0.6),
     'L0_xattn_qxln_b': (0.0, 0.8),
     'L0_xattn_kxln_w': (1.0, 0.6),
     'L0_xattn_kxln_b': (0.0, 0.8),
     'L0_xattn_proj_smooth': (0.05000000074505806, 0.2),
     'L0_ffn_norm_w': (1.0, 0.6)}
    factors = {'L0_ffn_gate_w': 3.954,
     'L0_ffn_gate_b': 8.0,
     'L0_ffn_w1': 3.662,
     'L0_ffn_b1': 8.0,
     'L0_ffn_w2': 3.56,
     'L0_ffn_b2': 8.0}
    for name, (base, spread) in spreads.items():
        noise = np.random.default_rng([zlib.crc32(name.encode()), seed]).standard_normal(out[name].shape)
        drawn = base * np.exp(spread * noise) if base else spread * noise
        out[name] = jnp.asarray(drawn.astype(out[name].dtype))
    for name, factor in factors.items():
        out[name] = (out[name] * factor).astype(out[name].dtype)
    return out
```

```python
from contextlib import ExitStack

import numpy as np

import concourse.bass as bass
from concourse import mybir

F32 = mybir.dt.float32
F32R = mybir.dt.float32r
BF16 = mybir.dt.bfloat16
U16 = mybir.dt.uint16
ALU = mybir.AluOpType
ACT = mybir.ActivationFunctionType
AX_X = mybir.AxisListType.X

B, S, C = 16, 56, 256
SC = 1500
NH, G, D = 16, 8, 128
HPG = NH // G
KC = C // 128
PAIRS = B // 2
T2 = 2 * S
N = B * S
HH = 8
CH = 512
TT_C, NT_C = 125, 12
E, I, TOPK = 16, 256, 4
SCALE = float(1.0 / np.sqrt(D))
EPS = 1e-5
FP8_MAX = 448.0
NEG = -1.0e30
BN = 6

V_LNW, V_LNB, V_QS, V_KS, V_QXS, V_VS, V_NW = 0, 2, 4, 6, 8, 10, 12
V_QLW, V_QLB, V_KLW, V_KLB, V_QXLW, V_QXLB, V_KXLW, V_KXLB = 14, 15, 16, 17, 18, 19, 20, 21
V_SQ, V_SK, V_SQX, V_SV, V_SPW, V_SPI = 22, 23, 24, 25, 26, 27
V_SM = 28
NV = V_SM + 2 * NH
R_BQKV, R_BO, R_GB = 0, 2 * 6 * CH, 2 * 6 * CH + C
NR = R_GB + E


class Phase(ExitStack):

    def __init__(self, nc):
        super().__init__()
        self.nc, self.sems = nc, []

    def clear(self):
        self.nc.clear_and_free_semaphores(self.sems)
        self.nc.all_engine_barrier()


class Signal:

    def __init__(self, nc, ctx, name, per=1, primed=0):
        self.sem = nc.alloc_semaphore(name)
        ctx.sems.append(self.sem)
        self.per, self.primed = per, primed

    def at(self, i, k):
        return i * self.per + (k + self.primed)


class Chain:

    def __init__(self, eng, step):
        self.eng, self.step, self.i, self.n = eng, step, 0, 0

    def round(self, i):
        self.i, self.n = i, 0

    def __call__(self, ins):
        self.n += 1
        ins.then_inc(self.step.sem, 1)
        self.eng.wait_ge(self.step.sem, self.step.at(self.i, self.n))

    def end(self):
        assert self.n == self.step.per, (self.step.sem, self.n)


def quantise(dve, link, out, y, work, m):
    link(dve.tensor_scalar(y, y, FP8_MAX, -FP8_MAX, ALU.min, ALU.max))
    link(dve.tensor_scalar(m.bitcast(U16), y.bitcast(U16), 0x7F80, None, ALU.bitwise_and))
    link(dve.tensor_scalar(m, m, 2.0 ** -6, 24.0, ALU.max, ALU.mult))
    link(dve.tensor_tensor(work, y, m, ALU.add))
    return dve.tensor_tensor(out, work, m, ALU.subtract)


def normalise_phase(nc, k, mode):
    with Phase(nc) as ctx:
        ctx.callback(ctx.clear)
        def sb(name, shape, dt=F32):
            return ctx.enter_context(nc.sbuf_tensor(f"{mode}_{name}", shape, dt))

        stats = sb("stats", [T2, PAIRS, BN])
        mv = sb("mv", [T2, PAIRS, 2])
        ve = sb("ve", [T2, PAIRS])
        rstd = sb("rstd", [T2, PAIRS])
        shift = sb("shift", [T2, PAIRS])
        mhalf = sb("mhalf", [T2, PAIRS])
        xn = sb("xn", [T2, PAIRS, C])
        xt = [ctx.enter_context(nc.psum_tensor(f"{mode}_xt{j}", [128, 4, 128], F32)) for j in range(4)]
        twice = mode != "attn"
        ready = Signal(nc, ctx, mode + "_ready")
        dve_step = Signal(nc, ctx, mode + "_dve_step")
        pow_in = Signal(nc, ctx, mode + "_pow_in")
        pow_out = Signal(nc, ctx, mode + "_pow_out")
        normed = Signal(nc, ctx, mode + "_normed")
        turned = Signal(nc, ctx, mode + "_turned")
        copied = Signal(nc, ctx, mode + "_copied")
        if mode == "xattn":
            lnt = sb("lnt", [128, KC, N])
            y = sb("y", [128, KC, N], BF16)
            m = sb("m", [128, KC, N], BF16)
            work = sb("work", [128, KC, N], BF16)
            rin = sb("rin", [128, 8])
        with nc.Block() as block:
            @block.gpsimd
            def _(pool):
                pool.memset(mhalf[:], -0.5).then_inc(ready.sem, 1)
                pool.wait_ge(ready.sem, 1)
                for r in range(2 if twice else 1):
                    pool.wait_ge(pow_in.sem, r + 1)
                    pool.tensor_tensor(rstd[:], ve[:], mhalf[:], ALU.pow).then_inc(pow_out.sem, 1)

            @block.vector
            def _(dve):
                link = Chain(dve, dve_step)

                def norm(r, dst, src, scale_only=False):
                    for p in range(PAIRS):
                        ins = dve.bn_stats(stats[:, p, :], src[:, p, :])
                    link(ins)
                    for p in range(PAIRS):
                        ins = dve.bn_aggr(mv[:, p, :], stats[:, p, :])
                    link(ins)
                    if scale_only:
                        link(dve.tensor_tensor(shift[:], mv[:, :, 0], mv[:, :, 0], ALU.mult))
                        link(dve.tensor_tensor(ve[:], mv[:, :, 1], shift[:], ALU.add))
                        link(dve.tensor_scalar(ve[:], ve[:], EPS, None, ALU.add))
                    else:
                        link(dve.tensor_scalar(ve[:], mv[:, :, 1], EPS, None, ALU.add))
                    dve.sem_inc(pow_in.sem, 1)
                    dve.wait_ge(pow_out.sem, r + 1)
                    if not scale_only:
                        link(dve.scalar_tensor_tensor(shift[:], mv[:, :, 0], -1.0, rstd[:], ALU.mult, ALU.mult))
                    for p in range(PAIRS):
                        if scale_only:
                            ins = dve.tensor_scalar(dst[:, p, :], src[:, p, :], rstd[:, p:p + 1], None, ALU.mult)
                        else:
                            ins = dve.tensor_scalar(dst[:, p, :], src[:, p, :], rstd[:, p:p + 1],
                                                    shift[:, p:p + 1], ALU.mult, ALU.add)
                    link(ins)

                if mode == "attn":
                    norm(0, xn, k.x)
                    dve.sem_inc(normed.sem, 1)
                    for p in range(PAIRS):
                        ins = dve.tensor_tensor(k.x[:, p, :], k.x[:, p, :], k.rows[0:T2, R_BO:R_BO + C], ALU.add)
                    link(ins)
                elif mode == "xattn":
                    norm(0, xn, k.x)
                    norm(1, xn, xn)
                    dve.sem_inc(normed.sem, 1)
                    for n, v in enumerate((V_QS, V_KS, V_QXS, V_VS)):
                        ins = dve.reciprocal(rin[:, 2 * n:2 * n + 2], k.vec[:, v:v + 2])
                    link(ins)
                    dve.wait_ge(copied.sem, 4)
                    for n in range(4):
                        for c in range(KC):
                            ins = dve.tensor_scalar(y[:, c, :], lnt[:, c, :], rin[:, 2 * n + c:2 * n + c + 1],
                                                    None, ALU.mult)
                        link(ins)
                        link(quantise(dve, link, k.xq[:, n], y[:], work[:], m[:]))
                else:
                    norm(0, k.xh, k.x)
                    norm(1, xn, k.xh, scale_only=True)
                    dve.sem_inc(normed.sem, 1)

            @block.tensor
            def _(pe):
                pe.wait_ge(normed.sem, 1)
                for j in range(4):
                    for p in range(4):
                        pair, c = 4 * (j % 2) + p, j // 2
                        ins = pe.transpose(xt[j][:, p, 0:T2], xn[:, pair, c * 128:(c + 1) * 128],
                                           k.ident[0:T2, 0:T2])
                    ins.then_inc(turned.sem, 1)

            @block.scalar
            def _(act):
                for j in range(4):
                    act.wait_ge(turned.sem, j + 1)
                    c, t0 = j // 2, (j % 2) * 4 * T2
                    src = xt[j][:, :, 0:T2]
                    dst = (lnt if mode == "xattn" else k.xT)[:, c, t0:t0 + 4 * T2].rearrange("p (a b) -> p a b", a=4)
                    if mode == "attn":
                        ins = act.activation(dst, src, ACT.Copy)
                    elif mode == "xattn":
                        ins = act.activation(dst, src, ACT.Identity, scale=k.vec[:, V_LNW + c:V_LNW + c + 1],
                                             bias=k.vec[:, V_LNB + c:V_LNB + c + 1])
                    else:
                        ins = act.mul(dst, src, k.vec[:, V_NW + c:V_NW + c + 1])
                    ins.then_inc(copied.sem, 1)


def attn_half(nc, k, hh):
    NTC = 4
    with Phase(nc) as ctx:
        ctx.callback(ctx.clear)
        def sb(name, shape, dt=F32):
            return ctx.enter_context(nc.sbuf_tensor(f"a{hh}_{name}", shape, dt))

        def bank(name, shape):
            return ctx.enter_context(nc.psum_tensor(f"a{hh}_{name}", shape, F32))

        def sig(name, per=1, primed=0):
            return Signal(nc, ctx, f"a{hh}_{name}", per, primed)

        w_raw = sb("w_raw", [128, 2, KC, CH])
        w_hi = sb("w_hi", [128, 6, KC, CH], F32R)
        w_lo = sb("w_lo", [128, 6, KC, CH], F32R)
        wo = sb("wo", [128, HH, C])
        bias = k.rows
        x_hi = sb("x_hi", [128, KC, T2], F32R)
        x_lo = sb("x_lo", [128, KC, T2], F32R)
        biased = [sb(f"biased{j}", [T2, CH]) for j in range(2)]
        crossed = [sb(f"crossed{j}", [T2, CH]) for j in range(2)]
        tok = [sb(f"tok{j}", [T2, CH]) for j in range(2)]
        qkT = sb("qkT", [128, 2 * HH, T2])
        v = sb("v", [T2, HH, D])
        sc = [sb(f"sc{j}", [T2, 4, T2]) for j in range(2)]
        ab = [sb(f"ab{j}", [T2, 4, T2]) for j in range(2)]
        sg = [sb(f"sg{j}", [T2, 4, T2]) for j in range(2)]
        mx = sb("mx", [T2, 2, 4])
        sm = sb("sm", [T2, 2, 4])
        aT = [sb(f"aT{j}", [T2, 4, T2]) for j in range(2)]
        zT = sb("zT", [128, HH, T2])
        pj = [bank(f"pj{j}", [T2, CH]) for j in range(2)]
        tp = [bank(f"tp{j}", [128, 4, T2]) for j in range(2)]
        ps = [bank(f"ps{j}", [T2, 4, T2]) for j in range(2)]
        pz = bank("pz", [128, 4, T2])
        po = bank("po", [T2, C])

        w_loaded, wo_loaded, w_hi_done, w_lo_done = sig("w_loaded"), sig("wo_loaded"), sig("w_hi_done"), sig("w_lo_done")
        xhi_done, xlo_done = sig("xhi_done"), sig("xlo_done")
        projected = sig("projected", 6, 1)
        proj_read = sig("proj_read", 6, 1)
        bias_done = sig("bias_done", NTC)
        cross_done = sig("cross_done", NTC)
        tok_done = sig("tok_done", NTC)
        turned = sig("turned", NTC + 2, 1)
        turned_read = sig("turned_read", NTC + 2, 1)
        scored = sig("scored", 2, 1)
        masked = sig("masked", 2, 1)
        signed = sig("signed", 2)
        shifted = sig("shifted", 2)
        exped = sig("exped", 2)
        weighed = sig("weighed", 2)
        mixed = sig("mixed", 2, 1)
        mixed_read = sig("mixed_read", 2, 1)
        summed = sig("summed", 1, 1)
        summed_read = sig("summed_read", 1, 1)
        dve_step = sig("dve_step", 10)

        with nc.Block() as block:
            @block.sync
            def _(sp):
                for c in range(6):
                    if c >= 2:
                        sp.wait_ge(w_lo_done.sem, c - 1)
                    sp.dma_start(w_raw[:, c % 2], k.d_attn_w[hh, c]).then_inc(w_loaded.sem, 16)
                    if c == 0:
                        sp.dma_start(wo[:], k.d_attn_wo[:, hh * HH:(hh + 1) * HH, :]).then_inc(wo_loaded.sem, 16)
                    sp.wait_ge(w_loaded.sem, 16 * (c + 1))

            @block.scalar
            def _(act):
                for c in range(6):
                    act.wait_ge(w_loaded.sem, 16 * (c + 1))
                    act.activation(w_hi[:, c], w_raw[:, c % 2], ACT.Copy).then_inc(w_hi_done.sem, 1)
                act.sem_inc(turned_read.sem, 1)
                act.sem_inc(mixed_read.sem, 1)
                with act.Fori(0, PAIRS) as i:
                    act.wait_ge(projected.sem, projected.at(i, 0))
                    act.activation(x_hi[:], k.xT[:, :, bass.ds(i * T2, T2)], ACT.Copy).then_inc(xhi_done.sem, 1)
                    act.wait_ge(scored.sem, scored.at(i, 0))
                    for c in range(NTC):
                        act.wait_ge(turned.sem, turned.at(i, c + 1))
                        act.activation(qkT[:, 4 * c:4 * c + 4, :], tp[c % 2][:], ACT.Copy).then_inc(turned_read.sem, 1)
                    for s in range(2):
                        act.wait_ge(masked.sem, masked.at(i, s + 1))
                        act.activation(ab[s][:], sc[s][:], ACT.Abs)
                        act.activation(sg[s][:], sc[s][:], ACT.Sign).then_inc(signed.sem, 1)
                    for s in range(2):
                        act.wait_ge(shifted.sem, shifted.at(i, s + 1))
                        act.activation(ab[s][:], ab[s][:], ACT.Exp).then_inc(exped.sem, 1)
                    for s in range(2):
                        act.wait_ge(turned.sem, turned.at(i, NTC + s + 1))
                        act.activation(aT[s][:], tp[s][0:T2], ACT.Copy).then_inc(turned_read.sem, 1)
                        if s == 0:
                            act.wait_ge(summed.sem, summed.at(i, 0))
                        act.wait_ge(mixed.sem, mixed.at(i, s + 1))
                        act.activation(zT[:, 4 * s:4 * s + 4, :], pz[:], ACT.Copy).then_inc(mixed_read.sem, 1)

            @block.gpsimd
            def _(pool):
                for c in range(6):
                    pool.wait_ge(w_hi_done.sem, c + 1)
                    pool.tensor_tensor(w_lo[:, c], w_raw[:, c % 2], w_hi[:, c].bitcast(F32),
                                       ALU.subtract).then_inc(w_lo_done.sem, 1)
                with pool.Fori(0, PAIRS) as i:
                    pool.wait_ge(xhi_done.sem, xhi_done.at(i, 1))
                    pool.tensor_tensor(x_lo[:], k.xT[:, :, bass.ds(i * T2, T2)], x_hi[:].bitcast(F32),
                                       ALU.subtract).then_inc(xlo_done.sem, 1)
                    for c in range(NTC):
                        pool.wait_ge(bias_done.sem, bias_done.at(i, c + 1))
                        src = biased[c % 2][:].rearrange("p (h e two) -> p h e two", h=4, two=2)
                        dst = crossed[c % 2][:].rearrange("p (h e two) -> p h e two", h=4, two=2)
                        sin = k.sin[:, 0:D // 2].unsqueeze(1).to_broadcast([T2, 4, D // 2])
                        nsin = k.sin[:, D // 2:D].unsqueeze(1).to_broadcast([T2, 4, D // 2])
                        pool.tensor_tensor(dst[:, :, :, 0], src[:, :, :, 1], nsin, ALU.mult)
                        pool.tensor_tensor(dst[:, :, :, 1], src[:, :, :, 0], sin, ALU.mult).then_inc(cross_done.sem, 1)

            @block.vector
            def _(dve):
                link = Chain(dve, dve_step)
                for s in (proj_read, masked, summed_read):
                    dve.sem_inc(s.sem, 1)
                with dve.Fori(0, PAIRS) as i:
                    link.round(i)

                    def add_bias(c):
                        dve.wait_ge(projected.sem, projected.at(i, c + 1))
                        out = biased[c % 2][:] if c < NTC else v[:, 4 * (c - NTC):4 * (c - NTC) + 4, :].rearrange("p h e -> p (h e)")
                        if c == NTC:
                            dve.wait_ge(mixed.sem, mixed.at(i, 0))
                        at = R_BQKV + (hh * 6 + c) * CH
                        return dve.tensor_tensor(out, pj[c % 2][:], bias[0:T2, at:at + CH], ALU.add)

                    for c in range(NTC):
                        ins = add_bias(c)
                        ins.then_inc(bias_done.sem, 1)
                        dve.wait_ge(bias_done.sem, bias_done.at(i, c + 1))
                        dve.wait_ge(turned.sem, turned.at(i, max(c - 1, 0)))
                        cos = k.cos[:, :].unsqueeze(1).to_broadcast([T2, 4, D])
                        t3 = tok[c % 2][:].rearrange("p (h e) -> p h e", h=4)
                        dve.tensor_tensor(t3, biased[c % 2][:].rearrange("p (h e) -> p h e", h=4), cos,
                                          ALU.mult).then_inc(proj_read.sem, 1)
                        dve.wait_ge(proj_read.sem, proj_read.at(i, c + 1))
                        dve.wait_ge(cross_done.sem, cross_done.at(i, c + 1))
                        dve.tensor_tensor(tok[c % 2][:], tok[c % 2][:], crossed[c % 2][:], ALU.add).then_inc(tok_done.sem, 1)
                    for c in range(NTC, 6):
                        add_bias(c).then_inc(proj_read.sem, 1)
                    for s in range(2):
                        dve.wait_ge(scored.sem, scored.at(i, s + 1))
                        link(dve.tensor_tensor(sc[s][:], ps[s][:],
                                               k.cmask[:, :].unsqueeze(1).to_broadcast([T2, 4, T2]), ALU.mult))
                        dve.tensor_reduce(mx[:, s, :], sc[s][:], AX_X, ALU.max,
                                          apply_absolute_value=True).then_inc(masked.sem, 1)
                    for s in range(2):
                        dve.wait_ge(signed.sem, signed.at(i, s + 1))
                        dve.wait_ge(masked.sem, masked.at(i, s + 1))
                        dve.tensor_tensor(ab[s][:], ab[s][:], mx[:, s, :].unsqueeze(2).to_broadcast([T2, 4, T2]),
                                          ALU.subtract).then_inc(shifted.sem, 1)
                    for s in range(2):
                        dve.wait_ge(exped.sem, exped.at(i, s + 1))
                        link(dve.tensor_tensor(sc[s][:], ab[s][:], sg[s][:], ALU.mult))
                        link(dve.tensor_reduce(sm[:, s, :], sc[s][:], AX_X, ALU.add, apply_absolute_value=True))
                        link(dve.tensor_scalar(sm[:, s, :], sm[:, s, :], 1e-6, None, ALU.add))
                        link(dve.reciprocal(sm[:, s, :], sm[:, s, :]))
                        dve.tensor_tensor(sc[s][:], sc[s][:], sm[:, s, :].unsqueeze(2).to_broadcast([T2, 4, T2]),
                                          ALU.mult).then_inc(weighed.sem, 1)
                    dve.wait_ge(summed.sem, summed.at(i, 1))
                    xp = k.x[:, bass.ds(i, 1), :].rearrange("p a c -> p (a c)")
                    dve.tensor_tensor(xp, po[:], xp, ALU.add).then_inc(summed_read.sem, 1)
                    link.end()

            @block.tensor
            def _(pe):
                for s in (projected, turned, scored, mixed, summed):
                    pe.sem_inc(s.sem, 1)
                pe.wait_ge(w_lo_done.sem, 6)
                pe.wait_ge(wo_loaded.sem, 16)
                with pe.Fori(0, PAIRS) as i:
                    pe.wait_ge(xlo_done.sem, xlo_done.at(i, 1))

                    def project(c):
                        pe.wait_ge(proj_read.sem, proj_read.at(i, max(c - 1, 0)))
                        terms = [(x, w, kc) for kc in range(KC) for x, w in ((x_hi, w_hi), (x_hi, w_lo), (x_lo, w_hi))]
                        for n, (x, w, kc) in enumerate(terms):
                            ins = pe.matmul(pj[c % 2][:], x[:, kc, :], w[:, c, kc, :], start=n == 0,
                                            stop=n == len(terms) - 1)
                        ins.then_inc(projected.sem, 1)

                    def turn(c):
                        pe.wait_ge(tok_done.sem, tok_done.at(i, c + 1))
                        pe.wait_ge(turned_read.sem, turned_read.at(i, max(c - 1, 0)))
                        for h in range(4):
                            ins = pe.transpose(tp[c % 2][:, h, :], tok[c % 2][:, h * D:(h + 1) * D], k.ident[0:T2, 0:T2])
                        ins.then_inc(turned.sem, 1)

                    for c in range(6):
                        project(c)
                        if 1 <= c <= NTC:
                            turn(c - 1)
                    for s in range(2):
                        pe.wait_ge(turned_read.sem, turned_read.at(i, NTC))
                        pe.wait_ge(masked.sem, masked.at(i, 0))
                        for h in range(4):
                            ins = pe.matmul(ps[s][:, h, :], qkT[:, 4 * s + h, :], qkT[:, HH + 4 * s + h, :],
                                            start=True, stop=True)
                        ins.then_inc(scored.sem, 1)
                    for s in range(2):
                        pe.wait_ge(weighed.sem, weighed.at(i, s + 1))
                        for h in range(4):
                            ins = pe.transpose(tp[s][0:T2, h, :], sc[s][:, h, :], k.ident[0:T2, 0:T2])
                        ins.then_inc(turned.sem, 1)
                    for s in range(2):
                        pe.wait_ge(turned_read.sem, turned_read.at(i, NTC + s + 1))
                        pe.wait_ge(proj_read.sem, proj_read.at(i, 6))
                        pe.wait_ge(mixed_read.sem, mixed_read.at(i, s))
                        for h in range(4):
                            ins = pe.matmul(pz[:, h, :], v[:, 4 * s + h, :], aT[s][:, h, :], start=True, stop=True)
                        ins.then_inc(mixed.sem, 1)
                    pe.wait_ge(mixed_read.sem, mixed_read.at(i, 2))
                    pe.wait_ge(summed_read.sem, summed_read.at(i, 0))
                    for h in range(HH):
                        ins = pe.matmul(po[:], zT[:, h, :], wo[:, h, :], start=h == 0, stop=h == HH - 1)
                    ins.then_inc(summed.sem, 1)


def xattn_half(nc, k, hh):
    NTC = 5
    SRC = (0, 0, 1, 2, 2, 3)
    INS = (V_QS, V_QS, V_KS, V_QXS, V_QXS, V_VS)
    OUTS = (V_SQ, V_SQ, V_SK, V_SQX, V_SQX, V_SV)
    LNW = (V_QLW, V_QLW, V_KLW, V_QXLW, V_QXLW)
    with Phase(nc) as ctx:
        ctx.callback(ctx.clear)
        def sb(name, shape, dt=F32):
            return ctx.enter_context(nc.sbuf_tensor(f"b{hh}_{name}", shape, dt))

        def bank(name, shape):
            return ctx.enter_context(nc.psum_tensor(f"b{hh}_{name}", shape, F32))

        def sig(name, per=1, primed=0):
            return Signal(nc, ctx, f"b{hh}_{name}", per, primed)

        w_raw = sb("w_raw", [128, 2, KC, CH])
        w_mean = sb("w_mean", [128, KC * 4])
        w_hi = sb("w_hi", [128, 6, KC, CH], F32R)
        w_lo = sb("w_lo", [128, 6, KC, CH], F32R)
        xq = sb("xq_pair", [128, 4, KC, T2], F32R)
        sq = [sb(f"sq{j}", [T2, CH]) for j in range(2)]
        ss = sb("ss", [T2, 2, 4])
        rs = sb("rs", [T2, 2, 4])
        mhalf = sb("mhalf", [T2, 4])
        tok = [sb(f"tok{j}", [T2, CH]) for j in range(2)]
        qkT = sb("qkT", [128, HH + 4, T2])
        qxT = sb("qxT", [128, HH, T2])
        v = sb("v", [T2, 4, D])
        sc = [sb(f"sc{j}", [T2, 4, T2]) for j in range(2)]
        mx = sb("mx", [T2, 2, 4])
        sm = sb("sm", [T2, 2, 4])
        aT = [sb(f"aT{j}", [T2, 4, T2]) for j in range(2)]
        y = [sb(f"y{j}", [128, 4, T2], BF16) for j in range(2)]
        m = sb("m", [128, 4, T2], BF16)
        work = sb("work", [128, 4, T2], BF16)
        cq = sb("cq", [128, HH, T2], BF16)
        pj = [bank(f"pj{j}", [T2, CH]) for j in range(3)]
        tp = [bank(f"tp{j}", [128, 4, T2]) for j in range(2)]
        ps = [bank(f"ps{j}", [T2, 4, T2]) for j in range(2)]
        pz = bank("pz", [128, 4, T2])

        w_loaded, w_ready, w_hi_done, w_lo_done = sig("w_loaded"), sig("w_ready"), sig("w_hi_done"), sig("w_lo_done")
        prep_step = sig("prep_step", 6 * 4)
        half_set = sig("half_set")
        xq_done = sig("xq_done")
        projected = sig("projected", 6, 1)
        squared = sig("squared", NTC)
        vared = sig("vared", NTC)
        powed = sig("powed", NTC)
        tok_done = sig("tok_done", 6, 1)
        turned = sig("turned", NTC + 2, 1)
        turned_read = sig("turned_read", NTC + 2, 1)
        qx_stored = sig("qx_stored")
        scored = sig("scored", 2, 1)
        masked = sig("masked", 2, 1)
        shifted = sig("shifted", 2)
        exped = sig("exped", 2)
        weighed = sig("weighed", 2)
        mixed = sig("mixed", 2, 1)
        mixed_read = sig("mixed_read", 2, 1)
        cq_done = sig("cq_done", 2)
        cq_stored = sig("cq_stored")
        dve_step = sig("dve_step", 0)

        with nc.Block() as block:
            @block.sync
            def _(sp):
                for c in range(6):
                    if c >= 2:
                        sp.wait_ge(w_lo_done.sem, c - 1)
                    sp.dma_start(w_raw[:, c % 2], k.d_xattn_w[hh, c]).then_inc(w_loaded.sem, 16)
                    sp.wait_ge(w_loaded.sem, 16 * (c + 1))
                sp.sem_inc(qx_stored.sem, 16)
                sp.sem_inc(cq_stored.sem, 16)
                with sp.Fori(0, PAIRS) as i:
                    sp.wait_ge(turned_read.sem, turned_read.at(i, NTC))
                    for b2 in range(2):
                        sp.dma_start(k.d_qx[bass.ds(2 * i + b2, 1), :, hh * HH:(hh + 1) * HH, :]
                                     .rearrange("a p h s -> p (a h) s"),
                                     qxT[:, :, b2 * S:(b2 + 1) * S]).then_inc(qx_stored.sem, 16)
                    sp.wait_ge(cq_done.sem, cq_done.at(i, 2))
                    sp.dma_start(k.d_core[bass.ds(i, 1), :, hh * HH:(hh + 1) * HH, :]
                                 .rearrange("a p h s -> p (a h) s"), cq[:]).then_inc(cq_stored.sem, 16)
                sp.wait_ge(qx_stored.sem, 16 + 32 * PAIRS)
                sp.wait_ge(cq_stored.sem, 16 + 16 * PAIRS)

            @block.scalar
            def _(act):
                for c in range(6):
                    act.wait_ge(w_ready.sem, c + 1)
                    act.activation(w_hi[:, c], w_raw[:, c % 2], ACT.Copy).then_inc(w_hi_done.sem, 1)
                act.sem_inc(turned_read.sem, 1)
                with act.Fori(0, PAIRS) as i:
                    act.wait_ge(projected.sem, projected.at(i, 0))
                    act.activation(xq[:].rearrange("p n k t -> p (n k) t"),
                                   k.xq[:, :, :, bass.ds(i * T2, T2)].rearrange("p n k t -> p (n k) t"),
                                   ACT.Copy).then_inc(xq_done.sem, 1)

                    def unturn(c):
                        act.wait_ge(turned.sem, turned.at(i, c + 1))
                        if c == 0:
                            act.wait_ge(scored.sem, scored.at(i, 0))
                        if c == 3:
                            act.wait_ge(qx_stored.sem, 32 * i + 16)
                        dst = qkT[:, 4 * c:4 * c + 4, :] if c < 3 else qxT[:, 4 * (c - 3):4 * (c - 3) + 4, :]
                        act.activation(dst, tp[c % 2][:], ACT.Identity, scale=k.vec[:, LNW[c]:LNW[c] + 1],
                                       bias=k.vec[:, LNW[c] + 1:LNW[c] + 2]).then_inc(turned_read.sem, 1)

                    for c in range(NTC):
                        act.wait_ge(projected.sem, projected.at(i, c + 1))
                        if c >= 2:
                            act.wait_ge(vared.sem, vared.at(i, c - 1))
                        act.activation(sq[c % 2][:], pj[c % 3][:], ACT.Square).then_inc(squared.sem, 1)
                        if c >= 2:
                            unturn(c - 2)
                    unturn(NTC - 2)
                    unturn(NTC - 1)
                    for s in range(2):
                        act.wait_ge(shifted.sem, shifted.at(i, s + 1))
                        act.activation(sc[s][:], sc[s][:], ACT.Exp, scale=SCALE).then_inc(exped.sem, 1)
                    for s in range(2):
                        act.wait_ge(turned.sem, turned.at(i, NTC + s + 1))
                        act.activation(aT[s][:], tp[(NTC + s) % 2][0:T2], ACT.Copy).then_inc(turned_read.sem, 1)

            @block.gpsimd
            def _(pool):
                pool.memset(mhalf[:], -0.5).then_inc(half_set.sem, 1)
                pool.wait_ge(half_set.sem, 1)
                for c in range(6):
                    pool.wait_ge(w_hi_done.sem, c + 1)
                    pool.tensor_tensor(w_lo[:, c], w_raw[:, c % 2], w_hi[:, c].bitcast(F32),
                                       ALU.subtract).then_inc(w_lo_done.sem, 1)
                with pool.Fori(0, PAIRS) as i:
                    for c in range(NTC):
                        pool.wait_ge(vared.sem, vared.at(i, c + 1))
                        pool.tensor_tensor(rs[:, c % 2, :], ss[:, c % 2, :], mhalf[:], ALU.pow).then_inc(powed.sem, 1)

            @block.vector
            def _(dve):
                prep = Chain(dve, prep_step)
                for c in range(6):
                    dve.wait_ge(w_loaded.sem, 16 * (c + 1))
                    raw = w_raw[:, c % 2]
                    for kc in range(KC):
                        ins = dve.tensor_scalar(raw[:, kc], raw[:, kc], k.vec[:, INS[c] + kc:INS[c] + kc + 1],
                                                k.vec[:, OUTS[c]:OUTS[c] + 1], ALU.mult, ALU.mult)
                    prep(ins)
                    if c < NTC:
                        heads = raw.rearrange("p k (h e) -> p (k h) e", h=4)
                        prep(dve.tensor_reduce(w_mean[:], heads, AX_X, ALU.add))
                        prep(dve.tensor_scalar(w_mean[:], w_mean[:], 1.0 / D, None, ALU.mult))
                        dve.tensor_tensor(heads, heads, w_mean[:].unsqueeze(2).to_broadcast([128, KC * 4, D]),
                                          ALU.subtract).then_inc(w_ready.sem, 1)
                    else:
                        dve.sem_inc(w_ready.sem, 1)
                for s in (tok_done, masked, mixed_read):
                    dve.sem_inc(s.sem, 1)
                link = Chain(dve, dve_step)
                with dve.Fori(0, PAIRS) as i:
                    link.round(i)
                    dve_step.per = 33

                    def normalise(c):
                        dve.wait_ge(powed.sem, powed.at(i, c + 1))
                        dve.wait_ge(turned.sem, turned.at(i, max(c - 1, 0)))
                        dve.tensor_tensor(tok[c % 2][:].rearrange("p (h e) -> p h e", h=4),
                                          pj[c % 3][:].rearrange("p (h e) -> p h e", h=4),
                                          rs[:, c % 2, :].unsqueeze(2).to_broadcast([T2, 4, D]),
                                          ALU.mult).then_inc(tok_done.sem, 1)

                    for c in range(NTC):
                        dve.wait_ge(squared.sem, squared.at(i, c + 1))
                        link(dve.tensor_reduce(ss[:, c % 2, :], sq[c % 2][:].rearrange("p (h e) -> p h e", h=4),
                                               AX_X, ALU.add))
                        dve.tensor_scalar(ss[:, c % 2, :], ss[:, c % 2, :], 1.0 / D, EPS, ALU.mult,
                                          ALU.add).then_inc(vared.sem, 1)
                        if c >= 1:
                            normalise(c - 1)
                    normalise(NTC - 1)
                    dve.wait_ge(projected.sem, projected.at(i, 6))
                    dve.wait_ge(mixed.sem, mixed.at(i, 0))
                    dve.tensor_copy(v[:].rearrange("p h e -> p (h e)"), pj[5 % 3][:]).then_inc(tok_done.sem, 1)
                    for s in range(2):
                        dve.wait_ge(scored.sem, scored.at(i, s + 1))
                        link(dve.tensor_tensor(sc[s][:], ps[s][:],
                                               k.bmask[:, :].unsqueeze(1).to_broadcast([T2, 4, T2]), ALU.add))
                        dve.tensor_reduce(mx[:, s, :], sc[s][:], AX_X, ALU.max).then_inc(masked.sem, 1)
                        dve.wait_ge(masked.sem, masked.at(i, s + 1))
                        dve.tensor_tensor(sc[s][:], sc[s][:], mx[:, s, :].unsqueeze(2).to_broadcast([T2, 4, T2]),
                                          ALU.subtract).then_inc(shifted.sem, 1)
                    for s in range(2):
                        dve.wait_ge(exped.sem, exped.at(i, s + 1))
                        link(dve.tensor_reduce(sm[:, s, :], sc[s][:], AX_X, ALU.add))
                        link(dve.reciprocal(sm[:, s, :], sm[:, s, :]))
                        dve.tensor_tensor(sc[s][:], sc[s][:], sm[:, s, :].unsqueeze(2).to_broadcast([T2, 4, T2]),
                                          ALU.mult).then_inc(weighed.sem, 1)
                    dve.wait_ge(cq_stored.sem, 16 * i + 16)
                    for s in range(2):
                        dve.wait_ge(mixed.sem, mixed.at(i, s + 1))
                        smooth = k.rsm[:, hh * HH + 4 * s:hh * HH + 4 * s + 4].unsqueeze(2).to_broadcast([128, 4, T2])
                        dve.tensor_tensor(y[s][:], pz[:], smooth, ALU.mult).then_inc(mixed_read.sem, 1)
                        dve.wait_ge(mixed_read.sem, mixed_read.at(i, s + 1))
                        quantise(dve, link, cq[:, 4 * s:4 * s + 4, :], y[s][:], work[:], m[:]).then_inc(cq_done.sem, 1)
                        dve.wait_ge(cq_done.sem, cq_done.at(i, s + 1))
                    assert link.n <= 33
                    dve.sem_inc(dve_step.sem, 33 - link.n)

            @block.tensor
            def _(pe):
                for s in (projected, turned, scored, mixed):
                    pe.sem_inc(s.sem, 1)
                pe.wait_ge(w_lo_done.sem, 6)
                with pe.Fori(0, PAIRS) as i:
                    pe.wait_ge(xq_done.sem, xq_done.at(i, 1))

                    def project(c):
                        pe.wait_ge(tok_done.sem, tok_done.at(i, max(c - 2, 0)))
                        for n in range(2 * KC):
                            w = (w_hi, w_lo)[n % 2]
                            ins = pe.matmul(pj[c % 3][:], xq[:, SRC[c], n // 2, :], w[:, c, n // 2, :],
                                            start=n == 0, stop=n == 2 * KC - 1)
                        ins.then_inc(projected.sem, 1)

                    def turn(c):
                        pe.wait_ge(tok_done.sem, tok_done.at(i, c + 1))
                        pe.wait_ge(turned_read.sem, turned_read.at(i, max(c - 1, 0)))
                        for h in range(4):
                            ins = pe.transpose(tp[c % 2][:, h, :], tok[c % 2][:, h * D:(h + 1) * D], k.ident[0:T2, 0:T2])
                        ins.then_inc(turned.sem, 1)

                    for c in range(6):
                        project(c)
                        if c >= 2:
                            turn(c - 2)
                    turn(NTC - 1)
                    for s in range(2):
                        pe.wait_ge(turned_read.sem, turned_read.at(i, 3))
                        pe.wait_ge(masked.sem, masked.at(i, 0))
                        for h in range(4):
                            ins = pe.matmul(ps[s][:, h, :], qkT[:, 4 * s + h, :], qkT[:, HH + (4 * s + h) // HPG, :],
                                            start=True, stop=True)
                        ins.then_inc(scored.sem, 1)
                    for s in range(2):
                        pe.wait_ge(weighed.sem, weighed.at(i, s + 1))
                        pe.wait_ge(turned_read.sem, turned_read.at(i, NTC + s - 1))
                        for h in range(4):
                            ins = pe.transpose(tp[(NTC + s) % 2][0:T2, h, :], sc[s][:, h, :], k.ident[0:T2, 0:T2])
                        ins.then_inc(turned.sem, 1)
                    for s in range(2):
                        pe.wait_ge(turned_read.sem, turned_read.at(i, NTC + s + 1))
                        pe.wait_ge(tok_done.sem, tok_done.at(i, 6))
                        pe.wait_ge(mixed_read.sem, mixed_read.at(i, s))
                        for h in range(4):
                            ins = pe.matmul(pz[:, h, :], v[:, (4 * s + h) // HPG, :], aT[s][:, h, :], start=True, stop=True)
                        ins.then_inc(mixed.sem, 1)


def context_phase(nc, k):
    HG = G // 2
    HC = HG * D
    QN = HPG * S
    STG = 3
    with Phase(nc) as ctx:
        ctx.callback(ctx.clear)
        def sb(name, shape, dt=F32):
            return ctx.enter_context(nc.sbuf_tensor(f"c_{name}", shape, dt))

        def sig(name, per=1, primed=0):
            return Signal(nc, ctx, f"c_{name}", per, primed)

        wk_hi = sb("wk_hi", [128, KC, G * D], F32R)
        wk_lo = sb("wk_lo", [128, KC, G * D], F32R)
        wv = sb("wv", [128, KC, G * D])
        stage = sb("stage", [128, 2, STG * C])
        cT_hi = sb("cT_hi", [128, KC, SC], F32R)
        cT_lo = sb("cT_lo", [128, KC, SC], F32R)
        c_hi = sb("c_hi", [TT_C, NT_C, C], F32R)
        c_lo = sb("c_lo", [TT_C, NT_C, C], F32R)
        qx = sb("qx", [128, NH, S])
        q_hi = sb("q_hi", [128, NH, S], F32R)
        q_lo = sb("q_lo", [128, NH, S], F32R)
        kT_hi = sb("kT_hi", [128, HG, SC], F32R)
        kT_lo = sb("kT_lo", [128, HG, SC], F32R)
        sq = [sb(f"sq{j}", [TT_C, HC]) for j in range(2)]
        kn = [sb(f"kn{j}", [TT_C, HC]) for j in range(2)]
        ss = sb("ss", [TT_C, 4, HG])
        rs = sb("rs", [TT_C, 4, HG])
        mhalf = sb("mhalf", [128, HG])
        P = [sb(f"P{j}", [QN, SC]) for j in range(2)]
        PT_hi = [sb(f"PT_hi{j}", [TT_C, NT_C, QN], F32R) for j in range(2)]
        PT_lo = [sb(f"PT_lo{j}", [TT_C, NT_C, QN], F32R) for j in range(2)]
        w_mean = sb("w_mean", [128, KC * G])
        qb = sb("qb", [QN, HG])
        mx = sb("mx", [QN, 2])
        ebias = sb("ebias", [QN, 2])
        esum = sb("esum", [QN, 4])
        rsum = sb("rsum", [QN, 1])
        U = sb("U", [QN, C])
        UT = sb("UT", [128, KC, QN])
        y = sb("y", [128, HPG, S], BF16)
        m = sb("m", [128, HPG, S], BF16)
        work = sb("work", [128, HPG, S], BF16)
        cq = sb("cq", [128, NH, S], BF16)
        psum = ctx.enter_context(nc.psum_tensor("c_psum", [128, 8, 512], F32))

        def p_scores(g):
            return psum[0:QN, 3 * (g % 2):3 * (g % 2) + 3, 0:500]

        p_turn = psum[:, 6, 0:4 * QN].rearrange("p (a b) -> p a b", a=4)
        p_mix = psum[:, 7, :]

        w_loaded, w_ready, w_hi_done, w_lo_done = sig("w_loaded"), sig("w_ready"), sig("w_hi_done"), sig("w_lo_done")
        prep_step = sig("prep_step", 3)
        half_set = sig("half_set")
        NSTG = 8
        staged = [sig(f"staged{j}", 4 * 16) for j in range(2)]
        split_hi = sig("split_hi", NSTG)
        split_lo = sig("split_lo", NSTG, 1)
        qx_loaded = sig("qx_loaded", 16)
        q_scaled = sig("q_scaled")
        q_hi_done = sig("q_hi_done")
        q_lo_done = sig("q_lo_done")
        projected = sig("projected", 2 * NT_C, 1)
        squared = sig("squared", 2 * NT_C)
        vared = sig("vared", 2 * NT_C)
        powed = sig("powed", 2 * NT_C)
        kn_done = sig("kn_done", 2 * NT_C, 1)
        k_turned = sig("k_turned", 2 * NT_C, 1)
        kT_hi_done = sig("kT_hi_done", 2 * NT_C)
        kT_lo_done = sig("kT_lo_done", 2 * NT_C, 1)
        qb_ready = sig("qb_ready", 2)
        scored = sig("scored", 2 * HG, 1)
        biased = sig("biased", 2 * HG)
        exped = sig("exped", 2 * HG, 1)
        p_turned = sig("p_turned", 2 * HG * 3, 1)
        PT_hi_done = sig("PT_hi_done", 2 * HG * 3)
        PT_lo_done = sig("PT_lo_done", 2 * HG * 3, 1)
        mixed = sig("mixed", 2 * HG, 1)
        U_done = sig("U_done", 2 * HG)
        U_turned = sig("U_turned", 2 * HG)
        UT_done = sig("UT_done", 2 * HG)
        out_done = sig("out_done", 2 * HG, 1)
        out_read = sig("out_read", 2 * HG, 1)
        cq_done = sig("cq_done", 2 * HG)
        cq_stored = sig("cq_stored", 16)
        store_begun = sig("store_begun")
        dve_step = sig("dve_step", 160)

        HT = SC // 2

        def piece(n):
            if n < 4:
                kc, t = n // 2, n % 2
                return (stage[:, n % 2, 0:HT], cT_hi[:, kc, t * HT:(t + 1) * HT], cT_lo[:, kc, t * HT:(t + 1) * HT])
            j = STG * (n - 4)
            return (stage[0:TT_C, n % 2, 0:STG * C].rearrange("p (a c) -> p a c", a=STG),
                    c_hi[:, j:j + STG, :], c_lo[:, j:j + STG, :])

        with nc.Block() as block:
            @block.sync
            def _(sp):
                for t in range(2):
                    sp.dma_start(k.c_wraw[:, t], k.d_ctx_wk[:, t]).then_inc(w_loaded.sem, 16)
                sp.dma_start(wv[:], k.d_ctx_wv).then_inc(w_loaded.sem, 16)
                sp.sem_inc(cq_stored.sem, 16)
                with sp.Fori(0, B) as b:
                    for n in range(NSTG):
                        sp.wait_ge(split_lo.sem, split_lo.at(b, max(n - 1, 0)) if n >= 2 else split_lo.at(b, 0))
                        if n < 4:
                            src = k.d_ctxT[bass.ds(b, 1), n // 2, :, (n % 2) * HT:(n % 2 + 1) * HT].rearrange("a p t -> (a p) t")
                        else:
                            src = k.d_ctx[bass.ds(b, 1), :, STG * (n - 4):STG * (n - 3), :].rearrange("a p j c -> (a p) j c")
                        sp.dma_start(piece(n)[0], src).then_inc(staged[n % 2].sem, 16)
                        if n == 3:
                            sp.wait_ge(q_lo_done.sem, q_lo_done.at(b, 0))
                            sp.dma_start(qx[:], k.d_qx[bass.ds(b, 1)].rearrange("a p h s -> (a p) h s")).then_inc(qx_loaded.sem, 16)
                    sp.wait_ge(cq_done.sem, cq_done.at(b, 2 * HG))
                    sp.sem_inc(store_begun.sem, 1)
                    sp.dma_start(k.d_xout[bass.ds(b, 1)].rearrange("a p h s -> (a p) h s"), cq[:]).then_inc(cq_stored.sem, 16)
                sp.wait_ge(cq_stored.sem, 16 + 16 * B)

            @block.scalar
            def _(act):
                act.wait_ge(w_ready.sem, 1)
                act.activation(wk_hi[:], k.c_wraw[:], ACT.Copy).then_inc(w_hi_done.sem, 1)
                act.sem_inc(exped.sem, 1)
                with act.Fori(0, B) as b:
                    def split(n):
                        act.wait_ge(staged[n % 2].sem, staged[n % 2].at(b, 16 * (n // 2 + 1)))
                        if n == 0:
                            act.wait_ge(projected.sem, projected.at(b, 0))
                        if n == 4:
                            act.wait_ge(mixed.sem, mixed.at(b, 0))
                        raw, hi, _ = piece(n)
                        act.activation(hi, raw, ACT.Copy).then_inc(split_hi.sem, 1)

                    for n in range(4):
                        split(n)
                    act.wait_ge(q_scaled.sem, q_scaled.at(b, 1))
                    act.activation(q_hi[:], qx[:], ACT.Copy).then_inc(q_hi_done.sem, 1)
                    for h in range(2):
                        o, og = NT_C * h, HG * h

                        def unturn(j):
                            act.wait_ge(k_turned.sem, k_turned.at(b, o + j + 1))
                            if j == 0:
                                act.wait_ge(scored.sem, scored.at(b, og))
                            src = psum[:, 4 + j % 2, 0:4 * TT_C].rearrange("p (g t) -> p g t", g=HG)
                            act.activation(kT_hi[:, :, j * TT_C:(j + 1) * TT_C], src, ACT.Copy).then_inc(kT_hi_done.sem, 1)

                        for j in range(NT_C):
                            act.wait_ge(projected.sem, projected.at(b, o + j + 1))
                            if j >= 2:
                                act.wait_ge(vared.sem, vared.at(b, o + j - 1))
                            act.activation(sq[j % 2][:], psum[0:TT_C, j % 4, :], ACT.Square).then_inc(squared.sem, 1)
                            if j >= 3:
                                unturn(j - 3)
                            if h == 0 and j in (2, 4, 6, 8):
                                split(4 + (j - 2) // 2)
                        for j in range(NT_C - 3, NT_C):
                            unturn(j)

                        def part(g, r):
                            act.wait_ge(p_turned.sem, p_turned.at(b, 3 * (og + g) + r + 1))
                            if r == 0:
                                act.wait_ge(mixed.sem, mixed.at(b, max(og + g - 1, 0)))
                            act.activation(PT_hi[g % 2][:, 4 * r:4 * r + 4, :], p_turn[0:TT_C],
                                           ACT.Copy).then_inc(PT_hi_done.sem, 1)

                        for g in range(HG + 1):
                            if g < HG:
                                act.wait_ge(biased.sem, biased.at(b, og + g + 1))
                                act.wait_ge(p_turned.sem, p_turned.at(b, 3 * max(og + g - 1, 0)))
                                act.activation(P[g % 2][:].rearrange("p (a t) -> p a t", a=3), p_scores(g), ACT.Exp,
                                               scale=SCALE, bias=ebias[:, g % 2:g % 2 + 1],
                                               accum_out=esum[:, g:g + 1]).then_inc(exped.sem, 1)
                            if g >= 1:
                                for r in range(3):
                                    part(g - 1, r)

            @block.gpsimd
            def _(pool):
                pool.memset(mhalf[:], -0.5).then_inc(half_set.sem, 1)
                pool.wait_ge(half_set.sem, 1)
                pool.wait_ge(w_hi_done.sem, 1)
                pool.tensor_tensor(wk_lo[:], k.c_wraw[:], wk_hi[:].bitcast(F32), ALU.subtract).then_inc(w_lo_done.sem, 1)
                pool.sem_inc(split_lo.sem, 1)
                pool.sem_inc(q_lo_done.sem, 1)
                with pool.Fori(0, B) as b:
                    def split(n):
                        pool.wait_ge(split_hi.sem, split_hi.at(b, n + 1))
                        raw, hi, lo = piece(n)
                        pool.tensor_tensor(lo, raw, hi.bitcast(F32), ALU.subtract).then_inc(split_lo.sem, 1)

                    for n in range(4):
                        split(n)
                    pool.wait_ge(q_hi_done.sem, q_hi_done.at(b, 1))
                    pool.tensor_tensor(q_lo[:], qx[:], q_hi[:].bitcast(F32), ALU.subtract).then_inc(q_lo_done.sem, 1)
                    for h in range(2):
                        for j in range(NT_C):
                            pool.wait_ge(vared.sem, vared.at(b, NT_C * h + j + 1))
                            pool.tensor_tensor(rs[:, j % 4, :], ss[:, j % 4, :], mhalf[0:TT_C], ALU.pow).then_inc(powed.sem, 1)
                            if h == 0 and j in (3, 5, 7, 9):
                                split(4 + (j - 3) // 2)

            @block.vector
            def _(dve):
                prep = Chain(dve, prep_step)
                dve.wait_ge(w_loaded.sem, 48)
                heads = k.c_wraw[:].rearrange("p k (h e) -> p (k h) e", h=G)
                prep(dve.tensor_reduce(w_mean[:], heads, AX_X, ALU.add))
                prep(dve.tensor_scalar(w_mean[:], w_mean[:], 1.0 / D, None, ALU.mult))
                dve.tensor_tensor(heads, heads, w_mean[:].unsqueeze(2).to_broadcast([128, KC * G, D]),
                                  ALU.subtract).then_inc(w_ready.sem, 1)
                for s in (kn_done, kT_lo_done, PT_lo_done, out_read):
                    dve.sem_inc(s.sem, 1)
                link = Chain(dve, dve_step)
                with dve.Fori(0, B) as b:
                    link.round(b)
                    dve.wait_ge(qx_loaded.sem, qx_loaded.at(b, 16))
                    dve.wait_ge(projected.sem, projected.at(b, 0))

                    def offsets(h):
                        dve.wait_ge(qb_ready.sem, qb_ready.at(b, h + 1))
                        link(dve.tensor_copy(qb[:], psum[0:QN, 7, 0:2 * HG:2]))

                    dve.wait_ge(qb_ready.sem, qb_ready.at(b, 1))
                    link(dve.tensor_copy(k.qb_all[:], psum[0:QN, 7, 0:2 * G].rearrange("p (g a) -> p g a", a=2)[:, :, 0]))
                    dve.tensor_scalar(qx[:], qx[:], k.vec[:, V_KXLW:V_KXLW + 1], None, ALU.mult).then_inc(q_scaled.sem, 1)
                    for h in range(2):
                        o, og = NT_C * h, HG * h

                        def normalise(j):
                            dve.wait_ge(powed.sem, powed.at(b, o + j + 1))
                            dve.wait_ge(k_turned.sem, k_turned.at(b, o + max(j - 1, 0)))
                            dve.tensor_tensor(kn[j % 2][:].rearrange("p (g e) -> p g e", g=HG),
                                              psum[0:TT_C, j % 4, :].rearrange("p (g e) -> p g e", g=HG),
                                              rs[:, j % 4, :].unsqueeze(2).to_broadcast([TT_C, HG, D]),
                                              ALU.mult).then_inc(kn_done.sem, 1)

                        def low(j):
                            dve.wait_ge(kT_hi_done.sem, kT_hi_done.at(b, o + j + 1))
                            src = psum[:, 4 + j % 2, 0:4 * TT_C].rearrange("p (g t) -> p g t", g=HG)
                            at = slice(j * TT_C, (j + 1) * TT_C)
                            dve.tensor_tensor(kT_lo[:, :, at], src, kT_hi[:, :, at].bitcast(F32),
                                              ALU.subtract).then_inc(kT_lo_done.sem, 1)

                        for j in range(NT_C + 4):
                            if j < NT_C:
                                dve.wait_ge(squared.sem, squared.at(b, o + j + 1))
                                link(dve.tensor_reduce(ss[:, j % 4, :], sq[j % 2][:].rearrange("p (g e) -> p g e", g=HG),
                                                       AX_X, ALU.add))
                                dve.tensor_scalar(ss[:, j % 4, :], ss[:, j % 4, :], 1.0 / D, EPS, ALU.mult,
                                                  ALU.add).then_inc(vared.sem, 1)
                            if 1 <= j <= NT_C:
                                normalise(j - 1)
                            if j >= 4:
                                low(j - 4)

                        def softmax_bias(g):
                            dve.wait_ge(scored.sem, scored.at(b, og + g + 1))
                            link(dve.tensor_reduce(mx[:, g % 2:g % 2 + 1], p_scores(g), mybir.AxisListType.XY, ALU.max))
                            link(dve.tensor_scalar(mx[:, g % 2:g % 2 + 1], mx[:, g % 2:g % 2 + 1],
                                                   k.qb_all[:, og + g:og + g + 1], None, ALU.add))
                            dve.wait_ge(exped.sem, exped.at(b, max(og + g - 1, 0)))
                            link(dve.tensor_tensor(mx[:, g % 2:g % 2 + 1], k.qb_all[:, og + g:og + g + 1],
                                                   mx[:, g % 2:g % 2 + 1], ALU.subtract))
                            dve.tensor_scalar(ebias[:, g % 2:g % 2 + 1], mx[:, g % 2:g % 2 + 1], SCALE, None,
                                              ALU.mult).then_inc(biased.sem, 1)

                        def part(g, r):
                            dve.wait_ge(PT_hi_done.sem, PT_hi_done.at(b, 3 * (og + g) + r + 1))
                            at = slice(4 * r, 4 * r + 4)
                            dve.tensor_tensor(PT_lo[g % 2][:, at, :], p_turn[0:TT_C], PT_hi[g % 2][:, at, :].bitcast(F32),
                                              ALU.subtract).then_inc(PT_lo_done.sem, 1)

                        for g in range(HG + 3):
                            if g < HG:
                                softmax_bias(g)
                            if g >= 3:
                                dve.wait_ge(U_turned.sem, U_turned.at(b, og + g - 3 + 1))
                                dve.tensor_copy(UT[:], p_mix[:, 256:256 + KC * QN].rearrange("p (k q) -> p k q", k=KC)
                                                ).then_inc(UT_done.sem, 1)
                            if 1 <= g <= HG:
                                part(g - 1, 0)
                            if g >= 3:
                                gg = g - 3
                                dve.wait_ge(out_done.sem, out_done.at(b, og + gg + 1))
                                if gg == 0 and h == 0:
                                    dve.wait_ge(cq_stored.sem, 16 * b + 16)
                                n = HPG * (og + gg)
                                smooth = k.rsm[:, NH + n:NH + n + HPG].unsqueeze(2).to_broadcast([128, HPG, S])
                                dve.tensor_tensor(y[:], p_mix[:, 0:QN].rearrange("p (a s) -> p a s", a=HPG), smooth,
                                                  ALU.mult).then_inc(out_read.sem, 1)
                                dve.wait_ge(out_read.sem, out_read.at(b, og + gg + 1))
                                quantise(dve, link, cq[:, n:n + HPG, :], y[:], work[:], m[:]).then_inc(cq_done.sem, 1)
                                dve.wait_ge(cq_done.sem, cq_done.at(b, og + gg + 1))
                            if 1 <= g <= HG:
                                part(g - 1, 1)
                                part(g - 1, 2)
                            if 2 <= g < HG + 2:
                                gg = g - 2
                                dve.wait_ge(exped.sem, exped.at(b, og + gg + 1))
                                link(dve.reciprocal(rsum[:], esum[:, gg:gg + 1]))
                                dve.wait_ge(mixed.sem, mixed.at(b, og + gg + 1))
                                dve.tensor_scalar(U[:], p_mix[0:QN, 0:C], rsum[:, 0:1], None, ALU.mult).then_inc(U_done.sem, 1)
                    assert link.n <= 160, link.n
                    dve.sem_inc(dve_step.sem, 160 - link.n)

            @block.tensor
            def _(pe):
                for s in (projected, k_turned, scored, p_turned, mixed, out_done):
                    pe.sem_inc(s.sem, 1)
                pe.wait_ge(w_lo_done.sem, 1)
                pe.wait_ge(w_loaded.sem, 48)
                with pe.Fori(0, B) as b:
                    pe.wait_ge(qx_loaded.sem, qx_loaded.at(b, 16))
                    pe.wait_ge(out_read.sem, out_read.at(b, 0))
                    for g in range(G):
                        ins = pe.matmul(psum[0:QN, 7, 2 * g:2 * g + 1], qx[:, HPG * g:HPG * g + HPG, :].rearrange("p a s -> p (a s)"),
                                        k.vec[:, V_KXLB:V_KXLB + 1], start=True, stop=True)
                    ins.then_inc(qb_ready.sem, 2)
                    for h in range(2):
                        o, og = NT_C * h, HG * h

                        def project(j):
                            if h == 0 and j == 0:
                                pe.wait_ge(split_lo.sem, split_lo.at(b, 4))
                            pe.wait_ge(kn_done.sem, kn_done.at(b, o + max(j - 3, 0)))
                            if j == 0:
                                pe.wait_ge(exped.sem, exped.at(b, og))
                            terms = [(x, w, kc) for kc in range(KC)
                                     for x, w in ((cT_hi, wk_hi), (cT_hi, wk_lo), (cT_lo, wk_hi))]
                            for n, (x, w, kc) in enumerate(terms):
                                ins = pe.matmul(psum[0:TT_C, j % 4, :], x[:, kc, j * TT_C:(j + 1) * TT_C],
                                                w[:, kc, h * HC:(h + 1) * HC], start=n == 0, stop=n == 5)
                            ins.then_inc(projected.sem, 1)

                        def turn(j):
                            pe.wait_ge(kn_done.sem, kn_done.at(b, o + j + 1))
                            pe.wait_ge(kT_lo_done.sem, kT_lo_done.at(b, o + max(j - 1, 0)))
                            for g in range(HG):
                                ins = pe.transpose(psum[:, 4 + j % 2, g * TT_C:(g + 1) * TT_C],
                                                   kn[j % 2][:, g * D:(g + 1) * D], k.ident[0:TT_C, 0:TT_C])
                            ins.then_inc(k_turned.sem, 1)

                        for j in range(NT_C + 2):
                            if j < NT_C:
                                project(j)
                            if j >= 2:
                                turn(j - 2)

                        def score(g):
                            if g == 0:
                                pe.wait_ge(kT_lo_done.sem, kT_lo_done.at(b, o + NT_C))
                                pe.wait_ge(q_lo_done.sem, q_lo_done.at(b, 1) + 1)
                            pe.wait_ge(exped.sem, exped.at(b, max(og + g - 1, 0)))
                            qs = slice(HPG * (og + g), HPG * (og + g) + HPG)
                            for t in range(3):
                                for n, (x, w) in enumerate(((q_hi, kT_hi), (q_hi, kT_lo), (q_lo, kT_hi))):
                                    ins = pe.matmul(psum[0:QN, 3 * (g % 2) + t, 0:500], x[:, qs, :].rearrange("p a s -> p (a s)"),
                                                    w[:, g, t * 500:(t + 1) * 500], start=n == 0, stop=n == 2)
                            ins.then_inc(scored.sem, 1)

                        def turn_part(g, r):
                            if r == 0:
                                pe.wait_ge(exped.sem, exped.at(b, og + g + 1))
                            pe.wait_ge(PT_lo_done.sem, PT_lo_done.at(b, 3 * (og + g) + r))
                            for a in range(4):
                                j = 4 * r + a
                                ins = pe.transpose(p_turn[0:TT_C, a, :], P[g % 2][:, j * TT_C:(j + 1) * TT_C],
                                                   k.ident[0:QN, 0:QN])
                            ins.then_inc(p_turned.sem, 1)

                        def mix_part(g, r):
                            if r == 0:
                                pe.wait_ge(out_read.sem, out_read.at(b, og + g))
                                if g == 0 and h == 0:
                                    pe.wait_ge(split_lo.sem, split_lo.at(b, NSTG))
                            pe.wait_ge(PT_lo_done.sem, PT_lo_done.at(b, 3 * (og + g) + r + 1))
                            for a in range(4):
                                j = 4 * r + a
                                for n, (x, w) in enumerate(((PT_hi, c_hi), (PT_hi, c_lo), (PT_lo, c_hi))):
                                    ins = pe.matmul(p_mix[0:QN, 0:C], x[g % 2][:, j, :], w[:, j, :],
                                                    start=j == 0 and n == 0, stop=j == NT_C - 1 and n == 2)
                            if r == 2:
                                ins.then_inc(mixed.sem, 1)

                        for g in range(HG + 3):
                            if g < HG:
                                score(g)
                            if g >= 3:
                                pe.wait_ge(U_done.sem, U_done.at(b, og + g - 3 + 1))
                                for kc in range(KC):
                                    ins = pe.transpose(p_mix[:, 256 + kc * QN:256 + (kc + 1) * QN], U[:, kc * 128:(kc + 1) * 128],
                                                       k.ident[0:QN, 0:QN])
                                ins.then_inc(U_turned.sem, 1)
                            if 1 <= g <= HG:
                                turn_part(g - 1, 0)
                            if g >= 3:
                                gg = og + g - 3
                                pe.wait_ge(UT_done.sem, UT_done.at(b, gg + 1))
                                for kc in range(KC):
                                    ins = pe.matmul(p_mix[:, 0:QN], wv[:, kc, gg * D:(gg + 1) * D], UT[:, kc, :],
                                                    start=kc == 0, stop=kc == KC - 1)
                                ins.then_inc(out_done.sem, 1)
                            for r in range(3):
                                if r and 1 <= g <= HG:
                                    turn_part(g - 1, r)
                                if 2 <= g < HG + 2:
                                    mix_part(g - 2, r)


def project_phase(nc, k):
    NT = 2 * NH
    with Phase(nc) as ctx:
        ctx.callback(ctx.clear)
        def sb(name, shape, dt=F32):
            return ctx.enter_context(nc.sbuf_tensor(f"d_{name}", shape, dt))

        def sig(name, per=1, primed=0):
            return Signal(nc, ctx, f"d_{name}", per, primed)

        w_raw = sb("w_raw", [128, 2, 4, C])
        w_hi = sb("w_hi", [128, NT, C], F32R)
        w_lo = sb("w_lo", [128, NT, C], F32R)
        cat = [sb(f"cat{j}", [128, NT, T2], BF16) for j in range(2)]
        catr = [sb(f"catr{j}", [128, NT, T2], F32R) for j in range(2)]
        osc = sb("osc", [128, 1])
        po = [ctx.enter_context(nc.psum_tensor(f"d_po{j}", [T2, C], F32)) for j in range(2)]
        w_loaded, w_hi_done, w_lo_done = [sig("w_loaded0"), sig("w_loaded1")], sig("w_hi_done"), sig("w_lo_done")
        cat_loaded = [sig(f"cat_loaded{j}", 48) for j in range(2)]
        cast = sig("cast", 2, 1)
        summed = sig("summed", 2, 1)
        added = sig("added", 2, 1)
        osc_done = sig("osc_done")
        with nc.Block() as block:
            @block.sync
            def _(sp):
                for c in range(NT // 4):
                    if c >= 2:
                        sp.wait_ge(w_lo_done.sem, c - 1)
                    sp.dma_start(w_raw[:, c % 2], k.d_proj_w[:, 4 * c:4 * c + 4, :]).then_inc(w_loaded[c % 2].sem, 16)
                with sp.Fori(0, PAIRS // 2) as i:
                    for j in range(2):
                        sp.wait_ge(cast.sem, cast.at(i, 0))
                        sp.dma_start(cat[j][:, 0:NH, :], k.d_core[bass.ds(2 * i + j, 1)].rearrange("a p h s -> (a p) h s")
                                     ).then_inc(cat_loaded[j].sem, 16)
                        for b2 in range(2):
                            sp.dma_start(cat[j][:, NH:NT, b2 * S:(b2 + 1) * S],
                                         k.d_xout[bass.ds(4 * i + 2 * j + b2, 1)].rearrange("a p h s -> (a p) h s")
                                         ).then_inc(cat_loaded[j].sem, 16)

            @block.scalar
            def _(act):
                for c in range(NT // 4):
                    act.wait_ge(w_loaded[c % 2].sem, 16 * (c // 2 + 1))
                    act.activation(w_hi[:, 4 * c:4 * c + 4, :], w_raw[:, c % 2], ACT.Copy).then_inc(w_hi_done.sem, 1)
                act.sem_inc(cast.sem, 1)
                with act.Fori(0, PAIRS // 2) as i:
                    for j in range(2):
                        act.wait_ge(cat_loaded[j].sem, cat_loaded[j].at(i, 48))
                        act.wait_ge(summed.sem, summed.at(i, 0))
                        act.activation(catr[j][:], cat[j][:], ACT.Copy).then_inc(cast.sem, 1)

            @block.gpsimd
            def _(pool):
                for c in range(NT // 4):
                    pool.wait_ge(w_hi_done.sem, c + 1)
                    pool.tensor_tensor(w_lo[:, 4 * c:4 * c + 4, :], w_raw[:, c % 2],
                                       w_hi[:, 4 * c:4 * c + 4, :].bitcast(F32), ALU.subtract).then_inc(w_lo_done.sem, 1)

            @block.vector
            def _(dve):
                dve.tensor_tensor(osc[:], k.vec[:, V_SPI:V_SPI + 1], k.vec[:, V_SPW:V_SPW + 1], ALU.mult).then_inc(osc_done.sem, 1)
                dve.wait_ge(osc_done.sem, 1)
                dve.sem_inc(added.sem, 1)
                with dve.Fori(0, PAIRS // 2) as i:
                    for j in range(2):
                        dve.wait_ge(summed.sem, summed.at(i, j + 1))
                        xp = k.x[:, bass.ds(2 * i + j, 1), :].rearrange("p a c -> p (a c)")
                        dve.scalar_tensor_tensor(xp, po[j][:], osc[0:T2, 0:1], xp, ALU.mult, ALU.add).then_inc(added.sem, 1)

            @block.tensor
            def _(pe):
                pe.sem_inc(summed.sem, 1)
                pe.wait_ge(w_lo_done.sem, NT // 4)
                with pe.Fori(0, PAIRS // 2) as i:
                    for j in range(2):
                        pe.wait_ge(cast.sem, cast.at(i, j + 1))
                        pe.wait_ge(added.sem, added.at(i, 0))
                        for t in range(NT):
                            for w in (w_hi, w_lo):
                                ins = pe.matmul(po[j][:], catr[j][:, t, :], w[:, t, :], start=t == 0 and w is w_hi,
                                                stop=t == NT - 1 and w is w_lo)
                        ins.then_inc(summed.sem, 1)


def gate_phase(nc, k):
    with Phase(nc) as ctx:
        ctx.callback(ctx.clear)
        def sb(name, shape, dt=F32):
            return ctx.enter_context(nc.sbuf_tensor(f"g_{name}", shape, dt))

        def sig(name, per=1, primed=0):
            return Signal(nc, ctx, f"g_{name}", per, primed)

        gw = sb("gw", [128, KC, E])
        b2 = sb("b2", [E, C])
        rank = sb("rank", [T2, E])
        lg = sb("lg", [T2, PAIRS, E])
        left = sb("left", [T2, PAIRS, E])
        eq = sb("eq", [T2, PAIRS, E])
        pick = sb("pick", [T2, PAIRS, E])
        best = sb("best", [T2, PAIRS])
        top = sb("top", [T2, PAIRS])
        tie = sb("tie", [T2, PAIRS])
        GT = sb("GT", [E, PAIRS, T2])
        pl = ctx.enter_context(nc.psum_tensor("g_pl", [T2, PAIRS, E], F32))
        pg = ctx.enter_context(nc.psum_tensor("g_pg", [128, 2, 512], F32))
        pb = ctx.enter_context(nc.psum_tensor("g_pb", [T2, 4, 2, C], F32))
        loaded, logits, ranked, exped_in, exped, gated, g_turned, g_copied, biased = (
            sig("loaded"), sig("logits"), sig("ranked"), sig("exped_in"), sig("exped"), sig("gated"),
            sig("g_turned"), sig("g_copied"), sig("biased"))
        dve_step = sig("dve_step")
        bc = [T2, PAIRS, E]
        with nc.Block() as block:
            @block.sync
            def _(sp):
                sp.dma_start(gw[:], k.d_gate_w).then_inc(loaded.sem, 16)
                sp.dma_start(b2[:], k.d_b2).then_inc(loaded.sem, 16)

            @block.gpsimd
            def _(pool):
                pool.iota(rank[:], [[-1, E]], base=E, channel_multiplier=0,
                          allow_small_or_imprecise_dtypes=True).then_inc(ranked.sem, 1)

            @block.tensor
            def _(pe):
                pe.wait_ge(loaded.sem, 32)
                for p in range(PAIRS):
                    for kc in range(KC):
                        ins = pe.matmul(pl[:, p, :], k.xT[:, kc, p * T2:(p + 1) * T2], gw[:, kc, :], start=kc == 0, stop=kc == KC - 1)
                ins.then_inc(logits.sem, 1)
                pe.wait_ge(gated.sem, 1)
                for p in range(PAIRS):
                    ins = pe.transpose(pg[0:E, p // 4, (p % 4) * T2:(p % 4 + 1) * T2], k.gates[:, p, :], k.ident[0:T2, 0:T2])
                ins.then_inc(g_turned.sem, 1)
                pe.wait_ge(g_copied.sem, 1)
                for p in range(PAIRS):
                    ins = pe.matmul(pb[:, p // 2, p % 2, :], GT[:, p, :], b2[:], start=True, stop=True)
                ins.then_inc(biased.sem, 1)

            @block.scalar
            def _(act):
                act.wait_ge(exped_in.sem, 1)
                act.activation(lg[:], lg[:], ACT.Exp).then_inc(exped.sem, 1)

            @block.vector
            def _(dve):
                link = Chain(dve, dve_step)
                dve.wait_ge(logits.sem, 1)
                gb = k.rows[0:T2, R_GB:R_GB + E].unsqueeze(1).to_broadcast(bc)
                link(dve.tensor_tensor(lg[:], pl[:], gb, ALU.add))
                link(dve.tensor_copy(left[:], lg[:]))
                dve.wait_ge(ranked.sem, 1)
                for r in range(TOPK):
                    link(dve.tensor_reduce(best[:], left[:], AX_X, ALU.max))
                    if r == 0:
                        link(dve.tensor_copy(top[:], best[:]))
                    link(dve.tensor_tensor(eq[:], left[:], best[:].unsqueeze(2).to_broadcast(bc), ALU.is_ge))
                    link(dve.tensor_tensor(eq[:], eq[:], rank[:].unsqueeze(1).to_broadcast(bc), ALU.mult))
                    link(dve.tensor_reduce(tie[:], eq[:], AX_X, ALU.max))
                    link(dve.tensor_tensor(eq[:], eq[:], tie[:].unsqueeze(2).to_broadcast(bc), ALU.is_equal))
                    if r == 0:
                        link(dve.tensor_copy(pick[:], eq[:]))
                    else:
                        link(dve.tensor_tensor(pick[:], pick[:], eq[:], ALU.add))
                    link(dve.scalar_tensor_tensor(left[:], eq[:], NEG, left[:], ALU.mult, ALU.add))
                link(dve.tensor_tensor(lg[:], lg[:], top[:].unsqueeze(2).to_broadcast(bc), ALU.subtract))
                dve.sem_inc(exped_in.sem, 1)
                dve.wait_ge(exped.sem, 1)
                link(dve.tensor_tensor(lg[:], lg[:], pick[:], ALU.mult))
                link(dve.tensor_reduce(best[:], lg[:], AX_X, ALU.add))
                link(dve.reciprocal(best[:], best[:]))
                dve.tensor_tensor(k.gates[:], lg[:], best[:].unsqueeze(2).to_broadcast(bc), ALU.mult).then_inc(gated.sem, 1)
                link(dve.tensor_tensor(k.x[:], k.x[:], k.xh[:], ALU.add))
                dve.wait_ge(g_turned.sem, 1)
                link(dve.tensor_copy(GT[:].rearrange("e (a p) t -> e a (p t)", a=2), pg[0:E, :, 0:4 * T2]))
                dve.sem_inc(g_copied.sem, 1)
                dve.wait_ge(biased.sem, 1)
                link(dve.tensor_tensor(k.x[:], pb[:].rearrange("t a b c -> t (a b) c"), k.x[:], ALU.add))


def expert_phase(nc, k):
    TH = 4 * T2
    NI = I // 128
    with Phase(nc) as ctx:
        ctx.callback(ctx.clear)
        def sb(name, shape, dt=F32):
            return ctx.enter_context(nc.sbuf_tensor(f"e_{name}", shape, dt))

        def sig(name, per=1, primed=0):
            return Signal(nc, ctx, f"e_{name}", per, primed)

        x_hi = sb("x_hi", [128, KC, N], F32R)
        x_lo = sb("x_lo", [128, KC, N], F32R)
        w1 = [sb(f"w1_{j}", [128, KC, 2 * I]) for j in range(2)]
        w2 = [sb(f"w2_{j}", [128, NI, C]) for j in range(2)]
        b1 = [sb(f"b1_{j}", [128, 2 * NI]) for j in range(2)]
        w1_hi = [sb(f"w1_hi{j}", [128, KC, 2 * I], F32R) for j in range(2)]
        w1_lo = [sb(f"w1_lo{j}", [128, KC, 2 * I], F32R) for j in range(2)]
        w2_hi = [sb(f"w2_hi{j}", [128, NI, C], F32R) for j in range(2)]
        w2_lo = [sb(f"w2_lo{j}", [128, NI, C], F32R) for j in range(2)]
        a = [sb(f"a{j}", [128, TH]) for j in range(2)]
        sg = [sb(f"sg{j}", [128, TH]) for j in range(2)]
        bb = [sb(f"bb{j}", [128, TH]) for j in range(2)]
        act_f = [sb(f"act_f{j}", [128, TH]) for j in range(2)]
        act_hi = [sb(f"act_hi{j}", [128, NI, TH], F32R) for j in range(2)]
        act_lo = [sb(f"act_lo{j}", [128, NI, TH], F32R) for j in range(2)]
        ph = [ctx.enter_context(nc.psum_tensor(f"e_ph{j}", [128, 512], F32)) for j in range(6)]
        py = [ctx.enter_context(nc.psum_tensor(f"e_py{j}", [T2, 2, C], F32)) for j in range(2)]

        x_split, x_done = sig("x_split"), sig("x_done")
        loaded = [sig(f"loaded{j}", 48) for j in range(2)]
        w_hi_done = sig("w_hi_done", 4)
        w_lo_done = sig("w_lo_done", 4, 1)
        hidden = sig("hidden", 4 * 2 * NI, 1)
        hid_read = sig("hid_read", 4 * 2 * NI, 1)
        sigmoided = sig("sigmoided", 4 * NI)
        acted = sig("acted", 4 * NI)
        act_hi_done = sig("act_hi_done", 4 * NI)
        act_lo_done = sig("act_lo_done", 4 * NI, 1)
        dve_step = sig("dve_step", 4 * NI * 3)
        mixed = sig("mixed", 4 * 2, 1)
        added = sig("added", 4 * 2, 1)
        stored = sig("stored")
        UN = 4

        with nc.Block() as block:
            @block.sync
            def _(sp):
                with sp.Fori(0, E // 2) as i:
                    for j in range(2):
                        sp.wait_ge(w_lo_done.sem, w_lo_done.at(i, 0))
                        sp.wait_ge(hid_read.sem, hid_read.at(i, 0))
                        e = 2 * i + j
                        sp.dma_start(w1[j][:], k.d_w1[bass.ds(e, 1)].rearrange("a p k n -> (a p) k n")).then_inc(loaded[j].sem, 16)
                        sp.dma_start(w2[j][:], k.d_w2[bass.ds(e, 1)].rearrange("a p k n -> (a p) k n")).then_inc(loaded[j].sem, 16)
                        sp.dma_start(b1[j][:], k.d_b1[bass.ds(e, 1)].rearrange("a p n -> (a p) n")).then_inc(loaded[j].sem, 16)
                sp.wait_ge(added.sem, 1 + (E // 2) * UN * 2)
                sp.dma_start(k.d_out, k.x[:]).then_inc(stored.sem, 16)
                sp.wait_ge(stored.sem, 16)

            @block.scalar
            def _(act):
                act.activation(x_hi[:], k.xT[:], ACT.Copy).then_inc(x_split.sem, 1)
                with act.Fori(0, E // 2) as i:
                    for j in range(2):
                        act.wait_ge(loaded[j].sem, loaded[j].at(i, 48))
                        act.wait_ge(mixed.sem, mixed.at(i, 0))
                        act.activation(w1_hi[j][:], w1[j][:], ACT.Copy).then_inc(w_hi_done.sem, 1)
                        act.activation(w2_hi[j][:], w2[j][:], ACT.Copy).then_inc(w_hi_done.sem, 1)
                    for u in range(UN):
                        for t in range(NI):
                            n = NI * u + t
                            act.wait_ge(hid_read.sem, hid_read.at(i, 2 * n + 2))
                            act.activation(sg[t][:], a[t][:], ACT.Sigmoid, scale=1.702).then_inc(sigmoided.sem, 1)
                            act.wait_ge(acted.sem, acted.at(i, n + 1))
                            act.wait_ge(mixed.sem, mixed.at(i, max(2 * (u - 1), 0)))
                            act.activation(act_hi[u % 2][:, t, :], act_f[t][:], ACT.Copy).then_inc(act_hi_done.sem, 1)

            @block.gpsimd
            def _(pool):
                pool.wait_ge(x_split.sem, 1)
                pool.tensor_tensor(x_lo[:], k.xT[:], x_hi[:].bitcast(F32), ALU.subtract).then_inc(x_done.sem, 1)
                pool.sem_inc(w_lo_done.sem, 1)
                pool.sem_inc(act_lo_done.sem, 1)
                with pool.Fori(0, E // 2) as i:
                    for j in range(2):
                        for n, (raw, hi, lo) in enumerate(((w1, w1_hi, w1_lo), (w2, w2_hi, w2_lo))):
                            pool.wait_ge(w_hi_done.sem, w_hi_done.at(i, 2 * j + n + 1))
                            pool.tensor_tensor(lo[j][:], raw[j][:], hi[j][:].bitcast(F32), ALU.subtract).then_inc(w_lo_done.sem, 1)
                    for u in range(UN):
                        for t in range(NI):
                            n = NI * u + t
                            pool.wait_ge(act_hi_done.sem, act_hi_done.at(i, n + 1))
                            pool.tensor_tensor(act_lo[u % 2][:, t, :], act_f[t][:], act_hi[u % 2][:, t, :].bitcast(F32),
                                               ALU.subtract).then_inc(act_lo_done.sem, 1)

            @block.vector
            def _(dve):
                dve.sem_inc(hid_read.sem, 1)
                dve.sem_inc(added.sem, 1)
                link = Chain(dve, dve_step)
                with dve.Fori(0, E // 2) as i:
                    link.round(i)

                    def add_up(u):
                        j, th = u // 2, u % 2
                        for q in range(2):
                            dve.wait_ge(mixed.sem, mixed.at(i, 2 * u + q + 1))
                            for p2 in range(2):
                                p = 4 * th + 2 * q + p2
                                ins = dve.scalar_tensor_tensor(k.x[:, p, :], py[q][:, p2, :],
                                                               k.gates[:, p, bass.ds(2 * i + j, 1)], k.x[:, p, :],
                                                               ALU.mult, ALU.add)
                            ins.then_inc(added.sem, 1)
                            dve.wait_ge(added.sem, added.at(i, 2 * u + q + 1))

                    for u in range(UN):
                        j = u // 2
                        for t in range(NI):
                            n = NI * u + t
                            dve.wait_ge(hidden.sem, hidden.at(i, 2 * n + 1))
                            dve.wait_ge(act_lo_done.sem, act_lo_done.at(i, max(n - 1, 0)))
                            dve.tensor_scalar(a[t][:], k.ph_at(ph, u, 2 * t),
                                              b1[j][:, 2 * t:2 * t + 1], 7.0, ALU.add, ALU.min).then_inc(hid_read.sem, 1)
                            dve.wait_ge(hidden.sem, hidden.at(i, 2 * n + 2))
                            dve.tensor_scalar(bb[t][:], k.ph_at(ph, u, 2 * t + 1), b1[j][:, 2 * t + 1:2 * t + 2], 7.0,
                                              ALU.add, ALU.min).then_inc(hid_read.sem, 1)
                            dve.wait_ge(hid_read.sem, hid_read.at(i, 2 * n + 2))
                            link(dve.tensor_scalar(bb[t][:], bb[t][:], -7.0, 1.0, ALU.max, ALU.add))
                            link(dve.tensor_tensor(bb[t][:], bb[t][:], a[t][:], ALU.mult))
                            dve.wait_ge(sigmoided.sem, sigmoided.at(i, n + 1))
                            link(dve.tensor_tensor(act_f[t][:], bb[t][:], sg[t][:], ALU.mult))
                            dve.sem_inc(acted.sem, 1)
                        if u >= 1:
                            add_up(u - 1)
                    add_up(UN - 1)
                    link.end()

            @block.tensor
            def _(pe):
                pe.sem_inc(hidden.sem, 1)
                pe.sem_inc(mixed.sem, 1)
                pe.wait_ge(x_done.sem, 1)
                with pe.Fori(0, E // 2) as i:
                    def hidden_layer(u):
                        j, th = u // 2, u % 2
                        if th == 0:
                            pe.wait_ge(w_lo_done.sem, w_lo_done.at(i, 2 * j + 2))
                        for t in range(2 * NI):
                            n = 2 * NI * u + t
                            pe.wait_ge(hid_read.sem, hid_read.at(i, max(2 * NI * (u - 1) + t + 1, 0)))
                            at = (t % 2) * I + (t // 2) * 128
                            terms = [(w, x, kc) for kc in range(KC)
                                     for w, x in ((w1_hi, x_hi), (w1_hi, x_lo), (w1_lo, x_hi))]
                            for m, (w, x, kc) in enumerate(terms):
                                ins = pe.matmul(k.ph_at(ph, u, t), w[j][:, kc, at:at + 128], x[:, kc, th * TH:(th + 1) * TH],
                                                start=m == 0, stop=m == len(terms) - 1)
                            ins.then_inc(hidden.sem, 1)

                    def output_layer(u):
                        j = u // 2
                        pe.wait_ge(act_lo_done.sem, act_lo_done.at(i, NI * (u + 1)))
                        for q in range(2):
                            pe.wait_ge(added.sem, added.at(i, max(2 * u + q - 1, 0)))
                            for p2 in range(2):
                                at = slice((2 * q + p2) * T2, (2 * q + p2 + 1) * T2)
                                terms = [(x, w, t) for t in range(NI)
                                         for x, w in ((act_hi, w2_hi), (act_hi, w2_lo), (act_lo, w2_hi))]
                                for m, (x, w, t) in enumerate(terms):
                                    ins = pe.matmul(py[q][:, p2, :], x[u % 2][:, t, at], w[j][:, t, :],
                                                    start=m == 0, stop=m == len(terms) - 1)
                            ins.then_inc(mixed.sem, 1)

                    for u in range(UN):
                        hidden_layer(u)
                        if u >= 1:
                            output_layer(u - 1)
                    output_layer(UN - 1)


class Shared:

    @staticmethod
    def ph_at(ph, u, t):
        return ph[t][:, 0:4 * T2]


def decoder_layer(nc, d, out):
    k = Shared()
    k.d_attn_w, k.d_attn_wo, k.d_xattn_w = d["attn_w"], d["attn_wo"], d["xattn_w"]
    k.d_ctx, k.d_ctxT, k.d_ctx_wk, k.d_ctx_wv = d["ctx"], d["ctxT"], d["ctx_wk"], d["ctx_wv"]
    k.d_proj_w, k.d_gate_w, k.d_b2, k.d_w1, k.d_w2, k.d_b1 = d["proj_w"], d["gate_w"], d["b2"], d["w1"], d["w2"], d["b1"]
    k.d_out = out.rearrange("(p b) s c -> (b s) p c", b=2)
    k.d_qx = nc.dram_tensor("context_queries", [B, 128, NH, S], F32, kind="Internal").ap()
    k.d_core = nc.dram_tensor("core_quantised", [PAIRS, 128, NH, T2], BF16, kind="Internal").ap()
    k.d_xout = nc.dram_tensor("xout_quantised", [B, 128, NH, S], BF16, kind="Internal").ap()
    with ExitStack() as ctx:
        def sb(name, shape, dt=F32):
            return ctx.enter_context(nc.sbuf_tensor(name, shape, dt))

        k.x = sb("x", [T2, PAIRS, C])
        k.ident = sb("ident", [128, 128])
        k.vec = sb("vec", [128, NV])
        k.rsm = sb("rsm", [128, 2 * NH])
        with ExitStack() as first:
            k.rows = first.enter_context(nc.sbuf_tensor("rows", [128, NR], F32))
            k.cos = first.enter_context(nc.sbuf_tensor("cos", [T2, D], F32))
            k.sin = first.enter_context(nc.sbuf_tensor("sin", [T2, D], F32))
            k.cmask = first.enter_context(nc.sbuf_tensor("cmask", [T2, T2], F32))
            k.xT = first.enter_context(nc.sbuf_tensor("xT_a", [128, KC, N], F32))
            loaded = first.enter_context(nc.semaphore("loaded"))
            smoothed = first.enter_context(nc.semaphore("smoothed"))
            id_zero = first.enter_context(nc.semaphore("id_zero"))
            with nc.Block() as block:
                @block.sync
                def _(sp):
                    sp.dma_start(k.x[:], d["x"].rearrange("(p b) s c -> (b s) p c", b=2)).then_inc(loaded, 16)
                    sp.dma_start(k.vec[:], d["vec"]).then_inc(loaded, 16)
                    sp.dma_start(k.rows[:], d["rows"].to_broadcast([128, NR])).then_inc(loaded, 16)
                    sp.dma_start(k.cos[:], d["cos"]).then_inc(loaded, 16)
                    sp.dma_start(k.sin[:], d["sin"]).then_inc(loaded, 16)
                    sp.dma_start(k.cmask[:], d["cmask"]).then_inc(loaded, 16)
                    sp.wait_ge(loaded, 96)

                @block.gpsimd
                def _(pool):
                    pool.memset(k.ident[:], 0.0).then_inc(id_zero, 1)
                    pool.wait_ge(id_zero, 1)
                    pool.affine_select(out=k.ident[:], in_=k.ident[:], compare_op=ALU.not_equal, fill=1.0, base=0,
                                       pattern=[[-1, 128]], channel_multiplier=1).then_inc(id_zero, 1)
                    pool.wait_ge(id_zero, 2)

                @block.vector
                def _(dve):
                    dve.wait_ge(loaded, 96)
                    dve.reciprocal(k.rsm[:], k.vec[:, V_SM:V_SM + 2 * NH]).then_inc(smoothed, 1)
                    dve.wait_ge(smoothed, 1)
            normalise_phase(nc, k, "attn")
            attn_half(nc, k, 0)
            attn_half(nc, k, 1)
        with ExitStack() as second:
            k.xq = second.enter_context(nc.sbuf_tensor("xq", [128, 4, KC, N], BF16))
            k.bmask = second.enter_context(nc.sbuf_tensor("bmask", [T2, T2], F32))
            bm = second.enter_context(nc.semaphore("bmask_loaded"))
            with nc.Block() as block:
                @block.sync
                def _(sp):
                    sp.dma_start(k.bmask[:], d["bmask"]).then_inc(bm, 16)
                    sp.wait_ge(bm, 16)
            xn_phase(nc, k)
            xattn_half(nc, k, 0)
            xattn_half(nc, k, 1)
        with ExitStack() as third:
            k.c_wraw = third.enter_context(nc.sbuf_tensor("c_wraw", [128, KC, G * D], F32))
            k.qb_all = third.enter_context(nc.sbuf_tensor("qb_all", [HPG * S, G], F32))
            context_phase(nc, k)
        project_phase(nc, k)
        with ExitStack() as fourth:
            k.xh = fourth.enter_context(nc.sbuf_tensor("xh", [T2, PAIRS, C], F32))
            k.xT = fourth.enter_context(nc.sbuf_tensor("xT_f", [128, KC, N], F32))
            k.rows = fourth.enter_context(nc.sbuf_tensor("rows_f", [128, NR], F32))
            k.gates = fourth.enter_context(nc.sbuf_tensor("gates", [T2, PAIRS, E], F32))
            rl = fourth.enter_context(nc.semaphore("rows_loaded"))
            with nc.Block() as block:
                @block.sync
                def _(sp):
                    sp.dma_start(k.rows[:, R_GB:R_GB + E], d["rows"][:, R_GB:R_GB + E].to_broadcast([128, E])).then_inc(rl, 16)
                    sp.wait_ge(rl, 16)
            normalise_phase(nc, k, "ffn")
            gate_phase(nc, k)
            expert_phase(nc, k)


def xn_phase(nc, k):
    normalise_phase(nc, k, "xattn")


def _per_head(w):
    return w.reshape(w.shape[0], KC, 128, D).transpose(2, 0, 1, 3)


def _chunk(w, h0):
    return w[:, h0:h0 + 4].transpose(0, 2, 1, 3).reshape(128, KC, CH)


def _rope():
    inv = 1.0 / np.float32(10000.0) ** (np.arange(0, D, 2, dtype=np.float32) / np.float32(D))
    f = (np.arange(S, dtype=np.float32)[:, None] * inv[None, :].astype(np.float32)).astype(np.float32)
    cos, sin = np.cos(f).astype(np.float32), np.sin(f).astype(np.float32)
    cos = np.tile(np.repeat(cos, 2, axis=1), (2, 1))
    sin = np.tile(np.concatenate([sin, -sin], axis=1), (2, 1))
    return cos, sin


def _masks():
    b = np.arange(T2) // S
    same = b[:, None] == b[None, :]
    causal = same & (np.arange(T2)[:, None] >= np.arange(T2)[None, :])
    return (causal * np.float32(1.0 / np.float32(np.sqrt(D)))).astype(np.float32), np.where(same, 0.0, NEG).astype(np.float32)


def kernel(**inputs):
    import concourse.bacc as _bacc
    from concourse.bass_utils import run_bass_kernel_spmd as _run

    f = {n: np.asarray(a) for n, a in inputs.items()}
    at = {n[len("L0_attn_"):]: a for n, a in f.items() if n.startswith("L0_attn_")}
    xa = {n[len("L0_xattn_"):]: a for n, a in f.items() if n.startswith("L0_xattn_")}
    ff = {n[len("L0_ffn_"):]: a for n, a in f.items() if n.startswith("L0_ffn_")}

    q, kk, v = (_per_head(at[n]) for n in ("W_Q", "W_K", "W_V"))
    attn_w = np.stack([np.stack([_chunk(w, 8 * h + 4 * c) for w in (q, kk, v) for c in range(2)]) for h in range(2)])

    def heads(w):
        return _per_head(w.reshape(-1, D, C).transpose(0, 2, 1))

    wq, wk, wqx, wv = (heads(xa[n]) for n in ("wq", "wk", "wqx", "wv"))
    xattn_w = np.stack([np.stack([_chunk(wq, 8 * h), _chunk(wq, 8 * h + 4), _chunk(wk, 4 * h),
                                  _chunk(wqx, 8 * h), _chunk(wqx, 8 * h + 4), _chunk(wv, 4 * h)]) for h in range(2)])
    kvx = heads(xa["w_kv_x"]).transpose(0, 2, 1, 3)

    def col(a):
        return a.reshape(-1, 128).T

    def one(a):
        return np.broadcast_to(a.reshape(1, 1), (128, 1))

    vec = np.concatenate(
        [col(xa["ln_w"]), col(xa["ln_b"]), col(xa["q_in_scale"]), col(xa["k_in_scale"]), col(xa["qx_in_scale"]),
         col(xa["v_in_scale"]), col(ff["norm_w"])]
        + [col(xa[n]) for n in ("qln_w", "qln_b", "kln_w", "kln_b", "qxln_w", "qxln_b", "kxln_w", "kxln_b")]
        + [one(xa[n]) for n in ("wq_scale", "wk_scale", "wqx_scale", "wv_scale", "proj_w_scale", "proj_in_scale")]
        + [col(xa["proj_smooth"])], axis=1)
    rows = np.concatenate([at[n][8 * h:8 * h + 8].reshape(-1) for h in range(2) for n in ("b_Q", "b_K", "b_V")]
                          + [at["b_O"], ff["gate_b"]]).reshape(1, -1)
    cos, sin = _rope()
    cmask, bmask = _masks()
    ctx = f["ctx_2048"]
    w1 = ff["w1"].reshape(E, I, 2, C).transpose(0, 3, 2, 1).reshape(E, KC, 128, 2 * I).transpose(0, 2, 1, 3)
    b1 = ff["b1"].reshape(E, I // 128, 128, 2).transpose(0, 2, 1, 3).reshape(E, 128, 2 * (I // 128))
    w2 = ff["w2"].transpose(0, 2, 1).reshape(E, I // 128, 128, C).transpose(0, 2, 1, 3)
    arrays = {
        "x": f["x"], "attn_w": attn_w, "attn_wo": at["W_O"].transpose(1, 0, 2), "xattn_w": xattn_w,
        "ctx": ctx.reshape(B, NT_C, TT_C, C).transpose(0, 2, 1, 3),
        "ctxT": ctx.transpose(0, 2, 1).reshape(B, KC, 128, SC),
        "ctx_wk": kvx[:, :, 0:G].reshape(128, KC, G * D), "ctx_wv": kvx[:, :, G:2 * G].reshape(128, KC, G * D),
        "proj_w": xa["wproj"].T.reshape(2 * NH, 128, C).transpose(1, 0, 2),
        "gate_w": ff["gate_w"].T.reshape(KC, 128, E).transpose(1, 0, 2), "b2": ff["b2"],
        "w1": w1, "w2": w2, "b1": b1, "vec": vec, "rows": rows, "cos": cos, "sin": sin, "cmask": cmask, "bmask": bmask,
    }
    arrays = {n: np.ascontiguousarray(a) for n, a in arrays.items()}
    nc = _bacc.Bacc("TRN2", target_bir_lowering=False, num_devices=1)
    d = {n: nc.dram_tensor(n + "_dram", a.shape, mybir.dt.from_np(a.dtype), kind="ExternalInput").ap()
         for n, a in arrays.items()}
    out = nc.dram_tensor("out_dram", (B, S, C), F32, kind="ExternalOutput").ap()
    decoder_layer(nc, d, out)
    r = _run(nc, [{n + "_dram": a for n, a in arrays.items()}], core_ids=[0])
    return r.results[0]["out_dram"]
```

```python
from contextlib import ExitStack

import numpy as np

import concourse.bass as bass
from concourse import mybir

F32 = mybir.dt.float32
F32R = mybir.dt.float32r
BF16 = mybir.dt.bfloat16
U16 = mybir.dt.uint16
ALU = mybir.AluOpType
ACT = mybir.ActivationFunctionType
AX_X = mybir.AxisListType.X

B, S, C = 16, 56, 256
SC = 1500
NH, G, D = 16, 8, 128
HPG = NH // G
KC = C // 128
PAIRS = B // 2
T2 = 2 * S
N = B * S
HH = 8
CH = 512
TT_C, NT_C = 125, 12
E, I, TOPK = 16, 256, 4
SCALE = float(1.0 / np.sqrt(D))
EPS = 1e-5
FP8_MAX = 448.0
NEG = -1.0e30
BN = 6

V_LNW, V_LNB, V_QS, V_KS, V_QXS, V_VS, V_NW = 0, 2, 4, 6, 8, 10, 12
V_QLW, V_QLB, V_KLW, V_KLB, V_QXLW, V_QXLB, V_KXLW, V_KXLB = 14, 15, 16, 17, 18, 19, 20, 21
V_SQ, V_SK, V_SQX, V_SV, V_SPW, V_SPI = 22, 23, 24, 25, 26, 27
V_SM = 28
NV = V_SM + 2 * NH
R_BQKV, R_BO, R_GB = 0, 2 * 6 * CH, 2 * 6 * CH + C
NR = R_GB + E


class Phase(ExitStack):

    def __init__(self, nc):
        super().__init__()
        self.nc, self.sems = nc, []

    def clear(self):
        self.nc.clear_and_free_semaphores(self.sems)
        self.nc.all_engine_barrier()


class Signal:

    def __init__(self, nc, ctx, name, per=1, primed=0):
        self.sem = nc.alloc_semaphore(name)
        ctx.sems.append(self.sem)
        self.per, self.primed = per, primed

    def at(self, i, k):
        return i * self.per + (k + self.primed)


class Chain:

    def __init__(self, eng, step):
        self.eng, self.step, self.i, self.n = eng, step, 0, 0

    def round(self, i):
        self.i, self.n = i, 0

    def __call__(self, ins):
        self.n += 1
        ins.then_inc(self.step.sem, 1)
        self.eng.wait_ge(self.step.sem, self.step.at(self.i, self.n))

    def end(self):
        assert self.n == self.step.per, (self.step.sem, self.n)


def quantise(dve, link, out, y, work, m):
    link(dve.tensor_scalar(y, y, FP8_MAX, -FP8_MAX, ALU.min, ALU.max))
    link(dve.tensor_scalar(m.bitcast(U16), y.bitcast(U16), 0x7F80, None, ALU.bitwise_and))
    link(dve.tensor_scalar(m, m, 2.0 ** -6, 24.0, ALU.max, ALU.mult))
    link(dve.tensor_tensor(work, y, m, ALU.add))
    return dve.tensor_tensor(out, work, m, ALU.subtract)


def normalise_phase(nc, k, mode):
    with Phase(nc) as ctx:
        ctx.callback(ctx.clear)
        def sb(name, shape, dt=F32):
            return ctx.enter_context(nc.sbuf_tensor(f"{mode}_{name}", shape, dt))

        stats = sb("stats", [T2, PAIRS, BN])
        mv = sb("mv", [T2, PAIRS, 2])
        ve = sb("ve", [T2, PAIRS])
        rstd = sb("rstd", [T2, PAIRS])
        shift = sb("shift", [T2, PAIRS])
        mhalf = sb("mhalf", [T2, PAIRS])
        xn = sb("xn", [T2, PAIRS, C])
        xt = [ctx.enter_context(nc.psum_tensor(f"{mode}_xt{j}", [128, 4, 128], F32)) for j in range(4)]
        twice = mode != "attn"
        ready = Signal(nc, ctx, mode + "_ready")
        dve_step = Signal(nc, ctx, mode + "_dve_step")
        pow_in = Signal(nc, ctx, mode + "_pow_in")
        pow_out = Signal(nc, ctx, mode + "_pow_out")
        normed = Signal(nc, ctx, mode + "_normed")
        turned = Signal(nc, ctx, mode + "_turned")
        copied = Signal(nc, ctx, mode + "_copied")
        if mode == "xattn":
            lnt = sb("lnt", [128, KC, N])
            y = sb("y", [128, KC, N], BF16)
            m = sb("m", [128, KC, N], BF16)
            work = sb("work", [128, KC, N], BF16)
            rin = sb("rin", [128, 8])
        with nc.Block() as block:
            @block.gpsimd
            def _(pool):
                pool.memset(mhalf[:], -0.5).then_inc(ready.sem, 1)
                pool.wait_ge(ready.sem, 1)
                for r in range(2 if twice else 1):
                    pool.wait_ge(pow_in.sem, r + 1)
                    pool.tensor_tensor(rstd[:], ve[:], mhalf[:], ALU.pow).then_inc(pow_out.sem, 1)

            @block.vector
            def _(dve):
                link = Chain(dve, dve_step)

                def norm(r, dst, src, scale_only=False):
                    for p in range(PAIRS):
                        ins = dve.bn_stats(stats[:, p, :], src[:, p, :])
                    link(ins)
                    for p in range(PAIRS):
                        ins = dve.bn_aggr(mv[:, p, :], stats[:, p, :])
                    link(ins)
                    if scale_only:
                        link(dve.tensor_tensor(shift[:], mv[:, :, 0], mv[:, :, 0], ALU.mult))
                        link(dve.tensor_tensor(ve[:], mv[:, :, 1], shift[:], ALU.add))
                        link(dve.tensor_scalar(ve[:], ve[:], EPS, None, ALU.add))
                    else:
                        link(dve.tensor_scalar(ve[:], mv[:, :, 1], EPS, None, ALU.add))
                    dve.sem_inc(pow_in.sem, 1)
                    dve.wait_ge(pow_out.sem, r + 1)
                    if not scale_only:
                        link(dve.scalar_tensor_tensor(shift[:], mv[:, :, 0], -1.0, rstd[:], ALU.mult, ALU.mult))
                    for p in range(PAIRS):
                        if scale_only:
                            ins = dve.tensor_scalar(dst[:, p, :], src[:, p, :], rstd[:, p:p + 1], None, ALU.mult)
                        else:
                            ins = dve.tensor_scalar(dst[:, p, :], src[:, p, :], rstd[:, p:p + 1],
                                                    shift[:, p:p + 1], ALU.mult, ALU.add)
                    link(ins)

                if mode == "attn":
                    norm(0, xn, k.x)
                    dve.sem_inc(normed.sem, 1)
                    for p in range(PAIRS):
                        ins = dve.tensor_tensor(k.x[:, p, :], k.x[:, p, :], k.rows[0:T2, R_BO:R_BO + C], ALU.add)
                    link(ins)
                elif mode == "xattn":
                    norm(0, xn, k.x)
                    norm(1, xn, xn)
                    dve.sem_inc(normed.sem, 1)
                    for n, v in enumerate((V_QS, V_KS, V_QXS, V_VS)):
                        ins = dve.reciprocal(rin[:, 2 * n:2 * n + 2], k.vec[:, v:v + 2])
                    link(ins)
                    dve.wait_ge(copied.sem, 4)
                    for n in range(4):
                        for c in range(KC):
                            ins = dve.tensor_scalar(y[:, c, :], lnt[:, c, :], rin[:, 2 * n + c:2 * n + c + 1],
                                                    None, ALU.mult)
                        link(ins)
                        link(quantise(dve, link, k.xq[:, n], y[:], work[:], m[:]))
                else:
                    norm(0, k.xh, k.x)
                    norm(1, xn, k.xh, scale_only=True)
                    dve.sem_inc(normed.sem, 1)

            @block.tensor
            def _(pe):
                pe.wait_ge(normed.sem, 1)
                for j in range(4):
                    for p in range(4):
                        pair, c = 4 * (j % 2) + p, j // 2
                        ins = pe.transpose(xt[j][:, p, 0:T2], xn[:, pair, c * 128:(c + 1) * 128],
                                           k.ident[0:T2, 0:T2])
                    ins.then_inc(turned.sem, 1)

            @block.scalar
            def _(act):
                for j in range(4):
                    act.wait_ge(turned.sem, j + 1)
                    c, t0 = j // 2, (j % 2) * 4 * T2
                    src = xt[j][:, :, 0:T2]
                    dst = (lnt if mode == "xattn" else k.xT)[:, c, t0:t0 + 4 * T2].rearrange("p (a b) -> p a b", a=4)
                    if mode == "attn":
                        ins = act.activation(dst, src, ACT.Copy)
                    elif mode == "xattn":
                        ins = act.activation(dst, src, ACT.Identity, scale=k.vec[:, V_LNW + c:V_LNW + c + 1],
                                             bias=k.vec[:, V_LNB + c:V_LNB + c + 1])
                    else:
                        ins = act.mul(dst, src, k.vec[:, V_NW + c:V_NW + c + 1])
                    ins.then_inc(copied.sem, 1)


def attn_half(nc, k, hh):
    NTC = 4
    with Phase(nc) as ctx:
        ctx.callback(ctx.clear)
        def sb(name, shape, dt=F32):
            return ctx.enter_context(nc.sbuf_tensor(f"a{hh}_{name}", shape, dt))

        def bank(name, shape):
            return ctx.enter_context(nc.psum_tensor(f"a{hh}_{name}", shape, F32))

        def sig(name, per=1, primed=0):
            return Signal(nc, ctx, f"a{hh}_{name}", per, primed)

        w_raw = sb("w_raw", [128, 2, KC, CH])
        w_hi = sb("w_hi", [128, 6, KC, CH], F32R)
        w_lo = sb("w_lo", [128, 6, KC, CH], F32R)
        wo = sb("wo", [128, HH, C])
        bias = k.rows
        x_hi = sb("x_hi", [128, KC, T2], F32R)
        x_lo = sb("x_lo", [128, KC, T2], F32R)
        biased = [sb(f"biased{j}", [T2, CH]) for j in range(2)]
        crossed = [sb(f"crossed{j}", [T2, CH]) for j in range(2)]
        tok = [sb(f"tok{j}", [T2, CH]) for j in range(2)]
        qkT = sb("qkT", [128, 2 * HH, T2])
        v = sb("v", [T2, HH, D])
        sc = [sb(f"sc{j}", [T2, 4, T2]) for j in range(2)]
        ab = [sb(f"ab{j}", [T2, 4, T2]) for j in range(2)]
        sg = [sb(f"sg{j}", [T2, 4, T2]) for j in range(2)]
        mx = sb("mx", [T2, 2, 4])
        sm = sb("sm", [T2, 2, 4])
        aT = [sb(f"aT{j}", [T2, 4, T2]) for j in range(2)]
        zT = sb("zT", [128, HH, T2])
        pj = [bank(f"pj{j}", [T2, CH]) for j in range(2)]
        tp = [bank(f"tp{j}", [128, 4, T2]) for j in range(2)]
        ps = [bank(f"ps{j}", [T2, 4, T2]) for j in range(2)]
        pz = bank("pz", [128, 4, T2])
        po = bank("po", [T2, C])

        w_loaded, wo_loaded, w_hi_done, w_lo_done = sig("w_loaded"), sig("wo_loaded"), sig("w_hi_done"), sig("w_lo_done")
        xhi_done, xlo_done = sig("xhi_done"), sig("xlo_done")
        projected = sig("projected", 6, 1)
        proj_read = sig("proj_read", 6, 1)
        bias_done = sig("bias_done", NTC)
        cross_done = sig("cross_done", NTC)
        tok_done = sig("tok_done", NTC)
        turned = sig("turned", NTC + 2, 1)
        turned_read = sig("turned_read", NTC + 2, 1)
        scored = sig("scored", 2, 1)
        masked = sig("masked", 2, 1)
        signed = sig("signed", 2)
        shifted = sig("shifted", 2)
        exped = sig("exped", 2)
        weighed = sig("weighed", 2)
        mixed = sig("mixed", 2, 1)
        mixed_read = sig("mixed_read", 2, 1)
        summed = sig("summed", 1, 1)
        summed_read = sig("summed_read", 1, 1)
        dve_step = sig("dve_step", 10)

        with nc.Block() as block:
            @block.sync
            def _(sp):
                for c in range(6):
                    if c >= 2:
                        sp.wait_ge(w_lo_done.sem, c - 1)
                    sp.dma_start(w_raw[:, c % 2], k.d_attn_w[hh, c]).then_inc(w_loaded.sem, 16)
                    if c == 0:
                        sp.dma_start(wo[:], k.d_attn_wo[:, hh * HH:(hh + 1) * HH, :]).then_inc(wo_loaded.sem, 16)
                    sp.wait_ge(w_loaded.sem, 16 * (c + 1))

            @block.scalar
            def _(act):
                for c in range(6):
                    act.wait_ge(w_loaded.sem, 16 * (c + 1))
                    act.activation(w_hi[:, c], w_raw[:, c % 2], ACT.Copy).then_inc(w_hi_done.sem, 1)
                act.sem_inc(turned_read.sem, 1)
                act.sem_inc(mixed_read.sem, 1)
                with act.Fori(0, PAIRS) as i:
                    act.wait_ge(projected.sem, projected.at(i, 0))
                    act.activation(x_hi[:], k.xT[:, :, bass.ds(i * T2, T2)], ACT.Copy).then_inc(xhi_done.sem, 1)
                    act.wait_ge(scored.sem, scored.at(i, 0))
                    for c in range(NTC):
                        act.wait_ge(turned.sem, turned.at(i, c + 1))
                        act.activation(qkT[:, 4 * c:4 * c + 4, :], tp[c % 2][:], ACT.Copy).then_inc(turned_read.sem, 1)
                    for s in range(2):
                        act.wait_ge(masked.sem, masked.at(i, s + 1))
                        act.activation(ab[s][:], sc[s][:], ACT.Abs)
                        act.activation(sg[s][:], sc[s][:], ACT.Sign).then_inc(signed.sem, 1)
                    for s in range(2):
                        act.wait_ge(shifted.sem, shifted.at(i, s + 1))
                        act.activation(ab[s][:], ab[s][:], ACT.Exp).then_inc(exped.sem, 1)
                    for s in range(2):
                        act.wait_ge(turned.sem, turned.at(i, NTC + s + 1))
                        act.activation(aT[s][:], tp[s][0:T2], ACT.Copy).then_inc(turned_read.sem, 1)
                        if s == 0:
                            act.wait_ge(summed.sem, summed.at(i, 0))
                        act.wait_ge(mixed.sem, mixed.at(i, s + 1))
                        act.activation(zT[:, 4 * s:4 * s + 4, :], pz[:], ACT.Copy).then_inc(mixed_read.sem, 1)

            @block.gpsimd
            def _(pool):
                for c in range(6):
                    pool.wait_ge(w_hi_done.sem, c + 1)
                    pool.tensor_tensor(w_lo[:, c], w_raw[:, c % 2], w_hi[:, c].bitcast(F32),
                                       ALU.subtract).then_inc(w_lo_done.sem, 1)
                with pool.Fori(0, PAIRS) as i:
                    pool.wait_ge(xhi_done.sem, xhi_done.at(i, 1))
                    pool.tensor_tensor(x_lo[:], k.xT[:, :, bass.ds(i * T2, T2)], x_hi[:].bitcast(F32),
                                       ALU.subtract).then_inc(xlo_done.sem, 1)
                    for c in range(NTC):
                        pool.wait_ge(bias_done.sem, bias_done.at(i, c + 1))
                        src = biased[c % 2][:].rearrange("p (h e two) -> p h e two", h=4, two=2)
                        dst = crossed[c % 2][:].rearrange("p (h e two) -> p h e two", h=4, two=2)
                        sin = k.sin[:, 0:D // 2].unsqueeze(1).to_broadcast([T2, 4, D // 2])
                        nsin = k.sin[:, D // 2:D].unsqueeze(1).to_broadcast([T2, 4, D // 2])
                        pool.tensor_tensor(dst[:, :, :, 0], src[:, :, :, 1], nsin, ALU.mult)
                        pool.tensor_tensor(dst[:, :, :, 1], src[:, :, :, 0], sin, ALU.mult).then_inc(cross_done.sem, 1)

            @block.vector
            def _(dve):
                link = Chain(dve, dve_step)
                for s in (proj_read, masked, summed_read):
                    dve.sem_inc(s.sem, 1)
                with dve.Fori(0, PAIRS) as i:
                    link.round(i)

                    def add_bias(c):
                        dve.wait_ge(projected.sem, projected.at(i, c + 1))
                        out = biased[c % 2][:] if c < NTC else v[:, 4 * (c - NTC):4 * (c - NTC) + 4, :].rearrange("p h e -> p (h e)")
                        if c == NTC:
                            dve.wait_ge(mixed.sem, mixed.at(i, 0))
                        at = R_BQKV + (hh * 6 + c) * CH
                        return dve.tensor_tensor(out, pj[c % 2][:], bias[0:T2, at:at + CH], ALU.add)

                    for c in range(NTC):
                        ins = add_bias(c)
                        ins.then_inc(bias_done.sem, 1)
                        dve.wait_ge(bias_done.sem, bias_done.at(i, c + 1))
                        dve.wait_ge(turned.sem, turned.at(i, max(c - 1, 0)))
                        cos = k.cos[:, :].unsqueeze(1).to_broadcast([T2, 4, D])
                        t3 = tok[c % 2][:].rearrange("p (h e) -> p h e", h=4)
                        dve.tensor_tensor(t3, biased[c % 2][:].rearrange("p (h e) -> p h e", h=4), cos,
                                          ALU.mult).then_inc(proj_read.sem, 1)
                        dve.wait_ge(proj_read.sem, proj_read.at(i, c + 1))
                        dve.wait_ge(cross_done.sem, cross_done.at(i, c + 1))
                        dve.tensor_tensor(tok[c % 2][:], tok[c % 2][:], crossed[c % 2][:], ALU.add).then_inc(tok_done.sem, 1)
                    for c in range(NTC, 6):
                        add_bias(c).then_inc(proj_read.sem, 1)
                    for s in range(2):
                        dve.wait_ge(scored.sem, scored.at(i, s + 1))
                        link(dve.tensor_tensor(sc[s][:], ps[s][:],
                                               k.cmask[:, :].unsqueeze(1).to_broadcast([T2, 4, T2]), ALU.mult))
                        dve.tensor_reduce(mx[:, s, :], sc[s][:], AX_X, ALU.max,
                                          apply_absolute_value=True).then_inc(masked.sem, 1)
                    for s in range(2):
                        dve.wait_ge(signed.sem, signed.at(i, s + 1))
                        dve.wait_ge(masked.sem, masked.at(i, s + 1))
                        dve.tensor_tensor(ab[s][:], ab[s][:], mx[:, s, :].unsqueeze(2).to_broadcast([T2, 4, T2]),
                                          ALU.subtract).then_inc(shifted.sem, 1)
                    for s in range(2):
                        dve.wait_ge(exped.sem, exped.at(i, s + 1))
                        link(dve.tensor_tensor(sc[s][:], ab[s][:], sg[s][:], ALU.mult))
                        link(dve.tensor_reduce(sm[:, s, :], sc[s][:], AX_X, ALU.add, apply_absolute_value=True))
                        link(dve.tensor_scalar(sm[:, s, :], sm[:, s, :], 1e-6, None, ALU.add))
                        link(dve.reciprocal(sm[:, s, :], sm[:, s, :]))
                        dve.tensor_tensor(sc[s][:], sc[s][:], sm[:, s, :].unsqueeze(2).to_broadcast([T2, 4, T2]),
                                          ALU.mult).then_inc(weighed.sem, 1)
                    dve.wait_ge(summed.sem, summed.at(i, 1))
                    xp = k.x[:, bass.ds(i, 1), :].rearrange("p a c -> p (a c)")
                    dve.tensor_tensor(xp, po[:], xp, ALU.add).then_inc(summed_read.sem, 1)
                    link.end()

            @block.tensor
            def _(pe):
                for s in (projected, turned, scored, mixed, summed):
                    pe.sem_inc(s.sem, 1)
                pe.wait_ge(w_lo_done.sem, 6)
                pe.wait_ge(wo_loaded.sem, 16)
                with pe.Fori(0, PAIRS) as i:
                    pe.wait_ge(xlo_done.sem, xlo_done.at(i, 1))

                    def project(c):
                        pe.wait_ge(proj_read.sem, proj_read.at(i, max(c - 1, 0)))
                        terms = [(x, w, kc) for kc in range(KC) for x, w in ((x_hi, w_hi), (x_hi, w_lo), (x_lo, w_hi))]
                        for n, (x, w, kc) in enumerate(terms):
                            ins = pe.matmul(pj[c % 2][:], x[:, kc, :], w[:, c, kc, :], start=n == 0,
                                            stop=n == len(terms) - 1)
                        ins.then_inc(projected.sem, 1)

                    def turn(c):
                        pe.wait_ge(tok_done.sem, tok_done.at(i, c + 1))
                        pe.wait_ge(turned_read.sem, turned_read.at(i, max(c - 1, 0)))
                        for h in range(4):
                            ins = pe.transpose(tp[c % 2][:, h, :], tok[c % 2][:, h * D:(h + 1) * D], k.ident[0:T2, 0:T2])
                        ins.then_inc(turned.sem, 1)

                    for c in range(6):
                        project(c)
                        if 1 <= c <= NTC:
                            turn(c - 1)
                    for s in range(2):
                        pe.wait_ge(turned_read.sem, turned_read.at(i, NTC))
                        pe.wait_ge(masked.sem, masked.at(i, 0))
                        for h in range(4):
                            ins = pe.matmul(ps[s][:, h, :], qkT[:, 4 * s + h, :], qkT[:, HH + 4 * s + h, :],
                                            start=True, stop=True)
                        ins.then_inc(scored.sem, 1)
                    for s in range(2):
                        pe.wait_ge(weighed.sem, weighed.at(i, s + 1))
                        for h in range(4):
                            ins = pe.transpose(tp[s][0:T2, h, :], sc[s][:, h, :], k.ident[0:T2, 0:T2])
                        ins.then_inc(turned.sem, 1)
                    for s in range(2):
                        pe.wait_ge(turned_read.sem, turned_read.at(i, NTC + s + 1))
                        pe.wait_ge(proj_read.sem, proj_read.at(i, 6))
                        pe.wait_ge(mixed_read.sem, mixed_read.at(i, s))
                        for h in range(4):
                            ins = pe.matmul(pz[:, h, :], v[:, 4 * s + h, :], aT[s][:, h, :], start=True, stop=True)
                        ins.then_inc(mixed.sem, 1)
                    pe.wait_ge(mixed_read.sem, mixed_read.at(i, 2))
                    pe.wait_ge(summed_read.sem, summed_read.at(i, 0))
                    for h in range(HH):
                        ins = pe.matmul(po[:], zT[:, h, :], wo[:, h, :], start=h == 0, stop=h == HH - 1)
                    ins.then_inc(summed.sem, 1)


def xattn_half(nc, k, hh):
    NTC = 5
    SRC = (0, 0, 1, 2, 2, 3)
    INS = (V_QS, V_QS, V_KS, V_QXS, V_QXS, V_VS)
    OUTS = (V_SQ, V_SQ, V_SK, V_SQX, V_SQX, V_SV)
    LNW = (V_QLW, V_QLW, V_KLW, V_QXLW, V_QXLW)
    with Phase(nc) as ctx:
        ctx.callback(ctx.clear)
        def sb(name, shape, dt=F32):
            return ctx.enter_context(nc.sbuf_tensor(f"b{hh}_{name}", shape, dt))

        def bank(name, shape):
            return ctx.enter_context(nc.psum_tensor(f"b{hh}_{name}", shape, F32))

        def sig(name, per=1, primed=0):
            return Signal(nc, ctx, f"b{hh}_{name}", per, primed)

        w_raw = sb("w_raw", [128, 2, KC, CH])
        w_mean = sb("w_mean", [128, KC * 4])
        w_hi = sb("w_hi", [128, 6, KC, CH], F32R)
        w_lo = sb("w_lo", [128, 6, KC, CH], F32R)
        xq = sb("xq_pair", [128, 4, KC, T2], F32R)
        sq = [sb(f"sq{j}", [T2, CH]) for j in range(2)]
        ss = sb("ss", [T2, 2, 4])
        rs = sb("rs", [T2, 2, 4])
        mhalf = sb("mhalf", [T2, 4])
        tok = [sb(f"tok{j}", [T2, CH]) for j in range(2)]
        qkT = sb("qkT", [128, HH + 4, T2])
        qxT = sb("qxT", [128, HH, T2])
        qxs = sb("qxs", [128, HH, T2])
        qx_hi = sb("qx_hi", [128, HH, T2], F32R)
        qx_lo = sb("qx_lo", [128, HH, T2], F32R)
        qb = sb("qb", [T2, HPG, 4])
        v = sb("v", [T2, 4, D])
        sc = [sb(f"sc{j}", [T2, 4, T2]) for j in range(2)]
        mx = sb("mx", [T2, 2, 4])
        sm = sb("sm", [T2, 2, 4])
        aT = [sb(f"aT{j}", [T2, 4, T2]) for j in range(2)]
        y = [sb(f"y{j}", [128, 4, T2], BF16) for j in range(2)]
        m = sb("m", [128, 4, T2], BF16)
        work = sb("work", [128, 4, T2], BF16)
        cq = sb("cq", [128, HH, T2], BF16)
        pj = [bank(f"pj{j}", [T2, CH]) for j in range(3)]
        tp = [bank(f"tp{j}", [128, 4, T2]) for j in range(2)]
        ps = [bank(f"ps{j}", [T2, 4, T2]) for j in range(2)]
        pzb = bank("pz", [128, 512])
        pz = pzb[:, 0:4 * T2].rearrange("p (h t) -> p h t", h=4)
        pqb = pzb[0:T2, 4 * T2:4 * T2 + HH].rearrange("p (a g) -> p a g", a=HPG)

        w_loaded, w_ready, w_hi_done, w_lo_done = sig("w_loaded"), sig("w_ready"), sig("w_hi_done"), sig("w_lo_done")
        prep_step = sig("prep_step", 6 * 4)
        half_set = sig("half_set")
        xq_done = sig("xq_done")
        projected = sig("projected", 6, 1)
        squared = sig("squared", NTC)
        vared = sig("vared", NTC)
        powed = sig("powed", NTC)
        tok_done = sig("tok_done", 6, 1)
        turned = sig("turned", NTC + 2, 1)
        turned_read = sig("turned_read", NTC + 2, 1)
        qb_made = sig("qb_made")
        qb_done = sig("qb_done", 1, 1)
        dma_begun = sig("dma_begun")
        qxs_done = sig("qxs_done")
        qx_hi_done = sig("qx_hi_done")
        qx_lo_done = sig("qx_lo_done")
        qx_stored = sig("qx_stored")
        scored = sig("scored", 2, 1)
        masked = sig("masked", 2, 1)
        shifted = sig("shifted", 2)
        exped = sig("exped", 2)
        weighed = sig("weighed", 2)
        mixed = sig("mixed", 2, 1)
        mixed_read = sig("mixed_read", 2, 1)
        cq_done = sig("cq_done", 2)
        cq_stored = sig("cq_stored")
        dve_step = sig("dve_step", 0)

        with nc.Block() as block:
            @block.sync
            def _(sp):
                for c in range(6):
                    if c >= 2:
                        sp.wait_ge(w_lo_done.sem, c - 1)
                    sp.dma_start(w_raw[:, c % 2], k.d_xattn_w[hh, c]).then_inc(w_loaded.sem, 16)
                    sp.wait_ge(w_loaded.sem, 16 * (c + 1))
                sp.sem_inc(qx_stored.sem, 16)
                sp.sem_inc(cq_stored.sem, 16)
                with sp.Fori(0, PAIRS) as i:
                    sp.wait_ge(qx_lo_done.sem, qx_lo_done.at(i, 1))
                    sp.sem_inc(dma_begun.sem, 1)
                    sp.wait_ge(qb_done.sem, qb_done.at(i, 1))
                    sp.sem_inc(dma_begun.sem, 1)
                    for b2 in range(2):
                        for src, dst in ((qx_hi, k.d_qhi), (qx_lo, k.d_qlo)):
                            sp.dma_start(dst[bass.ds(2 * i + b2, 1), :, hh * HH:(hh + 1) * HH, :]
                                         .rearrange("a p h s -> p (a h) s"),
                                         src[:, :, b2 * S:(b2 + 1) * S].bitcast(F32)).then_inc(qx_stored.sem, 16)
                        for a in range(HPG):
                            sp.dma_start(k.d_qb[bass.ds(2 * i + b2, 1), a * S:(a + 1) * S, 4 * hh:4 * hh + 4]
                                         .rearrange("a s g -> (a s) g"),
                                         qb[b2 * S:(b2 + 1) * S, a, :]).then_inc(qx_stored.sem, 16)
                    sp.wait_ge(cq_done.sem, cq_done.at(i, 2))
                    sp.dma_start(k.d_core[bass.ds(i, 1), :, hh * HH:(hh + 1) * HH, :]
                                 .rearrange("a p h s -> p (a h) s"), cq[:]).then_inc(cq_stored.sem, 16)
                sp.wait_ge(qx_stored.sem, 16 + 128 * PAIRS)
                sp.wait_ge(cq_stored.sem, 16 + 16 * PAIRS)

            @block.scalar
            def _(act):
                for c in range(6):
                    act.wait_ge(w_ready.sem, c + 1)
                    act.activation(w_hi[:, c], w_raw[:, c % 2], ACT.Copy).then_inc(w_hi_done.sem, 1)
                act.sem_inc(turned_read.sem, 1)
                with act.Fori(0, PAIRS) as i:
                    act.wait_ge(projected.sem, projected.at(i, 0))
                    act.activation(xq[:].rearrange("p n k t -> p (n k) t"),
                                   k.xq[:, :, :, bass.ds(i * T2, T2)].rearrange("p n k t -> p (n k) t"),
                                   ACT.Copy).then_inc(xq_done.sem, 1)

                    def unturn(c):
                        act.wait_ge(turned.sem, turned.at(i, c + 1))
                        if c == 0:
                            act.wait_ge(scored.sem, scored.at(i, 0))
                        if c == 3:
                            act.wait_ge(qb_done.sem, qb_done.at(i, 0))
                        dst = qkT[:, 4 * c:4 * c + 4, :] if c < 3 else qxT[:, 4 * (c - 3):4 * (c - 3) + 4, :]
                        act.activation(dst, tp[c % 2][:], ACT.Identity, scale=k.vec[:, LNW[c]:LNW[c] + 1],
                                       bias=k.vec[:, LNW[c] + 1:LNW[c] + 2]).then_inc(turned_read.sem, 1)

                    for c in range(NTC):
                        act.wait_ge(projected.sem, projected.at(i, c + 1))
                        if c >= 2:
                            act.wait_ge(vared.sem, vared.at(i, c - 1))
                        act.activation(sq[c % 2][:], pj[c % 3][:], ACT.Square).then_inc(squared.sem, 1)
                        if c >= 2:
                            unturn(c - 2)
                    unturn(NTC - 2)
                    unturn(NTC - 1)
                    act.wait_ge(qxs_done.sem, qxs_done.at(i, 1))
                    act.wait_ge(qx_stored.sem, 128 * i + 16)
                    act.activation(qx_hi[:], qxs[:], ACT.Copy).then_inc(qx_hi_done.sem, 1)
                    for s in range(2):
                        act.wait_ge(shifted.sem, shifted.at(i, s + 1))
                        act.activation(sc[s][:], sc[s][:], ACT.Exp, scale=SCALE).then_inc(exped.sem, 1)
                    for s in range(2):
                        act.wait_ge(turned.sem, turned.at(i, NTC + s + 1))
                        act.activation(aT[s][:], tp[(NTC + s) % 2][0:T2], ACT.Copy).then_inc(turned_read.sem, 1)

            @block.gpsimd
            def _(pool):
                pool.memset(mhalf[:], -0.5).then_inc(half_set.sem, 1)
                pool.wait_ge(half_set.sem, 1)
                for c in range(6):
                    pool.wait_ge(w_hi_done.sem, c + 1)
                    pool.tensor_tensor(w_lo[:, c], w_raw[:, c % 2], w_hi[:, c].bitcast(F32),
                                       ALU.subtract).then_inc(w_lo_done.sem, 1)
                with pool.Fori(0, PAIRS) as i:
                    for c in range(NTC):
                        pool.wait_ge(vared.sem, vared.at(i, c + 1))
                        pool.tensor_tensor(rs[:, c % 2, :], ss[:, c % 2, :], mhalf[:], ALU.pow).then_inc(powed.sem, 1)
                    pool.wait_ge(qx_hi_done.sem, qx_hi_done.at(i, 1))
                    pool.tensor_tensor(qx_lo[:], qxs[:], qx_hi[:].bitcast(F32), ALU.subtract).then_inc(qx_lo_done.sem, 1)

            @block.vector
            def _(dve):
                prep = Chain(dve, prep_step)
                for c in range(6):
                    dve.wait_ge(w_loaded.sem, 16 * (c + 1))
                    raw = w_raw[:, c % 2]
                    for kc in range(KC):
                        ins = dve.tensor_scalar(raw[:, kc], raw[:, kc], k.vec[:, INS[c] + kc:INS[c] + kc + 1],
                                                k.vec[:, OUTS[c]:OUTS[c] + 1], ALU.mult, ALU.mult)
                    prep(ins)
                    if c < NTC:
                        heads = raw.rearrange("p k (h e) -> p (k h) e", h=4)
                        prep(dve.tensor_reduce(w_mean[:], heads, AX_X, ALU.add))
                        prep(dve.tensor_scalar(w_mean[:], w_mean[:], 1.0 / D, None, ALU.mult))
                        dve.tensor_tensor(heads, heads, w_mean[:].unsqueeze(2).to_broadcast([128, KC * 4, D]),
                                          ALU.subtract).then_inc(w_ready.sem, 1)
                    else:
                        dve.sem_inc(w_ready.sem, 1)
                for s in (tok_done, masked, mixed_read, qb_done):
                    dve.sem_inc(s.sem, 1)
                link = Chain(dve, dve_step)
                with dve.Fori(0, PAIRS) as i:
                    link.round(i)
                    dve_step.per = 33

                    def normalise(c):
                        dve.wait_ge(powed.sem, powed.at(i, c + 1))
                        dve.wait_ge(turned.sem, turned.at(i, max(c - 1, 0)))
                        dve.tensor_tensor(tok[c % 2][:].rearrange("p (h e) -> p h e", h=4),
                                          pj[c % 3][:].rearrange("p (h e) -> p h e", h=4),
                                          rs[:, c % 2, :].unsqueeze(2).to_broadcast([T2, 4, D]),
                                          ALU.mult).then_inc(tok_done.sem, 1)

                    for c in range(NTC):
                        dve.wait_ge(squared.sem, squared.at(i, c + 1))
                        link(dve.tensor_reduce(ss[:, c % 2, :], sq[c % 2][:].rearrange("p (h e) -> p h e", h=4),
                                               AX_X, ALU.add))
                        dve.tensor_scalar(ss[:, c % 2, :], ss[:, c % 2, :], 1.0 / D, EPS, ALU.mult,
                                          ALU.add).then_inc(vared.sem, 1)
                        if c >= 1:
                            normalise(c - 1)
                    normalise(NTC - 1)
                    dve.wait_ge(projected.sem, projected.at(i, 6))
                    dve.wait_ge(mixed.sem, mixed.at(i, 0))
                    dve.tensor_copy(v[:].rearrange("p h e -> p (h e)"), pj[5 % 3][:]).then_inc(tok_done.sem, 1)
                    dve.wait_ge(turned_read.sem, turned_read.at(i, NTC))
                    dve.wait_ge(qx_stored.sem, 128 * i + 16)
                    dve.tensor_scalar(qxs[:], qxT[:], k.vec[:, V_KXLW:V_KXLW + 1], None, ALU.mult).then_inc(qxs_done.sem, 1)
                    dve.wait_ge(qxs_done.sem, qxs_done.at(i, 1))
                    dve.wait_ge(qb_made.sem, qb_made.at(i, 1))
                    dve.tensor_copy(qb[:], pqb).then_inc(qb_done.sem, 1)
                    for s in range(2):
                        dve.wait_ge(scored.sem, scored.at(i, s + 1))
                        link(dve.tensor_tensor(sc[s][:], ps[s][:],
                                               k.bmask[:, :].unsqueeze(1).to_broadcast([T2, 4, T2]), ALU.add))
                        dve.tensor_reduce(mx[:, s, :], sc[s][:], AX_X, ALU.max).then_inc(masked.sem, 1)
                        dve.wait_ge(masked.sem, masked.at(i, s + 1))
                        dve.tensor_tensor(sc[s][:], sc[s][:], mx[:, s, :].unsqueeze(2).to_broadcast([T2, 4, T2]),
                                          ALU.subtract).then_inc(shifted.sem, 1)
                    for s in range(2):
                        dve.wait_ge(exped.sem, exped.at(i, s + 1))
                        link(dve.tensor_reduce(sm[:, s, :], sc[s][:], AX_X, ALU.add))
                        link(dve.reciprocal(sm[:, s, :], sm[:, s, :]))
                        dve.tensor_tensor(sc[s][:], sc[s][:], sm[:, s, :].unsqueeze(2).to_broadcast([T2, 4, T2]),
                                          ALU.mult).then_inc(weighed.sem, 1)
                    dve.wait_ge(cq_stored.sem, 16 * i + 16)
                    for s in range(2):
                        dve.wait_ge(mixed.sem, mixed.at(i, s + 1))
                        smooth = k.rsm[:, hh * HH + 4 * s:hh * HH + 4 * s + 4].unsqueeze(2).to_broadcast([128, 4, T2])
                        dve.tensor_tensor(y[s][:], pz, smooth, ALU.mult).then_inc(mixed_read.sem, 1)
                        dve.wait_ge(mixed_read.sem, mixed_read.at(i, s + 1))
                        quantise(dve, link, cq[:, 4 * s:4 * s + 4, :], y[s][:], work[:], m[:]).then_inc(cq_done.sem, 1)
                        dve.wait_ge(cq_done.sem, cq_done.at(i, s + 1))
                    assert link.n <= 33
                    dve.sem_inc(dve_step.sem, 33 - link.n)

            @block.tensor
            def _(pe):
                for s in (projected, turned, scored, mixed):
                    pe.sem_inc(s.sem, 1)
                pe.wait_ge(w_lo_done.sem, 6)
                with pe.Fori(0, PAIRS) as i:
                    pe.wait_ge(xq_done.sem, xq_done.at(i, 1))

                    def project(c):
                        pe.wait_ge(tok_done.sem, tok_done.at(i, max(c - 2, 0)))
                        for n in range(2 * KC):
                            w = (w_hi, w_lo)[n % 2]
                            ins = pe.matmul(pj[c % 3][:], xq[:, SRC[c], n // 2, :], w[:, c, n // 2, :],
                                            start=n == 0, stop=n == 2 * KC - 1)
                        ins.then_inc(projected.sem, 1)

                    def turn(c):
                        pe.wait_ge(tok_done.sem, tok_done.at(i, c + 1))
                        pe.wait_ge(turned_read.sem, turned_read.at(i, max(c - 1, 0)))
                        for h in range(4):
                            ins = pe.transpose(tp[c % 2][:, h, :], tok[c % 2][:, h * D:(h + 1) * D], k.ident[0:T2, 0:T2])
                        ins.then_inc(turned.sem, 1)

                    for c in range(6):
                        project(c)
                        if c >= 2:
                            turn(c - 2)
                    turn(NTC - 1)
                    pe.wait_ge(turned_read.sem, turned_read.at(i, NTC))
                    pe.wait_ge(mixed_read.sem, mixed_read.at(i, 0))
                    for h in range(HH):
                        ins = pe.matmul(pqb[:, h % HPG, h // HPG:h // HPG + 1], qxT[:, h, :],
                                        k.vec[:, V_KXLB:V_KXLB + 1], start=True, stop=True)
                    ins.then_inc(qb_made.sem, 1)
                    for s in range(2):
                        pe.wait_ge(turned_read.sem, turned_read.at(i, 3))
                        pe.wait_ge(masked.sem, masked.at(i, 0))
                        for h in range(4):
                            ins = pe.matmul(ps[s][:, h, :], qkT[:, 4 * s + h, :], qkT[:, HH + (4 * s + h) // HPG, :],
                                            start=True, stop=True)
                        ins.then_inc(scored.sem, 1)
                    for s in range(2):
                        pe.wait_ge(weighed.sem, weighed.at(i, s + 1))
                        pe.wait_ge(turned_read.sem, turned_read.at(i, NTC + s - 1))
                        for h in range(4):
                            ins = pe.transpose(tp[(NTC + s) % 2][0:T2, h, :], sc[s][:, h, :], k.ident[0:T2, 0:T2])
                        ins.then_inc(turned.sem, 1)
                    for s in range(2):
                        pe.wait_ge(turned_read.sem, turned_read.at(i, NTC + s + 1))
                        pe.wait_ge(tok_done.sem, tok_done.at(i, 6))
                        pe.wait_ge(mixed_read.sem, mixed_read.at(i, s))
                        for h in range(4):
                            ins = pe.matmul(pz[:, h, :], v[:, (4 * s + h) // HPG, :], aT[s][:, h, :], start=True, stop=True)
                        ins.then_inc(mixed.sem, 1)


def context_phase(nc, k):
    QN = HPG * S
    NS = G
    DT = 2 * TT_C
    ND = SC // DT
    PER = 4 * ND
    PC = 3
    NPC = NT_C // PC
    L_SCORE, L_TURN, L_MIX, L_OUT = 3, 4, 5, 6
    with Phase(nc) as ctx:
        ctx.callback(ctx.clear)

        def sb(name, shape, dt=F32):
            return ctx.enter_context(nc.sbuf_tensor(f"c_{name}", shape, dt))

        def sig(name, per=1):
            return Signal(nc, ctx, f"c_{name}", per)

        wk_hi = sb("wk_hi", [128, KC, G * D], F32R)
        wk_lo = sb("wk_lo", [128, KC, G * D], F32R)
        wv = sb("wv", [128, KC, G * D])
        stageT = [sb(f"stageT{j}", [128, KC, DT]) for j in range(3)]
        stageC = [sb(f"stageC{j}", [TT_C, PC, C]) for j in range(2)]
        cT_hi = sb("cT_hi", [128, KC, SC], F32R)
        cT_lo = sb("cT_lo", [128, KC, SC], F32R)
        c_hi = sb("c_hi", [TT_C, NT_C, C], F32R)
        c_lo = sb("c_lo", [TT_C, NT_C, C], F32R)
        q_hi = sb("q_hi", [128, NH, S], F32R)
        q_lo = sb("q_lo", [128, NH, S], F32R)
        qb = sb("qb", [QN, G])
        kT_hi = sb("kT_hi", [128, 2, 2, SC], F32R)
        kT_lo = sb("kT_lo", [128, 2, 2, SC], F32R)
        sq = [sb(f"sq{j}", [TT_C, 4, D]) for j in range(2)]
        kn = [sb(f"kn{j}", [TT_C, 4, D]) for j in range(2)]
        ss = sb("ss", [TT_C, 4, 4])
        rs = sb("rs", [TT_C, 4, 4])
        mhalf = sb("mhalf", [128, 4])
        P = [sb(f"P{j}", [QN, SC]) for j in range(2)]
        PT_hi = [sb(f"PT_hi{j}", [TT_C, NT_C, QN], F32R) for j in range(2)]
        PT_lo = [sb(f"PT_lo{j}", [TT_C, NT_C, QN], F32R) for j in range(2)]
        w_mean = sb("w_mean", [128, KC * G])
        mx = sb("mx", [QN, 2])
        ebias = sb("ebias", [QN, 2])
        esum = sb("esum", [QN, 4])
        rsum = sb("rsum", [QN, 4])
        U = sb("U", [QN, C])
        UT = sb("UT", [128, KC, QN])
        y = sb("y", [128, HPG, S], BF16)
        m_ = sb("m", [128, HPG, S], BF16)
        work = sb("work", [128, HPG, S], BF16)
        cq = sb("cq", [128, NH, S], BF16)
        p_scores = ctx.enter_context(nc.psum_tensor("c_scores", [128, 3, 512], F32))
        p_keys = [ctx.enter_context(nc.psum_tensor(f"c_keys{j}", [128, 4, D], F32)) for j in range(2)]
        p_kturn = ctx.enter_context(nc.psum_tensor("c_kturn", [128, 512], F32))
        p_pturn = ctx.enter_context(nc.psum_tensor("c_pturn", [128, 4, 128], F32))
        p_mix = ctx.enter_context(nc.psum_tensor("c_mix", [128, 512], F32))
        scores = p_scores[0:QN, :, 0:SC // 3]
        kturned = p_kturn[:, 0:2 * DT].rearrange("p (g t) -> p g t", g=2)
        pturned = p_pturn[0:TT_C, :, 0:QN]
        ut_at, out_at = p_mix[:, C:C + KC * QN], p_mix[:, C:C + QN]

        w_loaded, w_ready, w_hi_done, w_lo_done = sig("w_loaded"), sig("w_ready"), sig("w_hi_done"), sig("w_lo_done")
        prep_step = sig("prep_step", 2)
        half_set = sig("half_set")
        stagedT = [sig(f"stagedT{j}", 2 * 16) for j in range(3)]
        stagedC = [sig(f"stagedC{j}", 2 * 16) for j in range(2)]
        cT_hi_done, cT_lo_done = sig("cT_hi_done", ND), sig("cT_lo_done", ND)
        c_hi_done, c_lo_done = sig("c_hi_done", NPC), sig("c_lo_done", NPC)
        q_loaded = [sig(f"q_loaded{j}", 48) for j in range(2)]
        projected, squared, vared, powed = sig("projected", PER), sig("squared", PER), sig("vared", PER), sig("powed", PER)
        kn_done, k_turned = sig("kn_done", PER), sig("k_turned", PER)
        kT_hi_done, kT_lo_done = sig("kT_hi_done", PER), sig("kT_lo_done", PER)
        scored, biased, exped, rsum_done = sig("scored", NS), sig("biased", NS), sig("exped", NS), sig("rsum_done", NS)
        p_turned, PT_hi_done, PT_lo_done = sig("p_turned", 3 * NS), sig("PT_hi_done", 3 * NS), sig("PT_lo_done", 3 * NS)
        mixed = sig("mixed", 3 * NS)
        U_done, U_turned, UT_done = sig("U_done", NS), sig("U_turned", NS), sig("UT_done", NS)
        out_done, out_read, cq_done = sig("out_done", NS), sig("out_read", NS), sig("cq_done", NS)
        cq_stored = [sig(f"cq_stored{j}", 16) for j in range(2)]
        dma_begun = sig("dma_begun")
        r_step, b_step, q_step = sig("r_step", PER), sig("b_step", 2 * NS), sig("q_step", 4 * NS)

        def wait(eng, signal_of, b, n):
            if not isinstance(b, int) or signal_of.at(b, n) > 0:
                eng.wait_ge(signal_of.sem, signal_of.at(b, n))

        def there(b, m):
            return not isinstance(b, int) or 0 <= NS * b + m < NS * B

        def run(eng, body):
            body(0)
            with eng.Fori(1, B) as b:
                body(b)
            body(B)

        def steps(b):
            return range(NS if not isinstance(b, int) or b < B else L_OUT)

        def keys_in(b):
            return not isinstance(b, int) or b < B

        with nc.Block() as block:
            @block.sync
            def _(sp):
                for t in range(KC):
                    sp.dma_start(k.c_wraw[:, t], k.d_ctx_wk[:, t]).then_inc(w_loaded.sem, 16)
                sp.dma_start(wv[:], k.d_ctx_wv).then_inc(w_loaded.sem, 16)

                def body(b):
                    def load_T(d):
                        wait(sp, cT_lo_done, b, d - 2)
                        sp.sem_inc(dma_begun.sem, 1)
                        sp.dma_start(stageT[d % 3][:], k.d_ctxT[bass.ds(b, 1), :, :, d * DT:(d + 1) * DT]
                                     .rearrange("a k p t -> p (a k) t")).then_inc(stagedT[d % 3].sem, 16)

                    def load_C(p):
                        wait(sp, c_lo_done, b, p - 1)
                        sp.sem_inc(dma_begun.sem, 1)
                        sp.dma_start(stageC[p % 2][:], k.d_ctx[bass.ds(b, 1), :, PC * p:PC * (p + 1), :]
                                     .rearrange("a p j c -> (a p) j c")).then_inc(stagedC[p % 2].sem, 16)

                    def load_q(hf):
                        wait(sp, scored, b, 4 * hf + 4 - NS)
                        sp.sem_inc(dma_begun.sem, 1)
                        wait(sp, biased, b, 4 * hf + 4 - NS)
                        sp.sem_inc(dma_begun.sem, 1)
                        hs = slice(hf * HH, (hf + 1) * HH)
                        for dst, src in ((q_hi, k.d_qhi), (q_lo, k.d_qlo)):
                            sp.dma_start(dst[:, hs, :].bitcast(F32), src[bass.ds(b, 1), :, hs, :]
                                         .rearrange("a p h s -> (a p) h s")).then_inc(q_loaded[hf].sem, 16)
                        sp.dma_start(qb[:, 4 * hf:4 * hf + 4], k.d_qb[bass.ds(b, 1), :, 4 * hf:4 * hf + 4]
                                     .rearrange("a q g -> (a q) g")).then_inc(q_loaded[hf].sem, 16)

                    def store(hf):
                        wait(sp, cq_done, b, 4 * hf + 4 - NS)
                        sp.sem_inc(dma_begun.sem, 1)
                        hs = slice(hf * HH, (hf + 1) * HH)
                        sp.dma_start(k.d_xout[bass.ds(b - 1, 1), :, hs, :].rearrange("a p h s -> (a p) h s"),
                                     cq[:, hs, :]).then_inc(cq_stored[hf].sem, 16)

                    loading, storing = keys_in(b), not isinstance(b, int) or b > 0
                    if loading:
                        for d in range(3):
                            load_T(d)
                        load_q(0)
                        for p in range(2):
                            load_C(p)
                        for d in range(3, ND):
                            load_T(d)
                    if storing:
                        store(0)
                    if loading:
                        load_q(1)
                        for p in range(2, NPC):
                            load_C(p)
                    if storing:
                        store(1)

                run(sp, body)
                for hf in range(2):
                    sp.wait_ge(cq_stored[hf].sem, 16 * B)

            @block.scalar
            def _(act):
                act.wait_ge(w_ready.sem, 1)
                act.activation(wk_hi[:], k.c_wraw[:], ACT.Copy).then_inc(w_hi_done.sem, 1)

                def body(b):
                    def split_T(d):
                        wait(act, stagedT[d % 3], b, 16 * (d // 3 + 1))
                        wait(act, projected, b, d + 1 - ND)
                        act.activation(cT_hi[:, :, d * DT:(d + 1) * DT], stageT[d % 3][:], ACT.Copy).then_inc(cT_hi_done.sem, 1)

                    def split_C(p):
                        wait(act, stagedC[p % 2], b, 16 * (p // 2 + 1))
                        wait(act, mixed, b, (PC * p + PC - 1) // 4 + 1 - 3)
                        act.activation(c_hi[:, PC * p:PC * (p + 1), :], stageC[p % 2][:], ACT.Copy).then_inc(c_hi_done.sem, 1)

                    def square(t):
                        wait(act, projected, b, t + 1)
                        wait(act, vared, b, t - 1)
                        act.activation(sq[t % 2][:], p_keys[t % 2][0:TT_C], ACT.Square).then_inc(squared.sem, 1)

                    def key_hi(t):
                        if not there(b, t // 3):
                            return
                        wait(act, k_turned, b, t + 1)
                        if t % ND == 0:
                            wait(act, scored, b, 2 * (t // ND) - 2)
                        q, d = t // ND, t % ND
                        act.activation(kT_hi[:, q % 2, :, d * DT:(d + 1) * DT], kturned, ACT.Copy).then_inc(kT_hi_done.sem, 1)

                    def exp(m):
                        if not there(b, m):
                            return
                        wait(act, biased, b, m + 1)
                        wait(act, p_turned, b, 3 * (m - 1))
                        act.activation(P[m % 2][:].rearrange("p (a t) -> p a t", a=3), scores, ACT.Exp, scale=SCALE,
                                       bias=ebias[:, m % 2:m % 2 + 1], accum_out=esum[:, m % 4:m % 4 + 1]).then_inc(exped.sem, 1)

                    def weights_hi(m, r):
                        if not there(b, m):
                            return
                        wait(act, p_turned, b, 3 * m + r + 1)
                        if r == 0:
                            wait(act, mixed, b, 3 * (m - 1))
                        act.activation(PT_hi[m % 2][:, 4 * r:4 * r + 4, :], pturned, ACT.Copy).then_inc(PT_hi_done.sem, 1)

                    def mixture(m):
                        if not there(b, m):
                            return
                        wait(act, rsum_done, b, m + 1)
                        wait(act, U_turned, b, m)
                        wait(act, mixed, b, 3 * m + 3)
                        act.mul(U[:], p_mix[0:QN, 0:C], rsum[:, m % 4:m % 4 + 1]).then_inc(U_done.sem, 1)

                    def mixture_turned(m):
                        if not there(b, m):
                            return
                        wait(act, U_turned, b, m + 1)
                        wait(act, out_done, b, m)
                        act.activation(UT[:].rearrange("p k q -> p (k q)"), ut_at, ACT.Copy).then_inc(UT_done.sem, 1)

                    for s in steps(b):
                        new = keys_in(b)
                        if new and s == 0:
                            for d in range(3):
                                split_T(d)
                        if new and s == 1:
                            for d in range(4, ND):
                                split_T(d)
                        mixture_turned(s - L_OUT)
                        weights_hi(s - L_TURN, 0)
                        key_hi(3 * s - 2)
                        if new:
                            square(3 * s)
                        exp(s - L_SCORE)
                        weights_hi(s - L_TURN, 1)
                        key_hi(3 * s - 1)
                        if new:
                            square(3 * s + 1)
                        if new and s == 0:
                            split_T(3)
                        if new and s == 4:
                            split_C(0)
                        weights_hi(s - L_TURN, 2)
                        key_hi(3 * s)
                        if new:
                            square(3 * s + 2)
                        mixture(s - L_MIX)
                        if new and s == 4:
                            for p in range(1, NPC):
                                split_C(p)

                run(act, body)

            @block.gpsimd
            def _(pool):
                pool.memset(mhalf[:], -0.5).then_inc(half_set.sem, 1)
                pool.wait_ge(half_set.sem, 1)
                pool.wait_ge(w_hi_done.sem, 1)
                pool.tensor_tensor(wk_lo[:], k.c_wraw[:], wk_hi[:].bitcast(F32), ALU.subtract).then_inc(w_lo_done.sem, 1)

                def body(b):
                    if not keys_in(b):
                        return

                    def split_T(d):
                        wait(pool, cT_hi_done, b, d + 1)
                        at = slice(d * DT, (d + 1) * DT)
                        pool.tensor_tensor(cT_lo[:, :, at], stageT[d % 3][:], cT_hi[:, :, at].bitcast(F32),
                                           ALU.subtract).then_inc(cT_lo_done.sem, 1)

                    def split_C(p):
                        wait(pool, c_hi_done, b, p + 1)
                        at = slice(PC * p, PC * (p + 1))
                        pool.tensor_tensor(c_lo[:, at, :], stageC[p % 2][:], c_hi[:, at, :].bitcast(F32),
                                           ALU.subtract).then_inc(c_lo_done.sem, 1)

                    def power(t):
                        wait(pool, vared, b, t + 1)
                        pool.tensor_tensor(rs[:, t % 4, :], ss[:, t % 4, :], mhalf[0:TT_C], ALU.pow).then_inc(powed.sem, 1)

                    for s in range(NS):
                        if s == 0:
                            for d in range(3):
                                split_T(d)
                        if s == 1:
                            for d in range(4, ND):
                                split_T(d)
                        power(3 * s)
                        power(3 * s + 1)
                        if s == 0:
                            split_T(3)
                        if s == 4:
                            split_C(0)
                        power(3 * s + 2)
                        if s == 4:
                            for p in range(1, NPC):
                                split_C(p)

                run(pool, body)

            @block.vector
            def _(dve):
                prep = Chain(dve, prep_step)
                dve.wait_ge(w_loaded.sem, 48)
                heads = k.c_wraw[:].rearrange("p k (h e) -> p (k h) e", h=G)
                prep(dve.tensor_reduce(w_mean[:], heads, AX_X, ALU.add))
                prep(dve.tensor_scalar(w_mean[:], w_mean[:], 1.0 / D, None, ALU.mult))
                dve.tensor_tensor(heads, heads, w_mean[:].unsqueeze(2).to_broadcast([128, KC * G, D]),
                                  ALU.subtract).then_inc(w_ready.sem, 1)

                def body(b):
                    def key_sums(t):
                        wait(dve, squared, b, t + 1)
                        dve.tensor_reduce(ss[:, t % 4, :], sq[t % 2][:], AX_X, ALU.add).then_inc(r_step.sem, 1)
                        wait(dve, r_step, b, t + 1)
                        dve.tensor_scalar(ss[:, t % 4, :], ss[:, t % 4, :], 1.0 / D, EPS, ALU.mult, ALU.add).then_inc(vared.sem, 1)

                    def key_norm(t):
                        if not there(b, t // 3):
                            return
                        wait(dve, powed, b, t + 1)
                        wait(dve, k_turned, b, t - 1)
                        dve.tensor_tensor(kn[t % 2][:], p_keys[t % 2][0:TT_C],
                                          rs[:, t % 4, :].unsqueeze(2).to_broadcast([TT_C, 4, D]),
                                          ALU.mult).then_inc(kn_done.sem, 1)

                    def key_lo(t):
                        if not there(b, t // 3):
                            return
                        wait(dve, kT_hi_done, b, t + 1)
                        q, at = t // ND, slice((t % ND) * DT, (t % ND + 1) * DT)
                        dve.tensor_tensor(kT_lo[:, q % 2, :, at], kturned, kT_hi[:, q % 2, :, at].bitcast(F32),
                                          ALU.subtract).then_inc(kT_lo_done.sem, 1)

                    def softmax_bias(m):
                        if not there(b, m):
                            return
                        one, g = slice(m % 2, m % 2 + 1), m % NS
                        wait(dve, scored, b, m + 1)
                        if m % 4 == 0:
                            wait(dve, q_loaded[g // 4], b, 48 if m >= 0 else 0)
                        dve.tensor_reduce(mx[:, one], scores, mybir.AxisListType.XY, ALU.max).then_inc(b_step.sem, 1)
                        wait(dve, b_step, b, 2 * m + 1)
                        dve.tensor_scalar(mx[:, one], mx[:, one], qb[:, g:g + 1], None, ALU.add).then_inc(b_step.sem, 1)
                        wait(dve, b_step, b, 2 * m + 2)
                        wait(dve, exped, b, m - 1)
                        dve.tensor_scalar(ebias[:, one], qb[:, g:g + 1], mx[:, one], SCALE, ALU.subtract,
                                          ALU.mult).then_inc(biased.sem, 1)

                    def weight_sum(m):
                        if not there(b, m):
                            return
                        wait(dve, exped, b, m + 1)
                        one = slice(m % 4, m % 4 + 1)
                        dve.reciprocal(rsum[:, one], esum[:, one]).then_inc(rsum_done.sem, 1)

                    def weights_lo(m, r):
                        if not there(b, m):
                            return
                        wait(dve, PT_hi_done, b, 3 * m + r + 1)
                        at = slice(4 * r, 4 * r + 4)
                        dve.tensor_tensor(PT_lo[m % 2][:, at, :], pturned, PT_hi[m % 2][:, at, :].bitcast(F32),
                                          ALU.subtract).then_inc(PT_lo_done.sem, 1)

                    def smoothed_output(m):
                        if not there(b, m):
                            return
                        n = HPG * (m % NS)
                        wait(dve, out_done, b, m + 1)
                        if m % 4 == 0:
                            wait(dve, cq_stored[m % NS // 4], b, 16 * (m // NS))
                        smooth = k.rsm[:, NH + n:NH + n + HPG].unsqueeze(2).to_broadcast([128, HPG, S])
                        dve.tensor_tensor(y[:], out_at.rearrange("p (a s) -> p a s", a=HPG), smooth,
                                          ALU.mult).then_inc(out_read.sem, 1)

                    def quantised_output(m):
                        if not there(b, m):
                            return
                        n = HPG * (m % NS)
                        wait(dve, out_read, b, m + 1)
                        made = [4 * m]

                        def link(ins):
                            made[0] += 1
                            ins.then_inc(q_step.sem, 1)
                            wait(dve, q_step, b, made[0])

                        quantise(dve, link, cq[:, n:n + HPG, :], y[:], work[:], m_[:]).then_inc(cq_done.sem, 1)

                    for s in steps(b):
                        new = keys_in(b)
                        weight_sum(s - L_TURN)
                        key_norm(3 * s - 1)
                        weights_lo(s - L_TURN, 0)
                        key_lo(3 * s - 2)
                        softmax_bias(s - L_SCORE)
                        if new:
                            key_sums(3 * s)
                        smoothed_output(s - L_OUT)
                        weights_lo(s - L_TURN, 1)
                        key_lo(3 * s - 1)
                        key_norm(3 * s)
                        if new:
                            key_sums(3 * s + 1)
                        quantised_output(s - L_OUT)
                        weights_lo(s - L_TURN, 2)
                        key_lo(3 * s)
                        key_norm(3 * s + 1)
                        if new:
                            key_sums(3 * s + 2)

                run(dve, body)

            @block.tensor
            def _(pe):
                pe.wait_ge(w_lo_done.sem, 1)
                pe.wait_ge(w_loaded.sem, 48)

                def body(b):
                    def keys(t):
                        q, d = t // ND, t % ND
                        if q == 0:
                            wait(pe, cT_lo_done, b, d + 1)
                        wait(pe, kn_done, b, t - 1)
                        terms = [(x, w, kc) for kc in range(KC)
                                 for x, w in ((cT_hi, wk_hi), (cT_hi, wk_lo), (cT_lo, wk_hi))]
                        for a in range(2):
                            at = d * DT + a * TT_C
                            for n, (x, w, kc) in enumerate(terms):
                                ins = pe.matmul(p_keys[t % 2][0:TT_C, 2 * a:2 * a + 2, :].rearrange("p g e -> p (g e)"),
                                                x[:, kc, at:at + TT_C], w[:, kc, 2 * q * D:2 * (q + 1) * D],
                                                start=n == 0, stop=n == len(terms) - 1)
                        ins.then_inc(projected.sem, 1)

                    def turn_keys(t):
                        if not there(b, t // 3):
                            return
                        wait(pe, kn_done, b, t + 1)
                        wait(pe, kT_lo_done, b, t)
                        for a in range(2):
                            for g in range(2):
                                ins = pe.transpose(kturned[:, g, a * TT_C:(a + 1) * TT_C], kn[t % 2][:, 2 * a + g, :],
                                                   k.ident[0:TT_C, 0:TT_C])
                        ins.then_inc(k_turned.sem, 1)

                    def score(m):
                        if not there(b, m):
                            return
                        g, par = m % NS, (m // 2) % 2
                        if m >= 0 and m % 4 == 0:
                            wait(pe, q_loaded[g // 4], b, 48)
                        wait(pe, kT_lo_done, b, ND * (m // 2) + ND)
                        wait(pe, exped, b, m)
                        for t in range(3):
                            for n, (x, w) in enumerate(((q_hi, kT_hi), (q_hi, kT_lo), (q_lo, kT_hi))):
                                ins = pe.matmul(scores[:, t, :], x[:, HPG * g:HPG * (g + 1), :].rearrange("p a s -> p (a s)"),
                                                w[:, par, m % 2, t * (SC // 3):(t + 1) * (SC // 3)], start=n == 0, stop=n == 2)
                        ins.then_inc(scored.sem, 1)

                    def turn_weights(m, r):
                        if not there(b, m):
                            return
                        wait(pe, exped, b, m + 1)
                        wait(pe, PT_lo_done, b, 3 * m + r)
                        for a in range(4):
                            j = 4 * r + a
                            ins = pe.transpose(pturned[:, a, :], P[m % 2][:, j * TT_C:(j + 1) * TT_C], k.ident[0:QN, 0:QN])
                        ins.then_inc(p_turned.sem, 1)

                    def mix(m, r):
                        if not there(b, m):
                            return
                        wait(pe, PT_lo_done, b, 3 * m + r + 1)
                        if r == 0:
                            wait(pe, out_read, b, m)
                        if m == 0:
                            wait(pe, c_lo_done, b, r + 2)
                        for a in range(4):
                            j = 4 * r + a
                            for n, (x, w) in enumerate(((PT_hi, c_hi), (PT_hi, c_lo), (PT_lo, c_hi))):
                                ins = pe.matmul(p_mix[0:QN, 0:C], x[m % 2][:, j, :], w[:, j, :],
                                                start=j == 0 and n == 0, stop=j == NT_C - 1 and n == 2)
                        ins.then_inc(mixed.sem, 1)

                    def turn_mixture(m):
                        if not there(b, m):
                            return
                        wait(pe, U_done, b, m + 1)
                        for kc in range(KC):
                            ins = pe.transpose(ut_at[:, kc * QN:(kc + 1) * QN], U[:, kc * 128:(kc + 1) * 128], k.ident[0:QN, 0:QN])
                        ins.then_inc(U_turned.sem, 1)

                    def project_out(m):
                        if not there(b, m):
                            return
                        g = m % NS
                        wait(pe, UT_done, b, m + 1)
                        for kc in range(KC):
                            ins = pe.matmul(out_at, wv[:, kc, g * D:(g + 1) * D], UT[:, kc, :], start=kc == 0, stop=kc == KC - 1)
                        ins.then_inc(out_done.sem, 1)

                    for s in steps(b):
                        new = keys_in(b)
                        score(s - L_SCORE)
                        turn_mixture(s - L_OUT)
                        turn_weights(s - L_TURN, 0)
                        turn_keys(3 * s - 2)
                        if new:
                            keys(3 * s)
                        project_out(s - L_OUT)
                        turn_weights(s - L_TURN, 1)
                        turn_keys(3 * s - 1)
                        if new:
                            keys(3 * s + 1)
                        mix(s - L_MIX, 0)
                        mix(s - L_MIX, 1)
                        turn_weights(s - L_TURN, 2)
                        turn_keys(3 * s)
                        if new:
                            keys(3 * s + 2)
                        mix(s - L_MIX, 2)

                run(pe, body)


def project_phase(nc, k):
    NT = 2 * NH
    with Phase(nc) as ctx:
        ctx.callback(ctx.clear)
        def sb(name, shape, dt=F32):
            return ctx.enter_context(nc.sbuf_tensor(f"d_{name}", shape, dt))

        def sig(name, per=1, primed=0):
            return Signal(nc, ctx, f"d_{name}", per, primed)

        w_raw = sb("w_raw", [128, 2, 4, C])
        w_hi = sb("w_hi", [128, NT, C], F32R)
        w_lo = sb("w_lo", [128, NT, C], F32R)
        cat = [sb(f"cat{j}", [128, NT, T2], BF16) for j in range(2)]
        catr = [sb(f"catr{j}", [128, NT, T2], F32R) for j in range(2)]
        osc = sb("osc", [128, 1])
        po = [ctx.enter_context(nc.psum_tensor(f"d_po{j}", [T2, C], F32)) for j in range(2)]
        w_loaded, w_hi_done, w_lo_done = [sig("w_loaded0"), sig("w_loaded1")], sig("w_hi_done"), sig("w_lo_done")
        cat_loaded = [sig(f"cat_loaded{j}", 48) for j in range(2)]
        cast = sig("cast", 2, 1)
        summed = sig("summed", 2, 1)
        added = sig("added", 2, 1)
        osc_done = sig("osc_done")
        with nc.Block() as block:
            @block.sync
            def _(sp):
                for c in range(NT // 4):
                    if c >= 2:
                        sp.wait_ge(w_lo_done.sem, c - 1)
                    sp.dma_start(w_raw[:, c % 2], k.d_proj_w[:, 4 * c:4 * c + 4, :]).then_inc(w_loaded[c % 2].sem, 16)
                with sp.Fori(0, PAIRS // 2) as i:
                    for j in range(2):
                        sp.wait_ge(cast.sem, cast.at(i, 0))
                        sp.dma_start(cat[j][:, 0:NH, :], k.d_core[bass.ds(2 * i + j, 1)].rearrange("a p h s -> (a p) h s")
                                     ).then_inc(cat_loaded[j].sem, 16)
                        for b2 in range(2):
                            sp.dma_start(cat[j][:, NH:NT, b2 * S:(b2 + 1) * S],
                                         k.d_xout[bass.ds(4 * i + 2 * j + b2, 1)].rearrange("a p h s -> (a p) h s")
                                         ).then_inc(cat_loaded[j].sem, 16)

            @block.scalar
            def _(act):
                for c in range(NT // 4):
                    act.wait_ge(w_loaded[c % 2].sem, 16 * (c // 2 + 1))
                    act.activation(w_hi[:, 4 * c:4 * c + 4, :], w_raw[:, c % 2], ACT.Copy).then_inc(w_hi_done.sem, 1)
                act.sem_inc(cast.sem, 1)
                with act.Fori(0, PAIRS // 2) as i:
                    for j in range(2):
                        act.wait_ge(cat_loaded[j].sem, cat_loaded[j].at(i, 48))
                        act.wait_ge(summed.sem, summed.at(i, 0))
                        act.activation(catr[j][:], cat[j][:], ACT.Copy).then_inc(cast.sem, 1)

            @block.gpsimd
            def _(pool):
                for c in range(NT // 4):
                    pool.wait_ge(w_hi_done.sem, c + 1)
                    pool.tensor_tensor(w_lo[:, 4 * c:4 * c + 4, :], w_raw[:, c % 2],
                                       w_hi[:, 4 * c:4 * c + 4, :].bitcast(F32), ALU.subtract).then_inc(w_lo_done.sem, 1)

            @block.vector
            def _(dve):
                dve.tensor_tensor(osc[:], k.vec[:, V_SPI:V_SPI + 1], k.vec[:, V_SPW:V_SPW + 1], ALU.mult).then_inc(osc_done.sem, 1)
                dve.wait_ge(osc_done.sem, 1)
                dve.sem_inc(added.sem, 1)
                with dve.Fori(0, PAIRS // 2) as i:
                    for j in range(2):
                        dve.wait_ge(summed.sem, summed.at(i, j + 1))
                        xp = k.x[:, bass.ds(2 * i + j, 1), :].rearrange("p a c -> p (a c)")
                        dve.scalar_tensor_tensor(xp, po[j][:], osc[0:T2, 0:1], xp, ALU.mult, ALU.add).then_inc(added.sem, 1)

            @block.tensor
            def _(pe):
                pe.sem_inc(summed.sem, 1)
                pe.wait_ge(w_lo_done.sem, NT // 4)
                with pe.Fori(0, PAIRS // 2) as i:
                    for j in range(2):
                        pe.wait_ge(cast.sem, cast.at(i, j + 1))
                        pe.wait_ge(added.sem, added.at(i, 0))
                        for t in range(NT):
                            for w in (w_hi, w_lo):
                                ins = pe.matmul(po[j][:], catr[j][:, t, :], w[:, t, :], start=t == 0 and w is w_hi,
                                                stop=t == NT - 1 and w is w_lo)
                        ins.then_inc(summed.sem, 1)


def gate_phase(nc, k):
    with Phase(nc) as ctx:
        ctx.callback(ctx.clear)
        def sb(name, shape, dt=F32):
            return ctx.enter_context(nc.sbuf_tensor(f"g_{name}", shape, dt))

        def sig(name, per=1, primed=0):
            return Signal(nc, ctx, f"g_{name}", per, primed)

        gw = sb("gw", [128, KC, E])
        b2 = sb("b2", [E, C])
        rank = sb("rank", [T2, E])
        lg = sb("lg", [T2, PAIRS, E])
        left = sb("left", [T2, PAIRS, E])
        eq = sb("eq", [T2, PAIRS, E])
        pick = sb("pick", [T2, PAIRS, E])
        best = sb("best", [T2, PAIRS])
        top = sb("top", [T2, PAIRS])
        tie = sb("tie", [T2, PAIRS])
        GT = sb("GT", [E, PAIRS, T2])
        pl = ctx.enter_context(nc.psum_tensor("g_pl", [T2, PAIRS, E], F32))
        pg = ctx.enter_context(nc.psum_tensor("g_pg", [128, 2, 512], F32))
        pb = ctx.enter_context(nc.psum_tensor("g_pb", [T2, 4, 2, C], F32))
        loaded, logits, ranked, exped_in, exped, gated, g_turned, g_copied, biased = (
            sig("loaded"), sig("logits"), sig("ranked"), sig("exped_in"), sig("exped"), sig("gated"),
            sig("g_turned"), sig("g_copied"), sig("biased"))
        dve_step = sig("dve_step")
        bc = [T2, PAIRS, E]
        with nc.Block() as block:
            @block.sync
            def _(sp):
                sp.dma_start(gw[:], k.d_gate_w).then_inc(loaded.sem, 16)
                sp.dma_start(b2[:], k.d_b2).then_inc(loaded.sem, 16)

            @block.gpsimd
            def _(pool):
                pool.iota(rank[:], [[-1, E]], base=E, channel_multiplier=0,
                          allow_small_or_imprecise_dtypes=True).then_inc(ranked.sem, 1)

            @block.tensor
            def _(pe):
                pe.wait_ge(loaded.sem, 32)
                for p in range(PAIRS):
                    for kc in range(KC):
                        ins = pe.matmul(pl[:, p, :], k.xT[:, kc, p * T2:(p + 1) * T2], gw[:, kc, :], start=kc == 0, stop=kc == KC - 1)
                ins.then_inc(logits.sem, 1)
                pe.wait_ge(gated.sem, 1)
                for p in range(PAIRS):
                    ins = pe.transpose(pg[0:E, p // 4, (p % 4) * T2:(p % 4 + 1) * T2], k.gates[:, p, :], k.ident[0:T2, 0:T2])
                ins.then_inc(g_turned.sem, 1)
                pe.wait_ge(g_copied.sem, 1)
                for p in range(PAIRS):
                    ins = pe.matmul(pb[:, p // 2, p % 2, :], GT[:, p, :], b2[:], start=True, stop=True)
                ins.then_inc(biased.sem, 1)

            @block.scalar
            def _(act):
                act.wait_ge(exped_in.sem, 1)
                act.activation(lg[:], lg[:], ACT.Exp).then_inc(exped.sem, 1)

            @block.vector
            def _(dve):
                link = Chain(dve, dve_step)
                dve.wait_ge(logits.sem, 1)
                gb = k.rows[0:T2, R_GB:R_GB + E].unsqueeze(1).to_broadcast(bc)
                link(dve.tensor_tensor(lg[:], pl[:], gb, ALU.add))
                link(dve.tensor_copy(left[:], lg[:]))
                dve.wait_ge(ranked.sem, 1)
                for r in range(TOPK):
                    link(dve.tensor_reduce(best[:], left[:], AX_X, ALU.max))
                    if r == 0:
                        link(dve.tensor_copy(top[:], best[:]))
                    link(dve.tensor_tensor(eq[:], left[:], best[:].unsqueeze(2).to_broadcast(bc), ALU.is_ge))
                    link(dve.tensor_tensor(eq[:], eq[:], rank[:].unsqueeze(1).to_broadcast(bc), ALU.mult))
                    link(dve.tensor_reduce(tie[:], eq[:], AX_X, ALU.max))
                    link(dve.tensor_tensor(eq[:], eq[:], tie[:].unsqueeze(2).to_broadcast(bc), ALU.is_equal))
                    if r == 0:
                        link(dve.tensor_copy(pick[:], eq[:]))
                    else:
                        link(dve.tensor_tensor(pick[:], pick[:], eq[:], ALU.add))
                    link(dve.scalar_tensor_tensor(left[:], eq[:], NEG, left[:], ALU.mult, ALU.add))
                link(dve.tensor_tensor(lg[:], lg[:], top[:].unsqueeze(2).to_broadcast(bc), ALU.subtract))
                dve.sem_inc(exped_in.sem, 1)
                dve.wait_ge(exped.sem, 1)
                link(dve.tensor_tensor(lg[:], lg[:], pick[:], ALU.mult))
                link(dve.tensor_reduce(best[:], lg[:], AX_X, ALU.add))
                link(dve.reciprocal(best[:], best[:]))
                dve.tensor_tensor(k.gates[:], lg[:], best[:].unsqueeze(2).to_broadcast(bc), ALU.mult).then_inc(gated.sem, 1)
                link(dve.tensor_tensor(k.x[:], k.x[:], k.xh[:], ALU.add))
                dve.wait_ge(g_turned.sem, 1)
                link(dve.tensor_copy(GT[:].rearrange("e (a p) t -> e a (p t)", a=2), pg[0:E, :, 0:4 * T2]))
                dve.sem_inc(g_copied.sem, 1)
                dve.wait_ge(biased.sem, 1)
                link(dve.tensor_tensor(k.x[:], pb[:].rearrange("t a b c -> t (a b) c"), k.x[:], ALU.add))


def expert_phase(nc, k):
    TH = 4 * T2
    NI = I // 128
    with Phase(nc) as ctx:
        ctx.callback(ctx.clear)
        def sb(name, shape, dt=F32):
            return ctx.enter_context(nc.sbuf_tensor(f"e_{name}", shape, dt))

        def sig(name, per=1, primed=0):
            return Signal(nc, ctx, f"e_{name}", per, primed)

        x_hi = sb("x_hi", [128, KC, N], F32R)
        x_lo = sb("x_lo", [128, KC, N], F32R)
        w1 = [sb(f"w1_{j}", [128, KC, 2 * I]) for j in range(2)]
        w2 = [sb(f"w2_{j}", [128, NI, C]) for j in range(2)]
        b1 = [sb(f"b1_{j}", [128, 2 * NI]) for j in range(2)]
        w1_hi = [sb(f"w1_hi{j}", [128, KC, 2 * I], F32R) for j in range(2)]
        w1_lo = [sb(f"w1_lo{j}", [128, KC, 2 * I], F32R) for j in range(2)]
        w2_hi = [sb(f"w2_hi{j}", [128, NI, C], F32R) for j in range(2)]
        w2_lo = [sb(f"w2_lo{j}", [128, NI, C], F32R) for j in range(2)]
        a = [sb(f"a{j}", [128, TH]) for j in range(2)]
        sg = [sb(f"sg{j}", [128, TH]) for j in range(2)]
        bb = [sb(f"bb{j}", [128, TH]) for j in range(2)]
        act_f = [sb(f"act_f{j}", [128, TH]) for j in range(2)]
        act_hi = [sb(f"act_hi{j}", [128, NI, TH], F32R) for j in range(2)]
        act_lo = [sb(f"act_lo{j}", [128, NI, TH], F32R) for j in range(2)]
        ph = [ctx.enter_context(nc.psum_tensor(f"e_ph{j}", [128, 512], F32)) for j in range(6)]
        py = [ctx.enter_context(nc.psum_tensor(f"e_py{j}", [T2, 2, C], F32)) for j in range(2)]

        x_split, x_done = sig("x_split"), sig("x_done")
        loaded = [sig(f"loaded{j}", 48) for j in range(2)]
        w_hi_done = sig("w_hi_done", 4)
        w_lo_done = sig("w_lo_done", 4, 1)
        hidden = sig("hidden", 4 * 2 * NI, 1)
        hid_read = sig("hid_read", 4 * 2 * NI, 1)
        sigmoided = sig("sigmoided", 4 * NI)
        acted = sig("acted", 4 * NI)
        act_hi_done = sig("act_hi_done", 4 * NI)
        act_lo_done = sig("act_lo_done", 4 * NI, 1)
        dve_step = sig("dve_step", 4 * NI * 3)
        mixed = sig("mixed", 4 * 2, 1)
        added = sig("added", 4 * 2, 1)
        stored = sig("stored")
        UN = 4

        with nc.Block() as block:
            @block.sync
            def _(sp):
                with sp.Fori(0, E // 2) as i:
                    for j in range(2):
                        sp.wait_ge(w_lo_done.sem, w_lo_done.at(i, 0))
                        sp.wait_ge(hid_read.sem, hid_read.at(i, 0))
                        e = 2 * i + j
                        sp.dma_start(w1[j][:], k.d_w1[bass.ds(e, 1)].rearrange("a p k n -> (a p) k n")).then_inc(loaded[j].sem, 16)
                        sp.dma_start(w2[j][:], k.d_w2[bass.ds(e, 1)].rearrange("a p k n -> (a p) k n")).then_inc(loaded[j].sem, 16)
                        sp.dma_start(b1[j][:], k.d_b1[bass.ds(e, 1)].rearrange("a p n -> (a p) n")).then_inc(loaded[j].sem, 16)
                sp.wait_ge(added.sem, 1 + (E // 2) * UN * 2)
                sp.dma_start(k.d_out, k.x[:]).then_inc(stored.sem, 16)
                sp.wait_ge(stored.sem, 16)

            @block.scalar
            def _(act):
                act.activation(x_hi[:], k.xT[:], ACT.Copy).then_inc(x_split.sem, 1)
                with act.Fori(0, E // 2) as i:
                    for j in range(2):
                        act.wait_ge(loaded[j].sem, loaded[j].at(i, 48))
                        act.wait_ge(mixed.sem, mixed.at(i, 0))
                        act.activation(w1_hi[j][:], w1[j][:], ACT.Copy).then_inc(w_hi_done.sem, 1)
                        act.activation(w2_hi[j][:], w2[j][:], ACT.Copy).then_inc(w_hi_done.sem, 1)
                    for u in range(UN):
                        for t in range(NI):
                            n = NI * u + t
                            act.wait_ge(hid_read.sem, hid_read.at(i, 2 * n + 2))
                            act.activation(sg[t][:], a[t][:], ACT.Sigmoid, scale=1.702).then_inc(sigmoided.sem, 1)
                            act.wait_ge(acted.sem, acted.at(i, n + 1))
                            act.wait_ge(mixed.sem, mixed.at(i, max(2 * (u - 1), 0)))
                            act.activation(act_hi[u % 2][:, t, :], act_f[t][:], ACT.Copy).then_inc(act_hi_done.sem, 1)

            @block.gpsimd
            def _(pool):
                pool.wait_ge(x_split.sem, 1)
                pool.tensor_tensor(x_lo[:], k.xT[:], x_hi[:].bitcast(F32), ALU.subtract).then_inc(x_done.sem, 1)
                pool.sem_inc(w_lo_done.sem, 1)
                pool.sem_inc(act_lo_done.sem, 1)
                with pool.Fori(0, E // 2) as i:
                    for j in range(2):
                        for n, (raw, hi, lo) in enumerate(((w1, w1_hi, w1_lo), (w2, w2_hi, w2_lo))):
                            pool.wait_ge(w_hi_done.sem, w_hi_done.at(i, 2 * j + n + 1))
                            pool.tensor_tensor(lo[j][:], raw[j][:], hi[j][:].bitcast(F32), ALU.subtract).then_inc(w_lo_done.sem, 1)
                    for u in range(UN):
                        for t in range(NI):
                            n = NI * u + t
                            pool.wait_ge(act_hi_done.sem, act_hi_done.at(i, n + 1))
                            pool.tensor_tensor(act_lo[u % 2][:, t, :], act_f[t][:], act_hi[u % 2][:, t, :].bitcast(F32),
                                               ALU.subtract).then_inc(act_lo_done.sem, 1)

            @block.vector
            def _(dve):
                dve.sem_inc(hid_read.sem, 1)
                dve.sem_inc(added.sem, 1)
                link = Chain(dve, dve_step)
                with dve.Fori(0, E // 2) as i:
                    link.round(i)

                    def add_up(u):
                        j, th = u // 2, u % 2
                        for q in range(2):
                            dve.wait_ge(mixed.sem, mixed.at(i, 2 * u + q + 1))
                            for p2 in range(2):
                                p = 4 * th + 2 * q + p2
                                ins = dve.scalar_tensor_tensor(k.x[:, p, :], py[q][:, p2, :],
                                                               k.gates[:, p, bass.ds(2 * i + j, 1)], k.x[:, p, :],
                                                               ALU.mult, ALU.add)
                            ins.then_inc(added.sem, 1)
                            dve.wait_ge(added.sem, added.at(i, 2 * u + q + 1))

                    for u in range(UN):
                        j = u // 2
                        for t in range(NI):
                            n = NI * u + t
                            dve.wait_ge(hidden.sem, hidden.at(i, 2 * n + 1))
                            dve.wait_ge(act_lo_done.sem, act_lo_done.at(i, max(n - 1, 0)))
                            dve.tensor_scalar(a[t][:], k.ph_at(ph, u, 2 * t),
                                              b1[j][:, 2 * t:2 * t + 1], 7.0, ALU.add, ALU.min).then_inc(hid_read.sem, 1)
                            dve.wait_ge(hidden.sem, hidden.at(i, 2 * n + 2))
                            dve.tensor_scalar(bb[t][:], k.ph_at(ph, u, 2 * t + 1), b1[j][:, 2 * t + 1:2 * t + 2], 7.0,
                                              ALU.add, ALU.min).then_inc(hid_read.sem, 1)
                            dve.wait_ge(hid_read.sem, hid_read.at(i, 2 * n + 2))
                            link(dve.tensor_scalar(bb[t][:], bb[t][:], -7.0, 1.0, ALU.max, ALU.add))
                            link(dve.tensor_tensor(bb[t][:], bb[t][:], a[t][:], ALU.mult))
                            dve.wait_ge(sigmoided.sem, sigmoided.at(i, n + 1))
                            link(dve.tensor_tensor(act_f[t][:], bb[t][:], sg[t][:], ALU.mult))
                            dve.sem_inc(acted.sem, 1)
                        if u >= 1:
                            add_up(u - 1)
                    add_up(UN - 1)
                    link.end()

            @block.tensor
            def _(pe):
                pe.sem_inc(hidden.sem, 1)
                pe.sem_inc(mixed.sem, 1)
                pe.wait_ge(x_done.sem, 1)
                with pe.Fori(0, E // 2) as i:
                    def hidden_layer(u):
                        j, th = u // 2, u % 2
                        if th == 0:
                            pe.wait_ge(w_lo_done.sem, w_lo_done.at(i, 2 * j + 2))
                        for t in range(2 * NI):
                            n = 2 * NI * u + t
                            pe.wait_ge(hid_read.sem, hid_read.at(i, max(2 * NI * (u - 1) + t + 1, 0)))
                            at = (t % 2) * I + (t // 2) * 128
                            terms = [(w, x, kc) for kc in range(KC)
                                     for w, x in ((w1_hi, x_hi), (w1_hi, x_lo), (w1_lo, x_hi))]
                            for m, (w, x, kc) in enumerate(terms):
                                ins = pe.matmul(k.ph_at(ph, u, t), w[j][:, kc, at:at + 128], x[:, kc, th * TH:(th + 1) * TH],
                                                start=m == 0, stop=m == len(terms) - 1)
                            ins.then_inc(hidden.sem, 1)

                    def output_layer(u):
                        j = u // 2
                        pe.wait_ge(act_lo_done.sem, act_lo_done.at(i, NI * (u + 1)))
                        for q in range(2):
                            pe.wait_ge(added.sem, added.at(i, max(2 * u + q - 1, 0)))
                            for p2 in range(2):
                                at = slice((2 * q + p2) * T2, (2 * q + p2 + 1) * T2)
                                terms = [(x, w, t) for t in range(NI)
                                         for x, w in ((act_hi, w2_hi), (act_hi, w2_lo), (act_lo, w2_hi))]
                                for m, (x, w, t) in enumerate(terms):
                                    ins = pe.matmul(py[q][:, p2, :], x[u % 2][:, t, at], w[j][:, t, :],
                                                    start=m == 0, stop=m == len(terms) - 1)
                            ins.then_inc(mixed.sem, 1)

                    for u in range(UN):
                        hidden_layer(u)
                        if u >= 1:
                            output_layer(u - 1)
                    output_layer(UN - 1)


class Shared:

    @staticmethod
    def ph_at(ph, u, t):
        return ph[t][:, 0:4 * T2]


def decoder_layer(nc, d, out):
    k = Shared()
    k.d_attn_w, k.d_attn_wo, k.d_xattn_w = d["attn_w"], d["attn_wo"], d["xattn_w"]
    k.d_ctx, k.d_ctxT, k.d_ctx_wk, k.d_ctx_wv = d["ctx"], d["ctxT"], d["ctx_wk"], d["ctx_wv"]
    k.d_proj_w, k.d_gate_w, k.d_b2, k.d_w1, k.d_w2, k.d_b1 = d["proj_w"], d["gate_w"], d["b2"], d["w1"], d["w2"], d["b1"]
    k.d_out = out.rearrange("(p b) s c -> (b s) p c", b=2)
    k.d_qhi = nc.dram_tensor("context_queries_hi", [B, 128, NH, S], F32, kind="Internal").ap()
    k.d_qlo = nc.dram_tensor("context_queries_lo", [B, 128, NH, S], F32, kind="Internal").ap()
    k.d_qb = nc.dram_tensor("context_offsets", [B, HPG * S, G], F32, kind="Internal").ap()
    k.d_core = nc.dram_tensor("core_quantised", [PAIRS, 128, NH, T2], BF16, kind="Internal").ap()
    k.d_xout = nc.dram_tensor("xout_quantised", [B, 128, NH, S], BF16, kind="Internal").ap()
    with ExitStack() as ctx:
        def sb(name, shape, dt=F32):
            return ctx.enter_context(nc.sbuf_tensor(name, shape, dt))

        k.x = sb("x", [T2, PAIRS, C])
        k.ident = sb("ident", [128, 128])
        k.vec = sb("vec", [128, NV])
        k.rsm = sb("rsm", [128, 2 * NH])
        with ExitStack() as first:
            k.rows = first.enter_context(nc.sbuf_tensor("rows", [128, NR], F32))
            k.cos = first.enter_context(nc.sbuf_tensor("cos", [T2, D], F32))
            k.sin = first.enter_context(nc.sbuf_tensor("sin", [T2, D], F32))
            k.cmask = first.enter_context(nc.sbuf_tensor("cmask", [T2, T2], F32))
            k.xT = first.enter_context(nc.sbuf_tensor("xT_a", [128, KC, N], F32))
            loaded = first.enter_context(nc.semaphore("loaded"))
            smoothed = first.enter_context(nc.semaphore("smoothed"))
            id_zero = first.enter_context(nc.semaphore("id_zero"))
            with nc.Block() as block:
                @block.sync
                def _(sp):
                    sp.dma_start(k.x[:], d["x"].rearrange("(p b) s c -> (b s) p c", b=2)).then_inc(loaded, 16)
                    sp.dma_start(k.vec[:], d["vec"]).then_inc(loaded, 16)
                    sp.dma_start(k.rows[:], d["rows"].to_broadcast([128, NR])).then_inc(loaded, 16)
                    sp.dma_start(k.cos[:], d["cos"]).then_inc(loaded, 16)
                    sp.dma_start(k.sin[:], d["sin"]).then_inc(loaded, 16)
                    sp.dma_start(k.cmask[:], d["cmask"]).then_inc(loaded, 16)
                    sp.wait_ge(loaded, 96)

                @block.gpsimd
                def _(pool):
                    pool.memset(k.ident[:], 0.0).then_inc(id_zero, 1)
                    pool.wait_ge(id_zero, 1)
                    pool.affine_select(out=k.ident[:], in_=k.ident[:], compare_op=ALU.not_equal, fill=1.0, base=0,
                                       pattern=[[-1, 128]], channel_multiplier=1).then_inc(id_zero, 1)
                    pool.wait_ge(id_zero, 2)

                @block.vector
                def _(dve):
                    dve.wait_ge(loaded, 96)
                    dve.reciprocal(k.rsm[:], k.vec[:, V_SM:V_SM + 2 * NH]).then_inc(smoothed, 1)
                    dve.wait_ge(smoothed, 1)
            normalise_phase(nc, k, "attn")
            attn_half(nc, k, 0)
            attn_half(nc, k, 1)
        with ExitStack() as second:
            k.xq = second.enter_context(nc.sbuf_tensor("xq", [128, 4, KC, N], BF16))
            k.bmask = second.enter_context(nc.sbuf_tensor("bmask", [T2, T2], F32))
            bm = second.enter_context(nc.semaphore("bmask_loaded"))
            with nc.Block() as block:
                @block.sync
                def _(sp):
                    sp.dma_start(k.bmask[:], d["bmask"]).then_inc(bm, 16)
                    sp.wait_ge(bm, 16)
            xn_phase(nc, k)
            xattn_half(nc, k, 0)
            xattn_half(nc, k, 1)
        with ExitStack() as third:
            k.c_wraw = third.enter_context(nc.sbuf_tensor("c_wraw", [128, KC, G * D], F32))
            context_phase(nc, k)
        project_phase(nc, k)
        with ExitStack() as fourth:
            k.xh = fourth.enter_context(nc.sbuf_tensor("xh", [T2, PAIRS, C], F32))
            k.xT = fourth.enter_context(nc.sbuf_tensor("xT_f", [128, KC, N], F32))
            k.rows = fourth.enter_context(nc.sbuf_tensor("rows_f", [128, NR], F32))
            k.gates = fourth.enter_context(nc.sbuf_tensor("gates", [T2, PAIRS, E], F32))
            rl = fourth.enter_context(nc.semaphore("rows_loaded"))
            with nc.Block() as block:
                @block.sync
                def _(sp):
                    sp.dma_start(k.rows[:, R_GB:R_GB + E], d["rows"][:, R_GB:R_GB + E].to_broadcast([128, E])).then_inc(rl, 16)
                    sp.wait_ge(rl, 16)
            normalise_phase(nc, k, "ffn")
            gate_phase(nc, k)
            expert_phase(nc, k)


def xn_phase(nc, k):
    normalise_phase(nc, k, "xattn")


def _per_head(w):
    return w.reshape(w.shape[0], KC, 128, D).transpose(2, 0, 1, 3)


def _chunk(w, h0):
    return w[:, h0:h0 + 4].transpose(0, 2, 1, 3).reshape(128, KC, CH)


def _rope():
    inv = 1.0 / np.float32(10000.0) ** (np.arange(0, D, 2, dtype=np.float32) / np.float32(D))
    f = (np.arange(S, dtype=np.float32)[:, None] * inv[None, :].astype(np.float32)).astype(np.float32)
    cos, sin = np.cos(f).astype(np.float32), np.sin(f).astype(np.float32)
    cos = np.tile(np.repeat(cos, 2, axis=1), (2, 1))
    sin = np.tile(np.concatenate([sin, -sin], axis=1), (2, 1))
    return cos, sin


def _masks():
    b = np.arange(T2) // S
    same = b[:, None] == b[None, :]
    causal = same & (np.arange(T2)[:, None] >= np.arange(T2)[None, :])
    return (causal * np.float32(1.0 / np.float32(np.sqrt(D)))).astype(np.float32), np.where(same, 0.0, NEG).astype(np.float32)


def kernel(**inputs):
    import concourse.bacc as _bacc
    from concourse.bass_utils import run_bass_kernel_spmd as _run

    f = {n: np.asarray(a) for n, a in inputs.items()}
    at = {n[len("L0_attn_"):]: a for n, a in f.items() if n.startswith("L0_attn_")}
    xa = {n[len("L0_xattn_"):]: a for n, a in f.items() if n.startswith("L0_xattn_")}
    ff = {n[len("L0_ffn_"):]: a for n, a in f.items() if n.startswith("L0_ffn_")}

    q, kk, v = (_per_head(at[n]) for n in ("W_Q", "W_K", "W_V"))
    attn_w = np.stack([np.stack([_chunk(w, 8 * h + 4 * c) for w in (q, kk, v) for c in range(2)]) for h in range(2)])

    def heads(w):
        return _per_head(w.reshape(-1, D, C).transpose(0, 2, 1))

    wq, wk, wqx, wv = (heads(xa[n]) for n in ("wq", "wk", "wqx", "wv"))
    xattn_w = np.stack([np.stack([_chunk(wq, 8 * h), _chunk(wq, 8 * h + 4), _chunk(wk, 4 * h),
                                  _chunk(wqx, 8 * h), _chunk(wqx, 8 * h + 4), _chunk(wv, 4 * h)]) for h in range(2)])
    kvx = heads(xa["w_kv_x"]).transpose(0, 2, 1, 3)

    def col(a):
        return a.reshape(-1, 128).T

    def one(a):
        return np.broadcast_to(a.reshape(1, 1), (128, 1))

    vec = np.concatenate(
        [col(xa["ln_w"]), col(xa["ln_b"]), col(xa["q_in_scale"]), col(xa["k_in_scale"]), col(xa["qx_in_scale"]),
         col(xa["v_in_scale"]), col(ff["norm_w"])]
        + [col(xa[n]) for n in ("qln_w", "qln_b", "kln_w", "kln_b", "qxln_w", "qxln_b", "kxln_w", "kxln_b")]
        + [one(xa[n]) for n in ("wq_scale", "wk_scale", "wqx_scale", "wv_scale", "proj_w_scale", "proj_in_scale")]
        + [col(xa["proj_smooth"])], axis=1)
    rows = np.concatenate([at[n][8 * h:8 * h + 8].reshape(-1) for h in range(2) for n in ("b_Q", "b_K", "b_V")]
                          + [at["b_O"], ff["gate_b"]]).reshape(1, -1)
    cos, sin = _rope()
    cmask, bmask = _masks()
    ctx = f["ctx_2048"]
    w1 = ff["w1"].reshape(E, I, 2, C).transpose(0, 3, 2, 1).reshape(E, KC, 128, 2 * I).transpose(0, 2, 1, 3)
    b1 = ff["b1"].reshape(E, I // 128, 128, 2).transpose(0, 2, 1, 3).reshape(E, 128, 2 * (I // 128))
    w2 = ff["w2"].transpose(0, 2, 1).reshape(E, I // 128, 128, C).transpose(0, 2, 1, 3)
    arrays = {
        "x": f["x"], "attn_w": attn_w, "attn_wo": at["W_O"].transpose(1, 0, 2), "xattn_w": xattn_w,
        "ctx": ctx.reshape(B, NT_C, TT_C, C).transpose(0, 2, 1, 3),
        "ctxT": ctx.transpose(0, 2, 1).reshape(B, KC, 128, SC),
        "ctx_wk": kvx[:, :, 0:G].reshape(128, KC, G * D), "ctx_wv": kvx[:, :, G:2 * G].reshape(128, KC, G * D),
        "proj_w": xa["wproj"].T.reshape(2 * NH, 128, C).transpose(1, 0, 2),
        "gate_w": ff["gate_w"].T.reshape(KC, 128, E).transpose(1, 0, 2), "b2": ff["b2"],
        "w1": w1, "w2": w2, "b1": b1, "vec": vec, "rows": rows, "cos": cos, "sin": sin, "cmask": cmask, "bmask": bmask,
    }
    arrays = {n: np.ascontiguousarray(a) for n, a in arrays.items()}
    nc = _bacc.Bacc("TRN2", target_bir_lowering=False, num_devices=1)
    d = {n: nc.dram_tensor(n + "_dram", a.shape, mybir.dt.from_np(a.dtype), kind="ExternalInput").ap()
         for n, a in arrays.items()}
    out = nc.dram_tensor("out_dram", (B, S, C), F32, kind="ExternalOutput").ap()
    decoder_layer(nc, d, out)
    r = _run(nc, [{n + "_dram": a for n, a in arrays.items()}], core_ids=[0])
    return r.results[0]["out_dram"]
```

```python
from contextlib import ExitStack

import numpy as np

import concourse.bass as bass
from concourse import mybir

F32 = mybir.dt.float32
F32R = mybir.dt.float32r
BF16 = mybir.dt.bfloat16
U16 = mybir.dt.uint16
ALU = mybir.AluOpType
ACT = mybir.ActivationFunctionType
AX_X = mybir.AxisListType.X

B, S, C = 16, 56, 256
SC = 1500
NH, G, D = 16, 8, 128
HPG = NH // G
KC = C // 128
PAIRS = B // 2
T2 = 2 * S
N = B * S
HH = 8
CH = 512
TT_C, NT_C = 125, 12
E, I, TOPK = 16, 256, 4
SCALE = float(1.0 / np.sqrt(D))
EPS = 1e-5
FP8_MAX = 448.0
NEG = -1.0e30
BN = 6

V_LNW, V_LNB, V_QS, V_KS, V_QXS, V_VS, V_NW = 0, 2, 4, 6, 8, 10, 12
V_QLW, V_QLB, V_KLW, V_KLB, V_QXLW, V_QXLB, V_KXLW, V_KXLB = 14, 15, 16, 17, 18, 19, 20, 21
V_SQ, V_SK, V_SQX, V_SV, V_SPW, V_SPI = 22, 23, 24, 25, 26, 27
V_SM = 28
NV = V_SM + 2 * NH
R_BQKV, R_BO, R_GB = 0, 2 * 6 * CH, 2 * 6 * CH + C
NR = R_GB + E


class Phase(ExitStack):

    def __init__(self, nc):
        super().__init__()
        self.nc, self.sems = nc, []

    def clear(self):
        self.nc.clear_and_free_semaphores(self.sems)
        self.nc.all_engine_barrier()


class Signal:

    def __init__(self, nc, ctx, name, per=1, primed=0):
        self.sem = nc.alloc_semaphore(name)
        ctx.sems.append(self.sem)
        self.per, self.primed = per, primed

    def at(self, i, k):
        return i * self.per + (k + self.primed)


class Chain:

    def __init__(self, eng, step):
        self.eng, self.step, self.i, self.n = eng, step, 0, 0

    def round(self, i):
        self.i, self.n = i, 0

    def __call__(self, ins):
        self.n += 1
        ins.then_inc(self.step.sem, 1)
        self.eng.wait_ge(self.step.sem, self.step.at(self.i, self.n))

    def end(self):
        assert self.n == self.step.per, (self.step.sem, self.n)


def quantise(dve, link, out, y, work, m):
    link(dve.tensor_scalar(y, y, FP8_MAX, -FP8_MAX, ALU.min, ALU.max))
    link(dve.tensor_scalar(m.bitcast(U16), y.bitcast(U16), 0x7F80, None, ALU.bitwise_and))
    link(dve.tensor_scalar(m, m, 2.0 ** -6, 24.0, ALU.max, ALU.mult))
    link(dve.tensor_tensor(work, y, m, ALU.add))
    return dve.tensor_tensor(out, work, m, ALU.subtract)


def normalise_phase(nc, k, mode):
    with Phase(nc) as ctx:
        ctx.callback(ctx.clear)
        def sb(name, shape, dt=F32):
            return ctx.enter_context(nc.sbuf_tensor(f"{mode}_{name}", shape, dt))

        stats = sb("stats", [T2, PAIRS, BN])
        mv = sb("mv", [T2, PAIRS, 2])
        ve = sb("ve", [T2, PAIRS])
        rstd = sb("rstd", [T2, PAIRS])
        shift = sb("shift", [T2, PAIRS])
        mhalf = sb("mhalf", [T2, PAIRS])
        xn = sb("xn", [T2, PAIRS, C])
        xt = [ctx.enter_context(nc.psum_tensor(f"{mode}_xt{j}", [128, 4, 128], F32)) for j in range(4)]
        twice = mode != "attn"
        ready = Signal(nc, ctx, mode + "_ready")
        dve_step = Signal(nc, ctx, mode + "_dve_step")
        pow_in = Signal(nc, ctx, mode + "_pow_in")
        pow_out = Signal(nc, ctx, mode + "_pow_out")
        normed = Signal(nc, ctx, mode + "_normed")
        turned = Signal(nc, ctx, mode + "_turned")
        copied = Signal(nc, ctx, mode + "_copied")
        if mode == "xattn":
            lnt = sb("lnt", [128, KC, N])
            y = sb("y", [128, KC, N], BF16)
            m = sb("m", [128, KC, N], BF16)
            work = sb("work", [128, KC, N], BF16)
            rin = sb("rin", [128, 8])
        with nc.Block() as block:
            @block.gpsimd
            def _(pool):
                pool.memset(mhalf[:], -0.5).then_inc(ready.sem, 1)
                pool.wait_ge(ready.sem, 1)
                for r in range(2 if twice else 1):
                    pool.wait_ge(pow_in.sem, r + 1)
                    pool.tensor_tensor(rstd[:], ve[:], mhalf[:], ALU.pow).then_inc(pow_out.sem, 1)

            @block.vector
            def _(dve):
                link = Chain(dve, dve_step)

                def norm(r, dst, src, scale_only=False):
                    for p in range(PAIRS):
                        ins = dve.bn_stats(stats[:, p, :], src[:, p, :])
                    link(ins)
                    for p in range(PAIRS):
                        ins = dve.bn_aggr(mv[:, p, :], stats[:, p, :])
                    link(ins)
                    if scale_only:
                        link(dve.tensor_tensor(shift[:], mv[:, :, 0], mv[:, :, 0], ALU.mult))
                        link(dve.tensor_tensor(ve[:], mv[:, :, 1], shift[:], ALU.add))
                        link(dve.tensor_scalar(ve[:], ve[:], EPS, None, ALU.add))
                    else:
                        link(dve.tensor_scalar(ve[:], mv[:, :, 1], EPS, None, ALU.add))
                    dve.sem_inc(pow_in.sem, 1)
                    dve.wait_ge(pow_out.sem, r + 1)
                    if not scale_only:
                        link(dve.scalar_tensor_tensor(shift[:], mv[:, :, 0], -1.0, rstd[:], ALU.mult, ALU.mult))
                    for p in range(PAIRS):
                        if scale_only:
                            ins = dve.tensor_scalar(dst[:, p, :], src[:, p, :], rstd[:, p:p + 1], None, ALU.mult)
                        else:
                            ins = dve.tensor_scalar(dst[:, p, :], src[:, p, :], rstd[:, p:p + 1],
                                                    shift[:, p:p + 1], ALU.mult, ALU.add)
                    link(ins)

                if mode == "attn":
                    norm(0, xn, k.x)
                    dve.sem_inc(normed.sem, 1)
                    for p in range(PAIRS):
                        ins = dve.tensor_tensor(k.x[:, p, :], k.x[:, p, :], k.rows[0:T2, R_BO:R_BO + C], ALU.add)
                    link(ins)
                elif mode == "xattn":
                    norm(0, xn, k.x)
                    norm(1, xn, xn)
                    dve.sem_inc(normed.sem, 1)
                    for n, v in enumerate((V_QS, V_KS, V_QXS, V_VS)):
                        ins = dve.reciprocal(rin[:, 2 * n:2 * n + 2], k.vec[:, v:v + 2])
                    link(ins)
                    dve.wait_ge(copied.sem, 4)
                    for n in range(4):
                        for c in range(KC):
                            ins = dve.tensor_scalar(y[:, c, :], lnt[:, c, :], rin[:, 2 * n + c:2 * n + c + 1],
                                                    None, ALU.mult)
                        link(ins)
                        link(quantise(dve, link, k.xq[:, n], y[:], work[:], m[:]))
                else:
                    norm(0, k.xh, k.x)
                    norm(1, xn, k.xh, scale_only=True)
                    dve.sem_inc(normed.sem, 1)

            @block.tensor
            def _(pe):
                pe.wait_ge(normed.sem, 1)
                for j in range(4):
                    for p in range(4):
                        pair, c = 4 * (j % 2) + p, j // 2
                        ins = pe.transpose(xt[j][:, p, 0:T2], xn[:, pair, c * 128:(c + 1) * 128],
                                           k.ident[0:T2, 0:T2])
                    ins.then_inc(turned.sem, 1)

            @block.scalar
            def _(act):
                for j in range(4):
                    act.wait_ge(turned.sem, j + 1)
                    c, t0 = j // 2, (j % 2) * 4 * T2
                    src = xt[j][:, :, 0:T2]
                    dst = (lnt if mode == "xattn" else k.xT)[:, c, t0:t0 + 4 * T2].rearrange("p (a b) -> p a b", a=4)
                    if mode == "attn":
                        ins = act.activation(dst, src, ACT.Copy)
                    elif mode == "xattn":
                        ins = act.activation(dst, src, ACT.Identity, scale=k.vec[:, V_LNW + c:V_LNW + c + 1],
                                             bias=k.vec[:, V_LNB + c:V_LNB + c + 1])
                    else:
                        ins = act.mul(dst, src, k.vec[:, V_NW + c:V_NW + c + 1])
                    ins.then_inc(copied.sem, 1)


class Steps:

    def __init__(self, rounds, per_round):
        self.rounds, self.per_round = rounds, per_round

    def wait(self, eng, signal_of, i, n):
        if not isinstance(i, int) or signal_of.at(i, n) > 0:
            eng.wait_ge(signal_of.sem, signal_of.at(i, n))

    def there(self, i, m):
        return not isinstance(i, int) or 0 <= self.per_round * i + m < self.per_round * self.rounds

    def run(self, eng, body):
        body(0)
        with eng.Fori(1, self.rounds) as i:
            body(i)
        body(self.rounds)


def attention_phase(nc, k):
    NTC = 4
    NCH = 6
    NST = 2
    with Phase(nc) as ctx:
        ctx.callback(ctx.clear)

        def sb(name, shape, dt=F32):
            return ctx.enter_context(nc.sbuf_tensor(f"a_{name}", shape, dt))

        def bank(name, shape):
            return ctx.enter_context(nc.psum_tensor(f"a_{name}", shape, F32))

        def sig(name, per_unit=1):
            return Signal(nc, ctx, f"a_{name}", 2 * per_unit)

        w_raw = [sb(f"w_raw{j}", [128, KC, CH]) for j in range(NST)]
        w_hi = sb("w_hi", [128, 2 * NCH, KC, CH], F32R)
        w_lo = sb("w_lo", [128, 2 * NCH, KC, CH], F32R)
        wo = sb("wo", [128, NH, C])
        x_hi = sb("x_hi", [128, KC, T2], F32R)
        x_lo = sb("x_lo", [128, KC, T2], F32R)
        biased = [sb(f"biased{j}", [T2, CH]) for j in range(2)]
        crossed = [sb(f"crossed{j}", [T2, CH]) for j in range(2)]
        tok = [sb(f"tok{j}", [T2, CH]) for j in range(2)]
        qkT = sb("qkT", [128, 2 * HH, T2])
        v = sb("v", [T2, HH, D])
        sc = [sb(f"sc{j}", [T2, 4, T2]) for j in range(2)]
        ab = [sb(f"ab{j}", [T2, 4, T2]) for j in range(2)]
        sg = [sb(f"sg{j}", [T2, 4, T2]) for j in range(2)]
        mx = sb("mx", [T2, 2, 4])
        sm = sb("sm", [T2, 2, 4])
        aT = [sb(f"aT{j}", [T2, 4, T2]) for j in range(2)]
        zT = sb("zT", [128, HH, T2])
        pj = [bank(f"pj{j}", [T2, CH]) for j in range(2)]
        tp = [bank(f"tp{j}", [128, 4, T2]) for j in range(2)]
        ps = [bank(f"ps{j}", [T2, 4, T2]) for j in range(2)]
        pz = bank("pz", [128, 4, T2])
        po = bank("po", [T2, C])

        w_loaded = [sig(f"w_loaded{j}") for j in range(NST)]
        wo_loaded, w_hi_done = sig("wo_loaded"), sig("w_hi_done")
        w_lo_done = [sig(f"w_lo_done{j}") for j in range(2)]
        xhi_done, xlo_done = Signal(nc, ctx, "a_xhi_done"), Signal(nc, ctx, "a_xlo_done")
        projected, bias_done = sig("projected", NCH), sig("bias_done", NCH)
        cosined, cross_done, tok_done = sig("cosined", NTC), sig("cross_done", NTC), sig("tok_done", NTC)
        turned, turned_read = sig("turned", NTC), sig("turned_read", NTC)
        scored, masked, maxed = sig("scored", 2), sig("masked", 2), sig("maxed", 2)
        signed, shifted, exped = sig("signed", 2), sig("shifted", 2), sig("exped", 2)
        sum_step, inverted, weighed = sig("sum_step", 6), sig("inverted", 2), sig("weighed", 2)
        w_turned, w_turned_read = sig("w_turned", 2), sig("w_turned_read", 2)
        mixed, mixed_read = sig("mixed", 2), sig("mixed_read", 2)
        summed, summed_read = sig("summed"), Signal(nc, ctx, "a_summed_read", 2, primed=1)
        pipe = Steps(PAIRS, 2)
        wait, there = pipe.wait, pipe.there

        def first(i, m):
            return isinstance(i, int) and i == 0 and m == 0

        with nc.Block() as block:
            @block.sync
            def _(sp):
                for c in range(2 * NCH):
                    if c >= NST:
                        old = c - NST
                        sp.wait_ge(w_lo_done[old // NCH].sem, old % NCH + 1)
                    sp.dma_start(w_raw[c % NST][:], k.d_attn_w[c // NCH, c % NCH]).then_inc(w_loaded[c % NST].sem, 16)
                    if c == 2 * NCH - 1:
                        sp.dma_start(wo[:], k.d_attn_wo).then_inc(wo_loaded.sem, 16)
                sp.wait_ge(wo_loaded.sem, 16)

            def weight_hi(act, c):
                act.wait_ge(w_loaded[c % NST].sem, 16 * (c // NST + 1))
                act.activation(w_hi[:, c], w_raw[c % NST][:], ACT.Copy).then_inc(w_hi_done.sem, 1)

            def weight_lo(eng, c):
                eng.wait_ge(w_hi_done.sem, c + 1)
                eng.tensor_tensor(w_lo[:, c], w_raw[c % NST][:], w_hi[:, c].bitcast(F32),
                                  ALU.subtract).then_inc(w_lo_done[c // NCH].sem, 1)

            @block.scalar
            def _(act):
                for c in range(NCH):
                    weight_hi(act, c)

                def body(i):
                    def absolute(m, s):
                        if not there(i, m):
                            return
                        wait(act, maxed, i, 2 * m + s + 1)
                        act.activation(ab[s][:], sc[s][:], ACT.Abs)
                        act.activation(sg[s][:], sc[s][:], ACT.Sign).then_inc(signed.sem, 1)

                    def exp(m, s):
                        if not there(i, m):
                            return
                        wait(act, shifted, i, 2 * m + s + 1)
                        act.activation(ab[s][:], ab[s][:], ACT.Exp).then_inc(exped.sem, 1)

                    def unturn(m, c):
                        if not there(i, m):
                            return
                        if c == 0:
                            wait(act, scored, i, 2 * m)
                        wait(act, turned, i, NTC * m + c + 1)
                        act.activation(qkT[:, 4 * c:4 * c + 4, :], tp[c // 3][:], ACT.Copy).then_inc(turned_read.sem, 1)
                        if first(i, m):
                            weight_hi(act, NCH + c)

                    def unturn_weights(m, s):
                        if not there(i, m):
                            return
                        wait(act, w_turned, i, 2 * m + s + 1)
                        act.activation(aT[s][:], tp[1][0:T2], ACT.Copy).then_inc(w_turned_read.sem, 1)

                    def head_outputs(m, s):
                        if not there(i, m):
                            return
                        if s == 0:
                            wait(act, summed, i, m)
                        wait(act, mixed, i, 2 * m + s + 1)
                        act.activation(zT[:, 4 * s:4 * s + 4, :], pz[:], ACT.Copy).then_inc(mixed_read.sem, 1)

                    for m in range(2):
                        if m == 0 and there(i, 0):
                            wait(act, projected, i, 0)
                            act.activation(x_hi[:], k.xT[:, :, bass.ds(i * T2, T2)], ACT.Copy).then_inc(xhi_done.sem, 1)
                        absolute(m - 1, 0)
                        unturn(m, 0)
                        absolute(m - 1, 1)
                        exp(m - 1, 0)
                        exp(m - 1, 1)
                        unturn(m, 1)
                        unturn_weights(m - 1, 0)
                        head_outputs(m - 1, 0)
                        unturn_weights(m - 1, 1)
                        unturn(m, 2)
                        unturn(m, 3)
                        head_outputs(m - 1, 1)
                        if first(i, m):
                            for c in range(NTC, NCH):
                                weight_hi(act, NCH + c)

                pipe.run(act, body)

            @block.gpsimd
            def _(pool):
                def body(i):
                    def cross(m, c):
                        if not there(i, m):
                            return
                        wait(pool, bias_done, i, NCH * m + c + 1)
                        wait(pool, tok_done, i, NTC * m + c - 1)
                        src = biased[c % 2][:].rearrange("p (h e two) -> p h e two", h=4, two=2)
                        dst = crossed[c % 2][:].rearrange("p (h e two) -> p h e two", h=4, two=2)
                        sin = k.sin[:, 0:D // 2].unsqueeze(1).to_broadcast([T2, 4, D // 2])
                        nsin = k.sin[:, D // 2:D].unsqueeze(1).to_broadcast([T2, 4, D // 2])
                        pool.tensor_tensor(dst[:, :, :, 0], src[:, :, :, 1], nsin, ALU.mult)
                        pool.tensor_tensor(dst[:, :, :, 1], src[:, :, :, 0], sin, ALU.mult).then_inc(cross_done.sem, 1)
                        if first(i, m):
                            weight_lo(pool, NCH + c)

                    def weigh(m, s):
                        if not there(i, m):
                            return
                        wait(pool, inverted, i, 2 * m + s + 1)
                        pool.tensor_tensor(sc[s][:], sc[s][:], sm[:, s, :].unsqueeze(2).to_broadcast([T2, 4, T2]),
                                           ALU.mult).then_inc(weighed.sem, 1)

                    for m in range(2):
                        if m == 0 and there(i, 0):
                            wait(pool, xhi_done, i, 1)
                            pool.tensor_tensor(x_lo[:], k.xT[:, :, bass.ds(i * T2, T2)], x_hi[:].bitcast(F32),
                                               ALU.subtract).then_inc(xlo_done.sem, 1)
                        cross(m, 0)
                        cross(m, 1)
                        weigh(m - 1, 0)
                        cross(m, 2)
                        weigh(m - 1, 1)
                        cross(m, 3)
                        if first(i, m):
                            for c in range(NTC, NCH):
                                weight_lo(pool, NCH + c)

                pipe.run(pool, body)

            @block.vector
            def _(dve):
                dve.sem_inc(summed_read.sem, 1)
                for c in range(NCH):
                    weight_lo(dve, c)

                def body(i):
                    def add_bias(m, c, out):
                        wait(dve, projected, i, NCH * m + c + 1)
                        at = R_BQKV + (m * NCH + c) * CH
                        dve.tensor_tensor(out, pj[c % 2][:], k.rows[0:T2, at:at + CH], ALU.add).then_inc(bias_done.sem, 1)

                    def rotate(m, c):
                        if not there(i, m):
                            return
                        add_bias(m, c, biased[c % 2][:])
                        wait(dve, bias_done, i, NCH * m + c + 1)
                        wait(dve, turned, i, NTC * m + c - 1)
                        cos = k.cos[:, :].unsqueeze(1).to_broadcast([T2, 4, D])
                        dve.tensor_tensor(tok[c % 2][:].rearrange("p (h e) -> p h e", h=4),
                                          biased[c % 2][:].rearrange("p (h e) -> p h e", h=4), cos,
                                          ALU.mult).then_inc(cosined.sem, 1)

                    def rotated(m, c):
                        if not there(i, m):
                            return
                        wait(dve, cosined, i, NTC * m + c + 1)
                        wait(dve, cross_done, i, NTC * m + c + 1)
                        dve.tensor_tensor(tok[c % 2][:], tok[c % 2][:], crossed[c % 2][:], ALU.add).then_inc(tok_done.sem, 1)

                    def values(m, s):
                        if not there(i, m):
                            return
                        wait(dve, mixed, i, 2 * (m - 1) + s + 1)
                        add_bias(m, NTC + s, v[:, 4 * s:4 * s + 4, :].rearrange("p h e -> p (h e)"))

                    def mask(m, s):
                        if not there(i, m):
                            return
                        wait(dve, scored, i, 2 * m + s + 1)
                        wait(dve, w_turned, i, 2 * (m - 1) + s + 1)
                        dve.tensor_tensor(sc[s][:], ps[s][:], k.cmask[:, :].unsqueeze(1).to_broadcast([T2, 4, T2]),
                                          ALU.mult).then_inc(masked.sem, 1)
                        wait(dve, masked, i, 2 * m + s + 1)
                        dve.tensor_reduce(mx[:, s, :], sc[s][:], AX_X, ALU.max,
                                          apply_absolute_value=True).then_inc(maxed.sem, 1)

                    def shift(m, s):
                        if not there(i, m):
                            return
                        wait(dve, signed, i, 2 * m + s + 1)
                        wait(dve, maxed, i, 2 * m + s + 1)
                        dve.tensor_tensor(ab[s][:], ab[s][:], mx[:, s, :].unsqueeze(2).to_broadcast([T2, 4, T2]),
                                          ALU.subtract).then_inc(shifted.sem, 1)

                    def row_sums(m, s):
                        if not there(i, m):
                            return
                        wait(dve, exped, i, 2 * m + s + 1)
                        n = 6 * m + 3 * s
                        dve.tensor_tensor(sc[s][:], ab[s][:], sg[s][:], ALU.mult).then_inc(sum_step.sem, 1)
                        wait(dve, sum_step, i, n + 1)
                        dve.tensor_reduce(sm[:, s, :], sc[s][:], AX_X, ALU.add,
                                          apply_absolute_value=True).then_inc(sum_step.sem, 1)
                        wait(dve, sum_step, i, n + 2)
                        dve.tensor_scalar(sm[:, s, :], sm[:, s, :], 1e-6, None, ALU.add).then_inc(sum_step.sem, 1)
                        wait(dve, sum_step, i, n + 3)
                        dve.reciprocal(sm[:, s, :], sm[:, s, :]).then_inc(inverted.sem, 1)

                    def add_up(m):
                        if not there(i, m):
                            return
                        pair = i - 1 if m < 0 else i
                        wait(dve, summed, i, m + 1)
                        wait(dve, summed_read, i, m)
                        xp = k.x[:, bass.ds(pair, 1), :].rearrange("p a c -> p (a c)")
                        dve.tensor_tensor(xp, po[:], xp, ALU.add).then_inc(summed_read.sem, 1)

                    for m in range(2):
                        rotate(m, 0)
                        mask(m - 1, 0)
                        rotated(m, 0)
                        rotate(m, 1)
                        mask(m - 1, 1)
                        shift(m - 1, 0)
                        rotated(m, 1)
                        shift(m - 1, 1)
                        row_sums(m - 1, 0)
                        rotate(m, 2)
                        row_sums(m - 1, 1)
                        rotate(m, 3)
                        rotated(m, 2)
                        add_up(m - 2)
                        rotated(m, 3)
                        values(m, 0)
                        values(m, 1)

                pipe.run(dve, body)

            @block.tensor
            def _(pe):
                def body(i):
                    def project(m, c):
                        if not there(i, m):
                            return
                        if isinstance(i, int) and i == 0:
                            pe.wait_ge(w_lo_done[m].sem, c + 1)
                        if m == 0 and c == 0:
                            wait(pe, xlo_done, i, 1)
                        wait(pe, bias_done, i, NCH * m + c - 1)
                        terms = [(x, w, kc) for kc in range(KC) for x, w in ((x_hi, w_hi), (x_hi, w_lo), (x_lo, w_hi))]
                        for n, (x, w, kc) in enumerate(terms):
                            ins = pe.matmul(pj[c % 2][:], x[:, kc, :], w[:, NCH * m + c, kc, :], start=n == 0,
                                            stop=n == len(terms) - 1)
                        ins.then_inc(projected.sem, 1)

                    def turn(m, c):
                        if not there(i, m):
                            return
                        wait(pe, tok_done, i, NTC * m + c + 1)
                        if c < 3:
                            wait(pe, turned_read, i, NTC * m + (c if c else -1))
                        else:
                            wait(pe, turned_read, i, NTC * m)
                            wait(pe, w_turned_read, i, 2 * m)
                        for h in range(4):
                            ins = pe.transpose(tp[c // 3][:, h, :], tok[c % 2][:, h * D:(h + 1) * D], k.ident[0:T2, 0:T2])
                        ins.then_inc(turned.sem, 1)

                    def turn_weights(m, s):
                        if not there(i, m):
                            return
                        wait(pe, weighed, i, 2 * m + s + 1)
                        if s == 0:
                            wait(pe, turned_read, i, NTC * (m + 1))
                        wait(pe, w_turned_read, i, 2 * m + s)
                        for h in range(4):
                            ins = pe.transpose(tp[1][0:T2, h, :], sc[s][:, h, :], k.ident[0:T2, 0:T2])
                        ins.then_inc(w_turned.sem, 1)

                    def mix(m, s):
                        if not there(i, m):
                            return
                        wait(pe, w_turned_read, i, 2 * m + s + 1)
                        wait(pe, bias_done, i, NCH * (m + 1) if s else NCH * m + NTC + 1)
                        wait(pe, mixed_read, i, 2 * m + s)
                        for h in range(4):
                            ins = pe.matmul(pz[:, h, :], v[:, 4 * s + h, :], aT[s][:, h, :], start=True, stop=True)
                        ins.then_inc(mixed.sem, 1)

                    def sum_heads(m, s):
                        if not there(i, m):
                            return
                        wait(pe, mixed_read, i, 2 * m + s + 1)
                        if s == 0:
                            wait(pe, summed_read, i, m)
                        for h in range(4 * s, 4 * s + 4):
                            ins = pe.matmul(po[:], zT[:, h, :], wo[:, m % 2 * HH + h, :], start=h == 0, stop=h == HH - 1)
                        if s == 1:
                            ins.then_inc(summed.sem, 1)

                    def score(m):
                        if not there(i, m):
                            return
                        wait(pe, turned_read, i, NTC * (m + 1))
                        for s in range(2):
                            wait(pe, masked, i, 2 * (m - 1) + s + 1)
                            for h in range(4):
                                ins = pe.matmul(ps[s][:, h, :], qkT[:, 4 * s + h, :], qkT[:, HH + 4 * s + h, :],
                                                start=True, stop=True)
                            ins.then_inc(scored.sem, 1)

                    for m in range(2):
                        if m == 0:
                            score(m - 1)
                        project(m, 0)
                        if m == 1:
                            score(m - 1)
                        project(m, 1)
                        sum_heads(m - 2, 0)
                        turn(m, 0)
                        project(m, 2)
                        project(m, 3)
                        turn(m, 1)
                        sum_heads(m - 2, 1)
                        turn_weights(m - 1, 0)
                        project(m, 4)
                        mix(m - 1, 0)
                        turn_weights(m - 1, 1)
                        turn(m, 2)
                        project(m, 5)
                        turn(m, 3)
                        mix(m - 1, 1)
                    if isinstance(i, int) and i == 0:
                        pe.wait_ge(wo_loaded.sem, 16)

                pipe.run(pe, body)


def xattn_phase(nc, k):
    NTC = 5
    NCH = 6
    NST = 3
    SRC = (0, 0, 1, 2, 2, 3)
    INS = (V_QS, V_QS, V_KS, V_QXS, V_QXS, V_VS)
    OUTS = (V_SQ, V_SQ, V_SK, V_SQX, V_SQX, V_SV)
    LNW = (V_QLW, V_QLW, V_KLW, V_QXLW, V_QXLW)
    with Phase(nc) as ctx:
        ctx.callback(ctx.clear)

        def sb(name, shape, dt=F32):
            return ctx.enter_context(nc.sbuf_tensor(f"b_{name}", shape, dt))

        def bank(name, shape):
            return ctx.enter_context(nc.psum_tensor(f"b_{name}", shape, F32))

        def sig(name, per_unit=1):
            return Signal(nc, ctx, f"b_{name}", 2 * per_unit)

        w_raw = [sb(f"w_raw{j}", [128, KC, CH]) for j in range(NST)]
        w_mean = sb("w_mean", [128, KC * 4])
        w_scale = sb("w_scale", [128, NCH, KC])
        w_hi = sb("w_hi", [128, 2 * NCH, KC, CH], F32R)
        w_lo = sb("w_lo", [128, 2 * NCH, KC, CH], F32R)
        xq = sb("xq_pair", [128, 4, KC, T2], F32R)
        sq = [sb(f"sq{j}", [T2, CH]) for j in range(2)]
        ss = sb("ss", [T2, 4, 4])
        rs = sb("rs", [T2, 4, 4])
        mhalf = sb("mhalf", [T2, 4])
        tok = [sb(f"tok{j}", [T2, CH]) for j in range(2)]
        qkT = sb("qkT", [128, HH + 4, T2])
        qxT = sb("qxT", [128, HH, T2])
        qxs = sb("qxs", [128, HH, T2])
        qx_hi = sb("qx_hi", [128, HH, T2], F32R)
        qx_lo = sb("qx_lo", [128, HH, T2], F32R)
        qb = sb("qb", [T2, HPG, 4])
        v = sb("v", [T2, 4, D])
        sc = [sb(f"sc{j}", [T2, 4, T2]) for j in range(2)]
        mx = sb("mx", [T2, 2, 4])
        sm = sb("sm", [T2, 2, 4])
        aT = [sb(f"aT{j}", [T2, 4, T2]) for j in range(2)]
        y = [sb(f"y{j}", [128, 4, T2], BF16) for j in range(2)]
        m_ = sb("m", [128, 4, T2], BF16)
        work = sb("work", [128, 4, T2], BF16)
        cq = sb("cq", [128, HH, T2], BF16)
        pj = [bank(f"pj{j}", [T2, CH]) for j in range(3)]
        tp = [bank(f"tp{j}", [128, 4, T2]) for j in range(2)]
        ps = [bank(f"ps{j}", [T2, 4, T2]) for j in range(2)]
        pzb = bank("pz", [128, 512])
        pz = pzb[:, 0:4 * T2].rearrange("p (h t) -> p h t", h=4)
        pqb = pzb[0:T2, 4 * T2:4 * T2 + HH].rearrange("p (a g) -> p a g", a=HPG)
        TP_OF = (0, 0, 0, 1, 0)

        w_loaded = [sig(f"w_loaded{j}") for j in range(NST)]
        w_scaled, w_summed, w_averaged, w_ready = sig("w_scaled"), sig("w_summed"), sig("w_averaged"), sig("w_ready")
        scale_done = sig("scale_done")
        w_hi_done, w_lo_done, half_set = sig("w_hi_done"), sig("w_lo_done"), sig("half_set")
        xq_done = Signal(nc, ctx, "b_xq_done")
        projected, v_done = sig("projected", NCH), sig("v_done")
        squared, sq_summed, vared, powed = sig("squared", NTC), sig("sq_summed", NTC), sig("vared", NTC), sig("powed", NTC)
        tok_done, turned, turned_read = sig("tok_done", NTC), sig("turned", NTC), sig("turned_read", NTC)
        qb_made, qb_done, qxs_done = sig("qb_made"), sig("qb_done"), sig("qxs_done")
        qx_hi_done, qx_lo_done, qx_stored = sig("qx_hi_done"), sig("qx_lo_done"), sig("qx_stored", 128)
        scored, masked, maxed, shifted = sig("scored", 2), sig("masked", 2), sig("maxed", 2), sig("shifted", 2)
        exped, row_summed, inverted, weighed = sig("exped", 2), sig("row_summed", 2), sig("inverted", 2), sig("weighed", 2)
        w_turned, w_turned_read = sig("w_turned", 2), sig("w_turned_read", 2)
        mixed, mixed_read = sig("mixed", 2), sig("mixed_read", 2)
        q_step, cq_done, cq_stored = sig("q_step", 8), sig("cq_done", 2), sig("cq_stored", 16)
        dma_begun = sig("dma_begun")
        pipe = Steps(PAIRS, 2)
        wait, there = pipe.wait, pipe.there

        def first(i, m):
            return isinstance(i, int) and i == 0 and m == 0

        with nc.Block() as block:
            @block.sync
            def _(sp):
                for c in range(2 * NCH):
                    if c >= NST:
                        sp.wait_ge(w_lo_done.sem, c - NST + 1)
                    sp.dma_start(w_raw[c % NST][:], k.d_xattn_w[c // NCH, c % NCH]).then_inc(w_loaded[c % NST].sem, 16)

                def body(i):
                    def store_core(m):
                        if not there(i, m):
                            return
                        pair, hh = (i - 1 if m < 0 else i), m % 2
                        wait(sp, cq_done, i, 2 * m + 2)
                        sp.sem_inc(dma_begun.sem, 1)
                        sp.dma_start(k.d_core[bass.ds(pair, 1), :, hh * HH:(hh + 1) * HH, :]
                                     .rearrange("a p h s -> p (a h) s"), cq[:]).then_inc(cq_stored.sem, 16)

                    def store_queries(m):
                        if not there(i, m):
                            return
                        pair, hh = (i - 1 if m < 0 else i), m % 2
                        wait(sp, qx_lo_done, i, m + 1)
                        sp.sem_inc(dma_begun.sem, 1)
                        wait(sp, qb_done, i, m + 1)
                        sp.sem_inc(dma_begun.sem, 1)
                        for b2 in range(2):
                            for src, dst in ((qx_hi, k.d_qhi), (qx_lo, k.d_qlo)):
                                sp.dma_start(dst[bass.ds(2 * pair + b2, 1), :, hh * HH:(hh + 1) * HH, :]
                                             .rearrange("a p h s -> p (a h) s"),
                                             src[:, :, b2 * S:(b2 + 1) * S].bitcast(F32)).then_inc(qx_stored.sem, 16)
                            for a in range(HPG):
                                sp.dma_start(k.d_qb[bass.ds(2 * pair + b2, 1), a * S:(a + 1) * S, 4 * hh:4 * hh + 4]
                                             .rearrange("a s g -> (a s) g"),
                                             qb[b2 * S:(b2 + 1) * S, a, :]).then_inc(qx_stored.sem, 16)

                    for m in range(2):
                        store_queries(m - 1)
                        store_core(m - 1)

                pipe.run(sp, body)
                wait(sp, qx_stored, PAIRS, 0)
                wait(sp, cq_stored, PAIRS, 0)

            def weight_hi(act, c):
                n = c % NCH
                if n < NTC:
                    act.wait_ge(w_ready.sem, c - c // NCH + 1)
                else:
                    act.wait_ge(w_loaded[c % NST].sem, 16 * (c // NST + 1))
                for kc in range(KC):
                    ins = act.mul(w_raw[c % NST][:, kc], w_raw[c % NST][:, kc], w_scale[:, n, kc:kc + 1])
                ins.then_inc(w_scaled.sem, 1)
                act.wait_ge(w_scaled.sem, c + 1)
                act.activation(w_hi[:, c], w_raw[c % NST][:], ACT.Copy).then_inc(w_hi_done.sem, 1)

            @block.scalar
            def _(act):
                act.wait_ge(scale_done.sem, 1)
                for c in range(NCH):
                    weight_hi(act, c)

                def body(i):
                    def square(m, c):
                        if not there(i, m):
                            return
                        wait(act, projected, i, NCH * m + c + 1)
                        wait(act, sq_summed, i, NTC * m + max(c - 1, 0))
                        act.activation(sq[c % 2][:], pj[c % 3][:], ACT.Square).then_inc(squared.sem, 1)

                    def exp(m, s):
                        if not there(i, m):
                            return
                        wait(act, shifted, i, 2 * m + s + 1)
                        act.activation(sc[s][:], sc[s][:], ACT.Exp, scale=SCALE).then_inc(exped.sem, 1)

                    def unturn(m, c):
                        if not there(i, m):
                            return
                        wait(act, turned, i, NTC * m + c + 1)
                        if c == 0:
                            wait(act, scored, i, 2 * m)
                        if c == 3:
                            wait(act, qb_made, i, m)
                        dst = qkT[:, 4 * c:4 * c + 4, :] if c < 3 else qxT[:, 4 * (c - 3):4 * (c - 3) + 4, :]
                        act.activation(dst, tp[TP_OF[c]][:], ACT.Identity, scale=k.vec[:, LNW[c]:LNW[c] + 1],
                                       bias=k.vec[:, LNW[c] + 1:LNW[c] + 2]).then_inc(turned_read.sem, 1)
                        if first(i, m) and c < 4:
                            weight_hi(act, NCH + c)

                    def unturn_weights(m, s):
                        if not there(i, m):
                            return
                        wait(act, w_turned, i, 2 * m + s + 1)
                        act.activation(aT[s][:], tp[1][0:T2], ACT.Copy).then_inc(w_turned_read.sem, 1)

                    def values(m):
                        if not there(i, m):
                            return
                        wait(act, projected, i, NCH * (m + 1))
                        wait(act, mixed, i, 2 * m)
                        act.activation(v[:].rearrange("p h e -> p (h e)"), pj[5 % 3][:], ACT.Copy).then_inc(v_done.sem, 1)

                    def context_queries(m):
                        if not there(i, m):
                            return
                        wait(act, turned_read, i, NTC * (m + 1))
                        wait(act, qx_lo_done, i, m)
                        act.mul(qxs[:], qxT[:], k.vec[:, V_KXLW:V_KXLW + 1]).then_inc(qxs_done.sem, 1)
                        wait(act, qxs_done, i, m + 1)
                        wait(act, qx_stored, i, 128 * m)
                        act.activation(qx_hi[:], qxs[:], ACT.Copy).then_inc(qx_hi_done.sem, 1)

                    for m in range(2):
                        if m == 0 and there(i, 0):
                            wait(act, projected, i, 0)
                            act.activation(xq[:].rearrange("p n k t -> p (n k) t"),
                                           k.xq[:, :, :, bass.ds(i * T2, T2)].rearrange("p n k t -> p (n k) t"),
                                           ACT.Copy).then_inc(xq_done.sem, 1)
                        square(m, 0)
                        unturn(m - 1, 4)
                        exp(m - 1, 0)
                        square(m, 1)
                        exp(m - 1, 1)
                        square(m, 2)
                        unturn(m, 0)
                        square(m, 3)
                        unturn_weights(m - 1, 0)
                        unturn(m, 1)
                        square(m, 4)
                        unturn_weights(m - 1, 1)
                        context_queries(m - 1)
                        unturn(m, 2)
                        unturn(m, 3)
                        values(m)
                        if first(i, m):
                            for c in (4, 5):
                                weight_hi(act, NCH + c)

                pipe.run(act, body)

            def weight_lo(pool, c):
                pool.wait_ge(w_hi_done.sem, c + 1)
                pool.tensor_tensor(w_lo[:, c], w_raw[c % NST][:], w_hi[:, c].bitcast(F32),
                                   ALU.subtract).then_inc(w_lo_done.sem, 1)

            @block.gpsimd
            def _(pool):
                pool.memset(mhalf[:], -0.5).then_inc(half_set.sem, 1)
                pool.wait_ge(half_set.sem, 1)
                for c in range(NCH):
                    weight_lo(pool, c)

                def body(i):
                    def power(m, c):
                        if not there(i, m):
                            return
                        wait(pool, vared, i, NTC * m + c + 1)
                        pool.tensor_tensor(rs[:, c % 4, :], ss[:, c % 4, :], mhalf[:], ALU.pow).then_inc(powed.sem, 1)

                    def weigh(m, s):
                        if not there(i, m):
                            return
                        wait(pool, inverted, i, 2 * m + s + 1)
                        pool.tensor_tensor(sc[s][:], sc[s][:], sm[:, s, :].unsqueeze(2).to_broadcast([T2, 4, T2]),
                                           ALU.mult).then_inc(weighed.sem, 1)

                    def queries_lo(m):
                        if not there(i, m):
                            return
                        wait(pool, qx_hi_done, i, m + 1)
                        pool.tensor_tensor(qx_lo[:], qxs[:], qx_hi[:].bitcast(F32), ALU.subtract).then_inc(qx_lo_done.sem, 1)

                    for m in range(2):
                        power(m, 0)
                        power(m, 1)
                        weigh(m - 1, 0)
                        power(m, 2)
                        weigh(m - 1, 1)
                        power(m, 3)
                        if first(i, m):
                            for c in range(4):
                                weight_lo(pool, NCH + c)
                        power(m, 4)
                        queries_lo(m - 1)
                        if first(i, m):
                            for c in range(4, NCH):
                                weight_lo(pool, NCH + c)

                pipe.run(pool, body)

            def centre_weights(dve, c):
                if c % NCH == NTC:
                    return
                n = c - c // NCH
                dve.wait_ge(w_loaded[c % NST].sem, 16 * (c // NST + 1))
                if n > 0:
                    dve.wait_ge(w_ready.sem, n)
                heads = w_raw[c % NST][:].rearrange("p k (h e) -> p (k h) e", h=4)
                dve.tensor_reduce(w_mean[:], heads, AX_X, ALU.add).then_inc(w_summed.sem, 1)
                dve.wait_ge(w_summed.sem, n + 1)
                dve.tensor_scalar(w_mean[:], w_mean[:], 1.0 / D, None, ALU.mult).then_inc(w_averaged.sem, 1)
                dve.wait_ge(w_averaged.sem, n + 1)
                dve.tensor_tensor(heads, heads, w_mean[:].unsqueeze(2).to_broadcast([128, KC * 4, D]),
                                  ALU.subtract).then_inc(w_ready.sem, 1)

            @block.vector
            def _(dve):
                for n in range(NCH):
                    ins = dve.tensor_scalar(w_scale[:, n, :], k.vec[:, INS[n]:INS[n] + KC], k.vec[:, OUTS[n]:OUTS[n] + 1],
                                            None, ALU.mult)
                ins.then_inc(scale_done.sem, 1)
                for c in range(NCH):
                    centre_weights(dve, c)

                def body(i):
                    def square_sums(m, c):
                        if not there(i, m):
                            return
                        n = NTC * m + c + 1
                        wait(dve, squared, i, n)
                        dve.tensor_reduce(ss[:, c % 4, :], sq[c % 2][:].rearrange("p (h e) -> p h e", h=4),
                                          AX_X, ALU.add).then_inc(sq_summed.sem, 1)
                        wait(dve, sq_summed, i, n)
                        dve.tensor_scalar(ss[:, c % 4, :], ss[:, c % 4, :], 1.0 / D, EPS, ALU.mult,
                                          ALU.add).then_inc(vared.sem, 1)

                    def normalise(m, c):
                        if not there(i, m):
                            return
                        wait(dve, powed, i, NTC * m + c + 1)
                        wait(dve, turned, i, NTC * m + c - 1 if c else NTC * m)
                        dve.tensor_tensor(tok[c % 2][:].rearrange("p (h e) -> p h e", h=4),
                                          pj[c % 3][:].rearrange("p (h e) -> p h e", h=4),
                                          rs[:, c % 4, :].unsqueeze(2).to_broadcast([T2, 4, D]),
                                          ALU.mult).then_inc(tok_done.sem, 1)
                        if first(i, m):
                            centre_weights(dve, NCH + c)

                    def shift(m, s):
                        if not there(i, m):
                            return
                        n = 2 * m + s + 1
                        wait(dve, scored, i, n)
                        wait(dve, w_turned, i, n - 2)
                        dve.tensor_tensor(sc[s][:], ps[s][:], k.bmask[:, :].unsqueeze(1).to_broadcast([T2, 4, T2]),
                                          ALU.add).then_inc(masked.sem, 1)
                        wait(dve, masked, i, n)
                        dve.tensor_reduce(mx[:, s, :], sc[s][:], AX_X, ALU.max).then_inc(maxed.sem, 1)
                        wait(dve, maxed, i, n)
                        dve.tensor_tensor(sc[s][:], sc[s][:], mx[:, s, :].unsqueeze(2).to_broadcast([T2, 4, T2]),
                                          ALU.subtract).then_inc(shifted.sem, 1)

                    def row_sums(m, s):
                        if not there(i, m):
                            return
                        n = 2 * m + s + 1
                        wait(dve, exped, i, n)
                        dve.tensor_reduce(sm[:, s, :], sc[s][:], AX_X, ALU.add).then_inc(row_summed.sem, 1)
                        wait(dve, row_summed, i, n)
                        dve.reciprocal(sm[:, s, :], sm[:, s, :]).then_inc(inverted.sem, 1)

                    def smooth_output(m, s):
                        if not there(i, m):
                            return
                        h0 = m % 2 * HH + 4 * s
                        wait(dve, mixed, i, 2 * m + s + 1)
                        smooth = k.rsm[:, h0:h0 + 4].unsqueeze(2).to_broadcast([128, 4, T2])
                        dve.tensor_tensor(y[s][:], pz, smooth, ALU.mult).then_inc(mixed_read.sem, 1)

                    def quantise_output(m, s):
                        if not there(i, m):
                            return
                        wait(dve, mixed_read, i, 2 * m + s + 1)
                        wait(dve, cq_done, i, 2 * m + s)
                        if s == 0:
                            wait(dve, cq_stored, i, 16 * m)
                        made = [8 * m + 4 * s]

                        def link(ins):
                            made[0] += 1
                            ins.then_inc(q_step.sem, 1)
                            wait(dve, q_step, i, made[0])

                        quantise(dve, link, cq[:, 4 * s:4 * s + 4, :], y[s][:], work[:], m_[:]).then_inc(cq_done.sem, 1)

                    def offsets(m):
                        if not there(i, m):
                            return
                        wait(dve, qb_made, i, m + 1)
                        wait(dve, qx_stored, i, 128 * m)
                        dve.tensor_copy(qb[:], pqb).then_inc(qb_done.sem, 1)

                    for m in range(2):
                        shift(m - 1, 0)
                        square_sums(m, 0)
                        shift(m - 1, 1)
                        normalise(m, 0)
                        offsets(m - 1)
                        square_sums(m, 1)
                        row_sums(m - 1, 0)
                        square_sums(m, 2)
                        normalise(m, 1)
                        row_sums(m - 1, 1)
                        square_sums(m, 3)
                        normalise(m, 2)
                        square_sums(m, 4)
                        smooth_output(m - 1, 0)
                        normalise(m, 3)
                        quantise_output(m - 1, 0)
                        normalise(m, 4)
                        smooth_output(m - 1, 1)
                        quantise_output(m - 1, 1)
                        if first(i, m):
                            centre_weights(dve, 2 * NCH - 1)

                pipe.run(dve, body)

            @block.tensor
            def _(pe):
                def body(i):
                    def project(m, c):
                        if not there(i, m):
                            return
                        if isinstance(i, int) and i == 0:
                            pe.wait_ge(w_lo_done.sem, NCH * m + c + 1)
                        if m == 0 and c == 0:
                            wait(pe, xq_done, i, 1)
                        if c == 2:
                            wait(pe, v_done, i, m)
                        else:
                            wait(pe, tok_done, i, NTC * m + (c - 2 if c >= 3 else c - 1))
                        for n in range(2 * KC):
                            w = (w_hi, w_lo)[n % 2]
                            ins = pe.matmul(pj[c % 3][:], xq[:, SRC[c], n // 2, :], w[:, NCH * m + c, n // 2, :],
                                            start=n == 0, stop=n == 2 * KC - 1)
                        ins.then_inc(projected.sem, 1)

                    def turn(m, c):
                        if not there(i, m):
                            return
                        wait(pe, tok_done, i, NTC * m + c + 1)
                        if c == 3:
                            wait(pe, turned_read, i, NTC * m - 1)
                            wait(pe, w_turned_read, i, 2 * m)
                        else:
                            wait(pe, turned_read, i, NTC * m + (3 if c == 4 else c))
                        for h in range(4):
                            ins = pe.transpose(tp[TP_OF[c]][:, h, :], tok[c % 2][:, h * D:(h + 1) * D], k.ident[0:T2, 0:T2])
                        ins.then_inc(turned.sem, 1)

                    def turn_weights(m, s):
                        if not there(i, m):
                            return
                        wait(pe, weighed, i, 2 * m + s + 1)
                        if s == 0:
                            wait(pe, turned_read, i, NTC * m + 4)
                        wait(pe, w_turned_read, i, 2 * m + s)
                        for h in range(4):
                            ins = pe.transpose(tp[1][0:T2, h, :], sc[s][:, h, :], k.ident[0:T2, 0:T2])
                        ins.then_inc(w_turned.sem, 1)

                    def mix(m, s):
                        if not there(i, m):
                            return
                        wait(pe, w_turned_read, i, 2 * m + s + 1)
                        wait(pe, v_done, i, m + 1)
                        wait(pe, mixed_read, i, 2 * m + s)
                        wait(pe, qb_done, i, m + 1)
                        for h in range(4):
                            ins = pe.matmul(pz[:, h, :], v[:, (4 * s + h) // HPG, :], aT[s][:, h, :], start=True, stop=True)
                        ins.then_inc(mixed.sem, 1)

                    def score(m):
                        if not there(i, m):
                            return
                        wait(pe, turned_read, i, NTC * m + 3)
                        for s in range(2):
                            wait(pe, masked, i, 2 * (m - 1) + s + 1)
                            for h in range(4):
                                ins = pe.matmul(ps[s][:, h, :], qkT[:, 4 * s + h, :], qkT[:, HH + (4 * s + h) // HPG, :],
                                                start=True, stop=True)
                            ins.then_inc(scored.sem, 1)

                    def offsets(m):
                        if not there(i, m):
                            return
                        wait(pe, turned_read, i, NTC * (m + 1))
                        wait(pe, mixed_read, i, 2 * m)
                        for h in range(HH):
                            ins = pe.matmul(pqb[:, h % HPG, h // HPG:h // HPG + 1], qxT[:, h, :],
                                            k.vec[:, V_KXLB:V_KXLB + 1], start=True, stop=True)
                        ins.then_inc(qb_made.sem, 1)

                    for m in range(2):
                        project(m, 0)
                        turn(m - 1, 4)
                        project(m, 1)
                        project(m, 2)
                        offsets(m - 1)
                        turn(m, 0)
                        project(m, 3)
                        turn_weights(m - 1, 0)
                        project(m, 4)
                        turn(m, 1)
                        turn_weights(m - 1, 1)
                        turn(m, 2)
                        mix(m - 1, 0)
                        project(m, 5)
                        turn(m, 3)
                        mix(m - 1, 1)
                        score(m)

                pipe.run(pe, body)


def context_phase(nc, k):
    QN = HPG * S
    NS = G
    DT = 2 * TT_C
    ND = SC // DT
    PER = 4 * ND
    PC = 3
    NPC = NT_C // PC
    L_SCORE, L_TURN, L_MIX, L_OUT = 3, 4, 5, 6
    with Phase(nc) as ctx:
        ctx.callback(ctx.clear)

        def sb(name, shape, dt=F32):
            return ctx.enter_context(nc.sbuf_tensor(f"c_{name}", shape, dt))

        def sig(name, per=1):
            return Signal(nc, ctx, f"c_{name}", per)

        wk_hi = sb("wk_hi", [128, KC, G * D], F32R)
        wk_lo = sb("wk_lo", [128, KC, G * D], F32R)
        wv = sb("wv", [128, KC, G * D])
        stageT = [sb(f"stageT{j}", [128, KC, DT]) for j in range(3)]
        stageC = [sb(f"stageC{j}", [TT_C, PC, C]) for j in range(2)]
        cT_hi = sb("cT_hi", [128, KC, SC], F32R)
        cT_lo = sb("cT_lo", [128, KC, SC], F32R)
        c_hi = sb("c_hi", [TT_C, NT_C, C], F32R)
        c_lo = sb("c_lo", [TT_C, NT_C, C], F32R)
        q_hi = sb("q_hi", [128, NH, S], F32R)
        q_lo = sb("q_lo", [128, NH, S], F32R)
        qb = sb("qb", [QN, G])
        kT_hi = sb("kT_hi", [128, 2, 2, SC], F32R)
        kT_lo = sb("kT_lo", [128, 2, 2, SC], F32R)
        sq = [sb(f"sq{j}", [TT_C, 4, D]) for j in range(2)]
        kn = [sb(f"kn{j}", [TT_C, 4, D]) for j in range(2)]
        ss = sb("ss", [TT_C, 4, 4])
        rs = sb("rs", [TT_C, 4, 4])
        mhalf = sb("mhalf", [128, 4])
        P = [sb(f"P{j}", [QN, SC]) for j in range(2)]
        PT_hi = [sb(f"PT_hi{j}", [TT_C, NT_C, QN], F32R) for j in range(2)]
        PT_lo = [sb(f"PT_lo{j}", [TT_C, NT_C, QN], F32R) for j in range(2)]
        w_mean = sb("w_mean", [128, KC * G])
        mx = sb("mx", [QN, 2])
        ebias = sb("ebias", [QN, 2])
        esum = sb("esum", [QN, 4])
        rsum = sb("rsum", [QN, 4])
        U = sb("U", [QN, C])
        UT = sb("UT", [128, KC, QN])
        y = sb("y", [128, HPG, S], BF16)
        m_ = sb("m", [128, HPG, S], BF16)
        work = sb("work", [128, HPG, S], BF16)
        cq = sb("cq", [128, NH, S], BF16)
        p_scores = ctx.enter_context(nc.psum_tensor("c_scores", [128, 3, 512], F32))
        p_keys = [ctx.enter_context(nc.psum_tensor(f"c_keys{j}", [128, 4, D], F32)) for j in range(2)]
        p_kturn = ctx.enter_context(nc.psum_tensor("c_kturn", [128, 512], F32))
        p_pturn = ctx.enter_context(nc.psum_tensor("c_pturn", [128, 4, 128], F32))
        p_mix = ctx.enter_context(nc.psum_tensor("c_mix", [128, 512], F32))
        scores = p_scores[0:QN, :, 0:SC // 3]
        kturned = p_kturn[:, 0:2 * DT].rearrange("p (g t) -> p g t", g=2)
        pturned = p_pturn[0:TT_C, :, 0:QN]
        ut_at, out_at = p_mix[:, C:C + KC * QN], p_mix[:, C:C + QN]

        w_loaded, w_ready, w_hi_done, w_lo_done = sig("w_loaded"), sig("w_ready"), sig("w_hi_done"), sig("w_lo_done")
        prep_step = sig("prep_step", 2)
        half_set = sig("half_set")
        stagedT = [sig(f"stagedT{j}", 2 * 16) for j in range(3)]
        stagedC = [sig(f"stagedC{j}", 2 * 16) for j in range(2)]
        cT_hi_done, cT_lo_done = sig("cT_hi_done", ND), sig("cT_lo_done", ND)
        c_hi_done, c_lo_done = sig("c_hi_done", NPC), sig("c_lo_done", NPC)
        q_loaded = [sig(f"q_loaded{j}", 48) for j in range(2)]
        projected, squared, vared, powed = sig("projected", PER), sig("squared", PER), sig("vared", PER), sig("powed", PER)
        kn_done, k_turned = sig("kn_done", PER), sig("k_turned", PER)
        kT_hi_done, kT_lo_done = sig("kT_hi_done", PER), sig("kT_lo_done", PER)
        scored, biased, exped, rsum_done = sig("scored", NS), sig("biased", NS), sig("exped", NS), sig("rsum_done", NS)
        p_turned, PT_hi_done, PT_lo_done = sig("p_turned", 3 * NS), sig("PT_hi_done", 3 * NS), sig("PT_lo_done", 3 * NS)
        mixed = sig("mixed", 3 * NS)
        U_done, U_turned, UT_done = sig("U_done", NS), sig("U_turned", NS), sig("UT_done", NS)
        out_done, out_read, cq_done = sig("out_done", NS), sig("out_read", NS), sig("cq_done", NS)
        cq_stored = [sig(f"cq_stored{j}", 16) for j in range(2)]
        dma_begun = sig("dma_begun")
        r_step, b_step, q_step = sig("r_step", PER), sig("b_step", 2 * NS), sig("q_step", 4 * NS)

        def wait(eng, signal_of, b, n):
            if not isinstance(b, int) or signal_of.at(b, n) > 0:
                eng.wait_ge(signal_of.sem, signal_of.at(b, n))

        def there(b, m):
            return not isinstance(b, int) or 0 <= NS * b + m < NS * B

        def run(eng, body):
            body(0)
            with eng.Fori(1, B) as b:
                body(b)
            body(B)

        def steps(b):
            return range(NS if not isinstance(b, int) or b < B else L_OUT)

        def keys_in(b):
            return not isinstance(b, int) or b < B

        with nc.Block() as block:
            @block.sync
            def _(sp):
                for t in range(KC):
                    sp.dma_start(k.c_wraw[:, t], k.d_ctx_wk[:, t]).then_inc(w_loaded.sem, 16)
                sp.dma_start(wv[:], k.d_ctx_wv).then_inc(w_loaded.sem, 16)

                def body(b):
                    def load_T(d):
                        wait(sp, cT_lo_done, b, d - 2)
                        sp.sem_inc(dma_begun.sem, 1)
                        sp.dma_start(stageT[d % 3][:], k.d_ctxT[bass.ds(b, 1), :, :, d * DT:(d + 1) * DT]
                                     .rearrange("a k p t -> p (a k) t")).then_inc(stagedT[d % 3].sem, 16)

                    def load_C(p):
                        wait(sp, c_lo_done, b, p - 1)
                        sp.sem_inc(dma_begun.sem, 1)
                        sp.dma_start(stageC[p % 2][:], k.d_ctx[bass.ds(b, 1), :, PC * p:PC * (p + 1), :]
                                     .rearrange("a p j c -> (a p) j c")).then_inc(stagedC[p % 2].sem, 16)

                    def load_q(hf):
                        wait(sp, scored, b, 4 * hf + 4 - NS)
                        sp.sem_inc(dma_begun.sem, 1)
                        wait(sp, biased, b, 4 * hf + 4 - NS)
                        sp.sem_inc(dma_begun.sem, 1)
                        hs = slice(hf * HH, (hf + 1) * HH)
                        for dst, src in ((q_hi, k.d_qhi), (q_lo, k.d_qlo)):
                            sp.dma_start(dst[:, hs, :].bitcast(F32), src[bass.ds(b, 1), :, hs, :]
                                         .rearrange("a p h s -> (a p) h s")).then_inc(q_loaded[hf].sem, 16)
                        sp.dma_start(qb[:, 4 * hf:4 * hf + 4], k.d_qb[bass.ds(b, 1), :, 4 * hf:4 * hf + 4]
                                     .rearrange("a q g -> (a q) g")).then_inc(q_loaded[hf].sem, 16)

                    def store(hf):
                        wait(sp, cq_done, b, 4 * hf + 4 - NS)
                        sp.sem_inc(dma_begun.sem, 1)
                        hs = slice(hf * HH, (hf + 1) * HH)
                        sp.dma_start(k.d_xout[bass.ds(b - 1, 1), :, hs, :].rearrange("a p h s -> (a p) h s"),
                                     cq[:, hs, :]).then_inc(cq_stored[hf].sem, 16)

                    loading, storing = keys_in(b), not isinstance(b, int) or b > 0
                    if loading:
                        for d in range(3):
                            load_T(d)
                        load_q(0)
                        for p in range(2):
                            load_C(p)
                        for d in range(3, ND):
                            load_T(d)
                    if storing:
                        store(0)
                    if loading:
                        load_q(1)
                        for p in range(2, NPC):
                            load_C(p)
                    if storing:
                        store(1)

                run(sp, body)
                for hf in range(2):
                    sp.wait_ge(cq_stored[hf].sem, 16 * B)

            @block.scalar
            def _(act):
                act.wait_ge(w_ready.sem, 1)
                act.activation(wk_hi[:], k.c_wraw[:], ACT.Copy).then_inc(w_hi_done.sem, 1)

                def body(b):
                    def split_T(d):
                        wait(act, stagedT[d % 3], b, 16 * (d // 3 + 1))
                        wait(act, projected, b, d + 1 - ND)
                        act.activation(cT_hi[:, :, d * DT:(d + 1) * DT], stageT[d % 3][:], ACT.Copy).then_inc(cT_hi_done.sem, 1)

                    def split_C(p):
                        wait(act, stagedC[p % 2], b, 16 * (p // 2 + 1))
                        wait(act, mixed, b, (PC * p + PC - 1) // 4 + 1 - 3)
                        act.activation(c_hi[:, PC * p:PC * (p + 1), :], stageC[p % 2][:], ACT.Copy).then_inc(c_hi_done.sem, 1)

                    def square(t):
                        wait(act, projected, b, t + 1)
                        wait(act, vared, b, t - 1)
                        act.activation(sq[t % 2][:], p_keys[t % 2][0:TT_C], ACT.Square).then_inc(squared.sem, 1)

                    def key_hi(t):
                        if not there(b, t // 3):
                            return
                        wait(act, k_turned, b, t + 1)
                        if t % ND == 0:
                            wait(act, scored, b, 2 * (t // ND) - 2)
                        q, d = t // ND, t % ND
                        act.activation(kT_hi[:, q % 2, :, d * DT:(d + 1) * DT], kturned, ACT.Copy).then_inc(kT_hi_done.sem, 1)

                    def exp(m):
                        if not there(b, m):
                            return
                        wait(act, biased, b, m + 1)
                        wait(act, p_turned, b, 3 * (m - 1))
                        act.activation(P[m % 2][:].rearrange("p (a t) -> p a t", a=3), scores, ACT.Exp, scale=SCALE,
                                       bias=ebias[:, m % 2:m % 2 + 1], accum_out=esum[:, m % 4:m % 4 + 1]).then_inc(exped.sem, 1)

                    def weights_hi(m, r):
                        if not there(b, m):
                            return
                        wait(act, p_turned, b, 3 * m + r + 1)
                        if r == 0:
                            wait(act, mixed, b, 3 * (m - 1))
                        act.activation(PT_hi[m % 2][:, 4 * r:4 * r + 4, :], pturned, ACT.Copy).then_inc(PT_hi_done.sem, 1)

                    def mixture(m):
                        if not there(b, m):
                            return
                        wait(act, rsum_done, b, m + 1)
                        wait(act, U_turned, b, m)
                        wait(act, mixed, b, 3 * m + 3)
                        act.mul(U[:], p_mix[0:QN, 0:C], rsum[:, m % 4:m % 4 + 1]).then_inc(U_done.sem, 1)

                    def mixture_turned(m):
                        if not there(b, m):
                            return
                        wait(act, U_turned, b, m + 1)
                        wait(act, out_done, b, m)
                        act.activation(UT[:].rearrange("p k q -> p (k q)"), ut_at, ACT.Copy).then_inc(UT_done.sem, 1)

                    def smoothed_output(m):
                        if not there(b, m):
                            return
                        n = HPG * (m % NS)
                        wait(act, out_done, b, m + 1)
                        wait(act, cq_done, b, m)
                        for a in range(HPG):
                            ins = act.mul(y[:, a, :], out_at[:, a * S:(a + 1) * S], k.rsm[:, NH + n + a:NH + n + a + 1])
                        ins.then_inc(out_read.sem, 1)

                    for s in steps(b):
                        new = keys_in(b)
                        if new and s == 0:
                            for d in range(3):
                                split_T(d)
                        if new and s == 1:
                            for d in range(4, ND):
                                split_T(d)
                        mixture_turned(s - L_OUT)
                        weights_hi(s - L_TURN, 0)
                        key_hi(3 * s - 2)
                        if new and s == 5:
                            split_C(2)
                        if new:
                            square(3 * s)
                        smoothed_output(s - L_OUT)
                        weights_hi(s - L_TURN, 1)
                        key_hi(3 * s - 1)
                        exp(s - L_SCORE)
                        if new:
                            square(3 * s + 1)
                        if new and s == 5:
                            split_C(3)
                        if new and s == 0:
                            split_T(3)
                        if new and s == 4:
                            split_C(0)
                        weights_hi(s - L_TURN, 2)
                        key_hi(3 * s)
                        if new:
                            square(3 * s + 2)
                        mixture(s - L_MIX)
                        if new and s == 4:
                            split_C(1)

                run(act, body)

            @block.gpsimd
            def _(pool):
                pool.memset(mhalf[:], -0.5).then_inc(half_set.sem, 1)
                pool.wait_ge(half_set.sem, 1)
                pool.wait_ge(w_hi_done.sem, 1)
                pool.tensor_tensor(wk_lo[:], k.c_wraw[:], wk_hi[:].bitcast(F32), ALU.subtract).then_inc(w_lo_done.sem, 1)

                def body(b):
                    if not keys_in(b):
                        return

                    def split_T(d):
                        wait(pool, cT_hi_done, b, d + 1)
                        at = slice(d * DT, (d + 1) * DT)
                        pool.tensor_tensor(cT_lo[:, :, at], stageT[d % 3][:], cT_hi[:, :, at].bitcast(F32),
                                           ALU.subtract).then_inc(cT_lo_done.sem, 1)

                    def split_C(p):
                        wait(pool, c_hi_done, b, p + 1)
                        at = slice(PC * p, PC * (p + 1))
                        pool.tensor_tensor(c_lo[:, at, :], stageC[p % 2][:], c_hi[:, at, :].bitcast(F32),
                                           ALU.subtract).then_inc(c_lo_done.sem, 1)

                    def power(t):
                        wait(pool, vared, b, t + 1)
                        pool.tensor_tensor(rs[:, t % 4, :], ss[:, t % 4, :], mhalf[0:TT_C], ALU.pow).then_inc(powed.sem, 1)

                    for s in range(NS):
                        if s == 0:
                            for d in range(3):
                                split_T(d)
                        if s == 1:
                            for d in range(4, ND):
                                split_T(d)
                        if s == 5:
                            split_C(2)
                        power(3 * s)
                        if s == 5:
                            split_C(3)
                        power(3 * s + 1)
                        if s == 0:
                            split_T(3)
                        if s == 4:
                            split_C(0)
                        power(3 * s + 2)
                        if s == 4:
                            split_C(1)

                run(pool, body)

            @block.vector
            def _(dve):
                prep = Chain(dve, prep_step)
                dve.wait_ge(w_loaded.sem, 48)
                heads = k.c_wraw[:].rearrange("p k (h e) -> p (k h) e", h=G)
                prep(dve.tensor_reduce(w_mean[:], heads, AX_X, ALU.add))
                prep(dve.tensor_scalar(w_mean[:], w_mean[:], 1.0 / D, None, ALU.mult))
                dve.tensor_tensor(heads, heads, w_mean[:].unsqueeze(2).to_broadcast([128, KC * G, D]),
                                  ALU.subtract).then_inc(w_ready.sem, 1)

                def body(b):
                    def key_sums(t):
                        wait(dve, squared, b, t + 1)
                        dve.tensor_reduce(ss[:, t % 4, :], sq[t % 2][:], AX_X, ALU.add).then_inc(r_step.sem, 1)
                        wait(dve, r_step, b, t + 1)
                        dve.tensor_scalar(ss[:, t % 4, :], ss[:, t % 4, :], 1.0 / D, EPS, ALU.mult, ALU.add).then_inc(vared.sem, 1)

                    def key_norm(t):
                        if not there(b, t // 3):
                            return
                        wait(dve, powed, b, t + 1)
                        wait(dve, k_turned, b, t - 1)
                        dve.tensor_tensor(kn[t % 2][:], p_keys[t % 2][0:TT_C],
                                          rs[:, t % 4, :].unsqueeze(2).to_broadcast([TT_C, 4, D]),
                                          ALU.mult).then_inc(kn_done.sem, 1)

                    def key_lo(t):
                        if not there(b, t // 3):
                            return
                        wait(dve, kT_hi_done, b, t + 1)
                        q, at = t // ND, slice((t % ND) * DT, (t % ND + 1) * DT)
                        dve.tensor_tensor(kT_lo[:, q % 2, :, at], kturned, kT_hi[:, q % 2, :, at].bitcast(F32),
                                          ALU.subtract).then_inc(kT_lo_done.sem, 1)

                    def softmax_bias(m):
                        if not there(b, m):
                            return
                        one, g = slice(m % 2, m % 2 + 1), m % NS
                        wait(dve, scored, b, m + 1)
                        if m % 4 == 0:
                            wait(dve, q_loaded[g // 4], b, 48 if m >= 0 else 0)
                        dve.tensor_reduce(mx[:, one], scores, mybir.AxisListType.XY, ALU.max).then_inc(b_step.sem, 1)
                        wait(dve, b_step, b, 2 * m + 1)
                        dve.tensor_scalar(mx[:, one], mx[:, one], qb[:, g:g + 1], None, ALU.add).then_inc(b_step.sem, 1)
                        wait(dve, b_step, b, 2 * m + 2)
                        wait(dve, exped, b, m - 1)
                        dve.tensor_scalar(ebias[:, one], qb[:, g:g + 1], mx[:, one], SCALE, ALU.subtract,
                                          ALU.mult).then_inc(biased.sem, 1)

                    def weight_sum(m):
                        if not there(b, m):
                            return
                        wait(dve, exped, b, m + 1)
                        one = slice(m % 4, m % 4 + 1)
                        dve.reciprocal(rsum[:, one], esum[:, one]).then_inc(rsum_done.sem, 1)

                    def weights_lo(m, r):
                        if not there(b, m):
                            return
                        wait(dve, PT_hi_done, b, 3 * m + r + 1)
                        at = slice(4 * r, 4 * r + 4)
                        dve.tensor_tensor(PT_lo[m % 2][:, at, :], pturned, PT_hi[m % 2][:, at, :].bitcast(F32),
                                          ALU.subtract).then_inc(PT_lo_done.sem, 1)

                    def quantised_output(m):
                        if not there(b, m):
                            return
                        n = HPG * (m % NS)
                        wait(dve, out_read, b, m + 1)
                        if m % 4 == 0:
                            wait(dve, cq_stored[m % NS // 4], b, 16 * (m // NS))
                        made = [4 * m]

                        def link(ins):
                            made[0] += 1
                            ins.then_inc(q_step.sem, 1)
                            wait(dve, q_step, b, made[0])

                        quantise(dve, link, cq[:, n:n + HPG, :], y[:], work[:], m_[:]).then_inc(cq_done.sem, 1)

                    for s in steps(b):
                        new = keys_in(b)
                        weight_sum(s - L_TURN)
                        key_norm(3 * s - 1)
                        weights_lo(s - L_TURN, 0)
                        key_lo(3 * s - 2)
                        softmax_bias(s - L_SCORE)
                        if new:
                            key_sums(3 * s)
                        weights_lo(s - L_TURN, 1)
                        key_lo(3 * s - 1)
                        key_norm(3 * s)
                        if new:
                            key_sums(3 * s + 1)
                        quantised_output(s - L_OUT)
                        weights_lo(s - L_TURN, 2)
                        key_lo(3 * s)
                        key_norm(3 * s + 1)
                        if new:
                            key_sums(3 * s + 2)

                run(dve, body)

            @block.tensor
            def _(pe):
                pe.wait_ge(w_lo_done.sem, 1)
                pe.wait_ge(w_loaded.sem, 48)

                def body(b):
                    def keys(t):
                        q, d = t // ND, t % ND
                        if q == 0:
                            wait(pe, cT_lo_done, b, d + 1)
                        wait(pe, kn_done, b, t - 1)
                        terms = [(x, w, kc) for kc in range(KC)
                                 for x, w in ((cT_hi, wk_hi), (cT_hi, wk_lo), (cT_lo, wk_hi))]
                        for a in range(2):
                            at = d * DT + a * TT_C
                            for n, (x, w, kc) in enumerate(terms):
                                ins = pe.matmul(p_keys[t % 2][0:TT_C, 2 * a:2 * a + 2, :].rearrange("p g e -> p (g e)"),
                                                x[:, kc, at:at + TT_C], w[:, kc, 2 * q * D:2 * (q + 1) * D],
                                                start=n == 0, stop=n == len(terms) - 1)
                        ins.then_inc(projected.sem, 1)

                    def turn_keys(t):
                        if not there(b, t // 3):
                            return
                        wait(pe, kn_done, b, t + 1)
                        wait(pe, kT_lo_done, b, t)
                        for a in range(2):
                            for g in range(2):
                                ins = pe.transpose(kturned[:, g, a * TT_C:(a + 1) * TT_C], kn[t % 2][:, 2 * a + g, :],
                                                   k.ident[0:TT_C, 0:TT_C])
                        ins.then_inc(k_turned.sem, 1)

                    def score(m):
                        if not there(b, m):
                            return
                        g, par = m % NS, (m // 2) % 2
                        if m >= 0 and m % 4 == 0:
                            wait(pe, q_loaded[g // 4], b, 48)
                        wait(pe, kT_lo_done, b, ND * (m // 2) + ND)
                        wait(pe, exped, b, m)
                        for t in range(3):
                            for n, (x, w) in enumerate(((q_hi, kT_hi), (q_hi, kT_lo), (q_lo, kT_hi))):
                                ins = pe.matmul(scores[:, t, :], x[:, HPG * g:HPG * (g + 1), :].rearrange("p a s -> p (a s)"),
                                                w[:, par, m % 2, t * (SC // 3):(t + 1) * (SC // 3)], start=n == 0, stop=n == 2)
                        ins.then_inc(scored.sem, 1)

                    def turn_weights(m, r):
                        if not there(b, m):
                            return
                        wait(pe, exped, b, m + 1)
                        wait(pe, PT_lo_done, b, 3 * m + r)
                        for a in range(4):
                            j = 4 * r + a
                            ins = pe.transpose(pturned[:, a, :], P[m % 2][:, j * TT_C:(j + 1) * TT_C], k.ident[0:QN, 0:QN])
                        ins.then_inc(p_turned.sem, 1)

                    def mix(m, r):
                        if not there(b, m):
                            return
                        wait(pe, PT_lo_done, b, 3 * m + r + 1)
                        if r == 0:
                            wait(pe, out_read, b, m)
                        if m == 0:
                            wait(pe, c_lo_done, b, r + 2)
                        for a in range(4):
                            j = 4 * r + a
                            for n, (x, w) in enumerate(((PT_hi, c_hi), (PT_hi, c_lo), (PT_lo, c_hi))):
                                ins = pe.matmul(p_mix[0:QN, 0:C], x[m % 2][:, j, :], w[:, j, :],
                                                start=j == 0 and n == 0, stop=j == NT_C - 1 and n == 2)
                        ins.then_inc(mixed.sem, 1)

                    def turn_mixture(m):
                        if not there(b, m):
                            return
                        wait(pe, U_done, b, m + 1)
                        for kc in range(KC):
                            ins = pe.transpose(ut_at[:, kc * QN:(kc + 1) * QN], U[:, kc * 128:(kc + 1) * 128], k.ident[0:QN, 0:QN])
                        ins.then_inc(U_turned.sem, 1)

                    def project_out(m):
                        if not there(b, m):
                            return
                        g = m % NS
                        wait(pe, UT_done, b, m + 1)
                        for kc in range(KC):
                            ins = pe.matmul(out_at, wv[:, kc, g * D:(g + 1) * D], UT[:, kc, :], start=kc == 0, stop=kc == KC - 1)
                        ins.then_inc(out_done.sem, 1)

                    for s in steps(b):
                        new = keys_in(b)
                        score(s - L_SCORE)
                        turn_mixture(s - L_OUT)
                        turn_weights(s - L_TURN, 0)
                        turn_keys(3 * s - 2)
                        if new:
                            keys(3 * s)
                        project_out(s - L_OUT)
                        turn_weights(s - L_TURN, 1)
                        turn_keys(3 * s - 1)
                        if new:
                            keys(3 * s + 1)
                        mix(s - L_MIX, 0)
                        mix(s - L_MIX, 1)
                        turn_weights(s - L_TURN, 2)
                        turn_keys(3 * s)
                        if new:
                            keys(3 * s + 2)
                        mix(s - L_MIX, 2)

                run(pe, body)


def project_phase(nc, k):
    CW = 4
    NCH = 2 * NH // CW
    with Phase(nc) as ctx:
        ctx.callback(ctx.clear)

        def sb(name, shape, dt=F32):
            return ctx.enter_context(nc.sbuf_tensor(f"d_{name}", shape, dt))

        def sig(name):
            return Signal(nc, ctx, f"d_{name}").sem

        w_raw = [sb(f"w_raw{j}", [128, CW, C]) for j in range(2)]
        w_hi = [sb(f"w_hi{j}", [128, CW, C], F32R) for j in range(2)]
        w_lo = [sb(f"w_lo{j}", [128, CW, C], F32R) for j in range(2)]
        cat = [sb(f"cat{j}", [128, CW * N], BF16) for j in range(2)]
        catr = [sb(f"catr{j}", [128, PAIRS, CW, T2], F32R) for j in range(2)]
        osc = sb("osc", [128, 1])
        po = [ctx.enter_context(nc.psum_tensor(f"d_po{j}", [T2, C], F32)) for j in range(PAIRS)]
        w_loaded, cat_loaded = [sig("w_loaded0"), sig("w_loaded1")], [sig("cat_loaded0"), sig("cat_loaded1")]
        w_hi_done, w_lo_done, cast, used = sig("w_hi_done"), sig("w_lo_done"), sig("cast"), sig("used")
        osc_done, summed, added = sig("osc_done"), sig("summed"), sig("added")

        with nc.Block() as block:
            @block.sync
            def _(sp):
                for c in range(NCH):
                    if c >= 2:
                        sp.wait_ge(w_lo_done, c - 1)
                    sp.dma_start(w_raw[c % 2][:], k.d_proj_w[:, CW * c:CW * (c + 1), :]).then_inc(w_loaded[c % 2], 16)
                    if c >= 2:
                        sp.wait_ge(cast, c - 1)
                    h0 = CW * (c % (NCH // 2))
                    src = (k.d_core if c < NCH // 2 else k.d_xout)[:, :, h0:h0 + CW, :].rearrange("a p h s -> p a (h s)")
                    dst = cat[c % 2][:].rearrange("q (a n) -> q a n", a=PAIRS if c < NCH // 2 else B)
                    sp.dma_start(dst, src).then_inc(cat_loaded[c % 2], 16)

            @block.scalar
            def _(act):
                for c in range(NCH):
                    act.wait_ge(w_loaded[c % 2], 16 * (c // 2 + 1))
                    if c >= 2:
                        act.wait_ge(used, c - 1)
                    act.activation(w_hi[c % 2][:], w_raw[c % 2][:], ACT.Copy).then_inc(w_hi_done, 1)
                    act.wait_ge(cat_loaded[c % 2], 16 * (c // 2 + 1))
                    if c < NCH // 2:
                        src = cat[c % 2][:].rearrange("q (p h t) -> q p h t", p=PAIRS, h=CW)
                        act.activation(catr[c % 2][:], src, ACT.Copy).then_inc(cast, 1)
                    else:
                        src = cat[c % 2][:].rearrange("q (p b h s) -> q p b h s", p=PAIRS, b=2, h=CW)
                        for b2 in range(2):
                            ins = act.activation(catr[c % 2][:, :, :, b2 * S:(b2 + 1) * S], src[:, :, b2], ACT.Copy)
                        ins.then_inc(cast, 1)

            @block.vector
            def _(dve):
                dve.tensor_tensor(osc[:], k.vec[:, V_SPI:V_SPI + 1], k.vec[:, V_SPW:V_SPW + 1], ALU.mult).then_inc(osc_done, 1)
                dve.wait_ge(osc_done, 1)
                for c in range(NCH):
                    dve.wait_ge(w_hi_done, c + 1)
                    dve.tensor_tensor(w_lo[c % 2][:], w_raw[c % 2][:], w_hi[c % 2][:].bitcast(F32),
                                      ALU.subtract).then_inc(w_lo_done, 1)
                for p in range(PAIRS):
                    dve.wait_ge(summed, p + 1)
                    dve.scalar_tensor_tensor(k.x[:, p, :], po[p][:], osc[0:T2, 0:1], k.x[:, p, :], ALU.mult,
                                             ALU.add).then_inc(added, 1)
                dve.wait_ge(added, PAIRS)

            @block.tensor
            def _(pe):
                for c in range(NCH):
                    pe.wait_ge(cast, c + 1)
                    pe.wait_ge(w_lo_done, c + 1)
                    for p in range(PAIRS):
                        for t in range(CW):
                            for w in (w_hi, w_lo):
                                ins = pe.matmul(po[p][:], catr[c % 2][:, p, t, :], w[c % 2][:, t, :],
                                                start=c == 0 and t == 0 and w is w_hi,
                                                stop=c == NCH - 1 and t == CW - 1 and w is w_lo)
                        if c == NCH - 1:
                            ins.then_inc(summed, 1)
                    if c < NCH - 1:
                        ins.then_inc(used, 1)


def gate_phase(nc, k):
    with Phase(nc) as ctx:
        ctx.callback(ctx.clear)
        def sb(name, shape, dt=F32):
            return ctx.enter_context(nc.sbuf_tensor(f"g_{name}", shape, dt))

        def sig(name, per=1, primed=0):
            return Signal(nc, ctx, f"g_{name}", per, primed)

        gw = sb("gw", [128, KC, E])
        b2 = sb("b2", [E, C])
        rank = sb("rank", [T2, E])
        lg = sb("lg", [T2, PAIRS, E])
        left = sb("left", [T2, PAIRS, E])
        eq = sb("eq", [T2, PAIRS, E])
        pick = sb("pick", [T2, PAIRS, E])
        best = sb("best", [T2, PAIRS])
        top = sb("top", [T2, PAIRS])
        tie = sb("tie", [T2, PAIRS])
        GT = sb("GT", [E, PAIRS, T2])
        pl = ctx.enter_context(nc.psum_tensor("g_pl", [T2, PAIRS, E], F32))
        pg = ctx.enter_context(nc.psum_tensor("g_pg", [128, 2, 512], F32))
        pb = ctx.enter_context(nc.psum_tensor("g_pb", [T2, 4, 2, C], F32))
        loaded, logits, ranked, exped_in, exped, gated, g_turned, g_copied, biased = (
            sig("loaded"), sig("logits"), sig("ranked"), sig("exped_in"), sig("exped"), sig("gated"),
            sig("g_turned"), sig("g_copied"), sig("biased"))
        dve_step = sig("dve_step")
        bc = [T2, PAIRS, E]
        with nc.Block() as block:
            @block.sync
            def _(sp):
                sp.dma_start(gw[:], k.d_gate_w).then_inc(loaded.sem, 16)
                sp.dma_start(b2[:], k.d_b2).then_inc(loaded.sem, 16)

            @block.gpsimd
            def _(pool):
                pool.iota(rank[:], [[-1, E]], base=E, channel_multiplier=0,
                          allow_small_or_imprecise_dtypes=True).then_inc(ranked.sem, 1)

            @block.tensor
            def _(pe):
                pe.wait_ge(loaded.sem, 32)
                for p in range(PAIRS):
                    for kc in range(KC):
                        ins = pe.matmul(pl[:, p, :], k.xT[:, kc, p * T2:(p + 1) * T2], gw[:, kc, :], start=kc == 0, stop=kc == KC - 1)
                ins.then_inc(logits.sem, 1)
                pe.wait_ge(gated.sem, 1)
                for p in range(PAIRS):
                    ins = pe.transpose(pg[0:E, p // 4, (p % 4) * T2:(p % 4 + 1) * T2], k.gates[:, p, :], k.ident[0:T2, 0:T2])
                ins.then_inc(g_turned.sem, 1)
                pe.wait_ge(g_copied.sem, 1)
                for p in range(PAIRS):
                    ins = pe.matmul(pb[:, p // 2, p % 2, :], GT[:, p, :], b2[:], start=True, stop=True)
                ins.then_inc(biased.sem, 1)

            @block.scalar
            def _(act):
                act.wait_ge(exped_in.sem, 1)
                act.activation(lg[:], lg[:], ACT.Exp).then_inc(exped.sem, 1)

            @block.vector
            def _(dve):
                link = Chain(dve, dve_step)
                dve.wait_ge(logits.sem, 1)
                gb = k.rows[0:T2, R_GB:R_GB + E].unsqueeze(1).to_broadcast(bc)
                link(dve.tensor_tensor(lg[:], pl[:], gb, ALU.add))
                link(dve.tensor_copy(left[:], lg[:]))
                dve.wait_ge(ranked.sem, 1)
                for r in range(TOPK):
                    link(dve.tensor_reduce(best[:], left[:], AX_X, ALU.max))
                    if r == 0:
                        link(dve.tensor_copy(top[:], best[:]))
                    link(dve.tensor_tensor(eq[:], left[:], best[:].unsqueeze(2).to_broadcast(bc), ALU.is_ge))
                    link(dve.tensor_tensor(eq[:], eq[:], rank[:].unsqueeze(1).to_broadcast(bc), ALU.mult))
                    link(dve.tensor_reduce(tie[:], eq[:], AX_X, ALU.max))
                    link(dve.tensor_tensor(eq[:], eq[:], tie[:].unsqueeze(2).to_broadcast(bc), ALU.is_equal))
                    if r == 0:
                        link(dve.tensor_copy(pick[:], eq[:]))
                    else:
                        link(dve.tensor_tensor(pick[:], pick[:], eq[:], ALU.add))
                    link(dve.scalar_tensor_tensor(left[:], eq[:], NEG, left[:], ALU.mult, ALU.add))
                link(dve.tensor_tensor(lg[:], lg[:], top[:].unsqueeze(2).to_broadcast(bc), ALU.subtract))
                dve.sem_inc(exped_in.sem, 1)
                dve.wait_ge(exped.sem, 1)
                link(dve.tensor_tensor(lg[:], lg[:], pick[:], ALU.mult))
                link(dve.tensor_reduce(best[:], lg[:], AX_X, ALU.add))
                link(dve.reciprocal(best[:], best[:]))
                dve.tensor_tensor(k.gates[:], lg[:], best[:].unsqueeze(2).to_broadcast(bc), ALU.mult).then_inc(gated.sem, 1)
                link(dve.tensor_tensor(k.x[:], k.x[:], k.xh[:], ALU.add))
                dve.wait_ge(g_turned.sem, 1)
                link(dve.tensor_copy(GT[:].rearrange("e (a p) t -> e a (p t)", a=2), pg[0:E, :, 0:4 * T2]))
                dve.sem_inc(g_copied.sem, 1)
                dve.wait_ge(biased.sem, 1)
                link(dve.tensor_tensor(k.x[:], pb[:].rearrange("t a b c -> t (a b) c"), k.x[:], ALU.add))


def expert_phase(nc, k):
    TH = 4 * T2
    NI = I // 128
    UN = 4
    NW = 2
    with Phase(nc) as ctx:
        ctx.callback(ctx.clear)

        def sb(name, shape, dt=F32):
            return ctx.enter_context(nc.sbuf_tensor(f"e_{name}", shape, dt))

        def sig(name, per_unit=1):
            return Signal(nc, ctx, f"e_{name}", UN * per_unit)

        x_hi = sb("x_hi", [128, KC, N], F32R)
        x_lo = sb("x_lo", [128, KC, N], F32R)
        w1 = [sb(f"w1_{j}", [128, KC, 2 * I]) for j in range(2)]
        w2 = [sb(f"w2_{j}", [128, NI, C]) for j in range(2)]
        b1 = sb("b1", [128, E, 2 * NI])
        w1_hi = [sb(f"w1_hi{j}", [128, KC, 2 * I], F32R) for j in range(2)]
        w1_lo = [sb(f"w1_lo{j}", [128, KC, 2 * I], F32R) for j in range(2)]
        w2_hi = [sb(f"w2_hi{j}", [128, NI, C], F32R) for j in range(2)]
        w2_lo = [sb(f"w2_lo{j}", [128, NI, C], F32R) for j in range(2)]
        a = [sb(f"a{j}", [128, TH]) for j in range(2)]
        sg = [sb(f"sg{j}", [128, TH]) for j in range(2)]
        bb = [sb(f"bb{j}", [128, TH]) for j in range(2)]
        act_f = [sb(f"act_f{j}", [128, TH]) for j in range(2)]
        act_hi = [sb(f"act_hi{j}", [128, NI, TH], F32R) for j in range(2)]
        act_lo = [sb(f"act_lo{j}", [128, NI, TH], F32R) for j in range(2)]
        ph = [ctx.enter_context(nc.psum_tensor(f"e_ph{j}", [128, TH], F32)) for j in range(2 * NI)]
        py = [ctx.enter_context(nc.psum_tensor(f"e_py{j}", [T2, 2, C], F32)) for j in range(2)]

        x_split, x_done, b_loaded, stored = sig("x_split"), sig("x_done"), sig("b_loaded"), sig("stored")
        loaded = [Signal(nc, ctx, f"e_loaded{j}", 16 * NW) for j in range(2)]
        w_hi_done, w_lo_done = Signal(nc, ctx, "e_w_hi_done", 2 * NW), Signal(nc, ctx, "e_w_lo_done", 2 * NW)
        hidden, hid_read = sig("hidden", 2 * NI), sig("hid_read", 2 * NI)
        clipped, gated, sigmoided, acted = sig("clipped", NI), sig("gated", NI), sig("sigmoided", NI), sig("acted", NI)
        act_hi_done, act_lo_done = sig("act_hi_done", NI), sig("act_lo_done", NI)
        mixed, added = sig("mixed", 2), sig("added", 2)
        pipe = Steps(E // 2, UN)
        wait, there = pipe.wait, pipe.there

        def run(eng, body):
            body(0)
            with eng.Fori(1, E // 2 - 1) as i:
                body(i)
            body(E // 2 - 1)
            body(E // 2)

        def next_expert(i, m):
            return there(i, m) and m % 2 == 0 and (not isinstance(i, int) or 2 * i + m // 2 + 1 < E)

        with nc.Block() as block:
            @block.sync
            def _(sp):
                def load(i, j):
                    e = 2 * i + j
                    sp.dma_start(w1[j][:], k.d_w1[bass.ds(e, 1)].rearrange("a p k n -> (a p) k n")).then_inc(loaded[j].sem, 16)
                    sp.dma_start(w2[j][:], k.d_w2[bass.ds(e, 1)].rearrange("a p k n -> (a p) k n")).then_inc(loaded[j].sem, 16)

                load(0, 0)
                sp.dma_start(b1[:], k.d_b1.rearrange("e p n -> p e n")).then_inc(b_loaded.sem, 16)
                load(0, 1)
                with sp.Fori(1, E // 2) as i:
                    for j in range(2):
                        sp.wait_ge(w_lo_done.sem, w_lo_done.at(i, NW * (j + 1) - 2 * NW))
                        load(i, j)
                sp.wait_ge(added.sem, added.at(E // 2, 0))
                sp.dma_start(k.d_out, k.x[:]).then_inc(stored.sem, 16)
                sp.wait_ge(stored.sem, 16)

            @block.scalar
            def _(act):
                def weights_hi(i, m):
                    j = m % 2
                    wait(act, loaded[j], i, 16 * NW * (m // 2 + 1))
                    act.activation(w1_hi[j][:], w1[j][:], ACT.Copy).then_inc(w_hi_done.sem, 1)
                    act.activation(w2_hi[j][:], w2[j][:], ACT.Copy).then_inc(w_hi_done.sem, 1)

                act.activation(x_hi[:], k.xT[:], ACT.Copy).then_inc(x_split.sem, 1)
                weights_hi(0, 0)

                def body(i):
                    for m in range(UN):
                        for t in range(NI):
                            if there(i, m):
                                n = NI * m + t
                                wait(act, hid_read, i, 2 * n + 2)
                                act.activation(sg[t][:], a[t][:], ACT.Sigmoid, scale=1.702).then_inc(sigmoided.sem, 1)
                                wait(act, acted, i, n + 1)
                                wait(act, mixed, i, 2 * (m - 1))
                                act.activation(act_hi[m % 2][:, t, :], act_f[t][:], ACT.Copy).then_inc(act_hi_done.sem, 1)
                        if next_expert(i, m):
                            wait(act, mixed, i, 2 * m)
                            weights_hi(i, m // 2 + 1)

                run(act, body)

            @block.gpsimd
            def _(pool):
                def weights_lo(i, m):
                    j = m % 2
                    for n, (raw, hi, lo) in enumerate(((w1, w1_hi, w1_lo), (w2, w2_hi, w2_lo))):
                        wait(pool, w_hi_done, i, NW * m + n + 1)
                        pool.tensor_tensor(lo[j][:], raw[j][:], hi[j][:].bitcast(F32), ALU.subtract).then_inc(w_lo_done.sem, 1)

                weights_lo(0, 0)

                def body(i):
                    for m in range(UN):
                        for t in range(NI):
                            if there(i, m):
                                n = NI * m + t
                                wait(pool, act_hi_done, i, n + 1)
                                pool.tensor_tensor(act_lo[m % 2][:, t, :], act_f[t][:],
                                                   act_hi[m % 2][:, t, :].bitcast(F32), ALU.subtract).then_inc(act_lo_done.sem, 1)
                        if next_expert(i, m):
                            weights_lo(i, m // 2 + 1)

                run(pool, body)

            @block.vector
            def _(dve):
                dve.wait_ge(x_split.sem, 1)
                dve.tensor_tensor(x_lo[:], k.xT[:], x_hi[:].bitcast(F32), ALU.subtract).then_inc(x_done.sem, 1)
                dve.wait_ge(b_loaded.sem, 16)

                def body(i):
                    def gate_part(m, t):
                        if not there(i, m):
                            return
                        n = NI * m + t
                        bias = b1[:, bass.ds(2 * i + m // 2, 1), 2 * t:2 * t + 1].rearrange("p a n -> p (a n)")
                        wait(dve, hidden, i, 2 * n + 1)
                        dve.tensor_scalar(a[t][:], ph[2 * t][:], bias, 7.0, ALU.add, ALU.min).then_inc(hid_read.sem, 1)

                    def linear_part(m, t):
                        if not there(i, m):
                            return
                        n = NI * m + t
                        bias = b1[:, bass.ds(2 * i + m // 2, 1), 2 * t + 1:2 * t + 2].rearrange("p a n -> p (a n)")
                        wait(dve, hidden, i, 2 * n + 2)
                        dve.tensor_scalar(bb[t][:], ph[2 * t + 1][:], bias, 7.0, ALU.add, ALU.min).then_inc(hid_read.sem, 1)
                        wait(dve, hid_read, i, 2 * n + 2)
                        dve.tensor_scalar(bb[t][:], bb[t][:], -7.0, 1.0, ALU.max, ALU.add).then_inc(clipped.sem, 1)
                        wait(dve, clipped, i, n + 1)
                        dve.tensor_tensor(bb[t][:], bb[t][:], a[t][:], ALU.mult).then_inc(gated.sem, 1)

                    def activate(m, t):
                        if not there(i, m):
                            return
                        n = NI * m + t
                        wait(dve, gated, i, n + 1)
                        wait(dve, sigmoided, i, n + 1)
                        wait(dve, act_lo_done, i, n - 1)
                        dve.tensor_tensor(act_f[t][:], bb[t][:], sg[t][:], ALU.mult).then_inc(acted.sem, 1)

                    def add_up(m, q):
                        if not there(i, m):
                            return
                        wait(dve, mixed, i, 2 * m + q + 1)
                        wait(dve, added, i, 2 * m + q - 3)
                        for p2 in range(2):
                            p = 4 * (m % 2) + 2 * q + p2
                            ins = dve.scalar_tensor_tensor(k.x[:, p, :], py[q][:, p2, :],
                                                           k.gates[:, p, bass.ds(2 * i + m // 2, 1)], k.x[:, p, :],
                                                           ALU.mult, ALU.add)
                        ins.then_inc(added.sem, 1)

                    for m in range(UN):
                        gate_part(m, 0)
                        linear_part(m, 0)
                        activate(m, 0)
                        gate_part(m, 1)
                        linear_part(m, 1)
                        activate(m, 1)
                        add_up(m - 1, 0)
                        add_up(m - 1, 1)

                run(dve, body)

            @block.tensor
            def _(pe):
                pe.wait_ge(x_done.sem, 1)

                def body(i):
                    def hidden_layer(m):
                        if not there(i, m):
                            return
                        j, th = m // 2, m % 2
                        if th == 0:
                            wait(pe, w_lo_done, i, NW * (j + 1))
                        for t in range(2 * NI):
                            wait(pe, hid_read, i, 2 * NI * (m - 1) + t + 1)
                            at = (t % 2) * I + (t // 2) * 128
                            terms = [(w, x, kc) for kc in range(KC)
                                     for w, x in ((w1_hi, x_hi), (w1_hi, x_lo), (w1_lo, x_hi))]
                            for n, (w, x, kc) in enumerate(terms):
                                ins = pe.matmul(ph[t][:], w[j][:, kc, at:at + 128], x[:, kc, th * TH:(th + 1) * TH],
                                                start=n == 0, stop=n == len(terms) - 1)
                            ins.then_inc(hidden.sem, 1)

                    def output_layer(m):
                        if not there(i, m):
                            return
                        wait(pe, act_lo_done, i, NI * (m + 1))
                        for q in range(2):
                            wait(pe, added, i, 2 * m + q - 1)
                            for p2 in range(2):
                                at = slice((2 * q + p2) * T2, (2 * q + p2 + 1) * T2)
                                terms = [(x, w, t) for t in range(NI)
                                         for x, w in ((act_hi, w2_hi), (act_hi, w2_lo), (act_lo, w2_hi))]
                                for n, (x, w, t) in enumerate(terms):
                                    ins = pe.matmul(py[q][:, p2, :], x[m % 2][:, t, at], w[m // 2 % 2][:, t, :],
                                                    start=n == 0, stop=n == len(terms) - 1)
                            ins.then_inc(mixed.sem, 1)

                    for m in range(UN):
                        hidden_layer(m)
                        output_layer(m - 1)

                run(pe, body)


class Shared:
    pass


def decoder_layer(nc, d, out):
    k = Shared()
    k.d_attn_w, k.d_attn_wo, k.d_xattn_w = d["attn_w"], d["attn_wo"], d["xattn_w"]
    k.d_ctx, k.d_ctxT, k.d_ctx_wk, k.d_ctx_wv = d["ctx"], d["ctxT"], d["ctx_wk"], d["ctx_wv"]
    k.d_proj_w, k.d_gate_w, k.d_b2, k.d_w1, k.d_w2, k.d_b1 = d["proj_w"], d["gate_w"], d["b2"], d["w1"], d["w2"], d["b1"]
    k.d_out = out.rearrange("(p b) s c -> (b s) p c", b=2)
    k.d_qhi = nc.dram_tensor("context_queries_hi", [B, 128, NH, S], F32, kind="Internal").ap()
    k.d_qlo = nc.dram_tensor("context_queries_lo", [B, 128, NH, S], F32, kind="Internal").ap()
    k.d_qb = nc.dram_tensor("context_offsets", [B, HPG * S, G], F32, kind="Internal").ap()
    k.d_core = nc.dram_tensor("core_quantised", [PAIRS, 128, NH, T2], BF16, kind="Internal").ap()
    k.d_xout = nc.dram_tensor("xout_quantised", [B, 128, NH, S], BF16, kind="Internal").ap()
    with ExitStack() as ctx:
        def sb(name, shape, dt=F32):
            return ctx.enter_context(nc.sbuf_tensor(name, shape, dt))

        k.x = sb("x", [T2, PAIRS, C])
        k.ident = sb("ident", [128, 128])
        k.vec = sb("vec", [128, NV])
        k.rsm = sb("rsm", [128, 2 * NH])
        with ExitStack() as first:
            k.rows = first.enter_context(nc.sbuf_tensor("rows", [128, NR], F32))
            k.cos = first.enter_context(nc.sbuf_tensor("cos", [T2, D], F32))
            k.sin = first.enter_context(nc.sbuf_tensor("sin", [T2, D], F32))
            k.cmask = first.enter_context(nc.sbuf_tensor("cmask", [T2, T2], F32))
            k.xT = first.enter_context(nc.sbuf_tensor("xT_a", [128, KC, N], F32))
            loaded = first.enter_context(nc.semaphore("loaded"))
            smoothed = first.enter_context(nc.semaphore("smoothed"))
            id_zero = first.enter_context(nc.semaphore("id_zero"))
            with nc.Block() as block:
                @block.sync
                def _(sp):
                    sp.dma_start(k.x[:], d["x"].rearrange("(p b) s c -> (b s) p c", b=2)).then_inc(loaded, 16)
                    sp.dma_start(k.vec[:], d["vec"]).then_inc(loaded, 16)
                    sp.dma_start(k.rows[:], d["rows"].to_broadcast([128, NR])).then_inc(loaded, 16)
                    sp.dma_start(k.cos[:], d["cos"]).then_inc(loaded, 16)
                    sp.dma_start(k.sin[:], d["sin"]).then_inc(loaded, 16)
                    sp.dma_start(k.cmask[:], d["cmask"]).then_inc(loaded, 16)
                    sp.wait_ge(loaded, 96)

                @block.gpsimd
                def _(pool):
                    pool.memset(k.ident[:], 0.0).then_inc(id_zero, 1)
                    pool.wait_ge(id_zero, 1)
                    pool.affine_select(out=k.ident[:], in_=k.ident[:], compare_op=ALU.not_equal, fill=1.0, base=0,
                                       pattern=[[-1, 128]], channel_multiplier=1).then_inc(id_zero, 1)
                    pool.wait_ge(id_zero, 2)

                @block.vector
                def _(dve):
                    dve.wait_ge(loaded, 96)
                    dve.reciprocal(k.rsm[:], k.vec[:, V_SM:V_SM + 2 * NH]).then_inc(smoothed, 1)
                    dve.wait_ge(smoothed, 1)
            normalise_phase(nc, k, "attn")
            attention_phase(nc, k)
        with ExitStack() as second:
            k.xq = second.enter_context(nc.sbuf_tensor("xq", [128, 4, KC, N], BF16))
            k.bmask = second.enter_context(nc.sbuf_tensor("bmask", [T2, T2], F32))
            bm = second.enter_context(nc.semaphore("bmask_loaded"))
            with nc.Block() as block:
                @block.sync
                def _(sp):
                    sp.dma_start(k.bmask[:], d["bmask"]).then_inc(bm, 16)
                    sp.wait_ge(bm, 16)
            normalise_phase(nc, k, "xattn")
            xattn_phase(nc, k)
        with ExitStack() as third:
            k.c_wraw = third.enter_context(nc.sbuf_tensor("c_wraw", [128, KC, G * D], F32))
            context_phase(nc, k)
        project_phase(nc, k)
        with ExitStack() as fourth:
            k.xh = fourth.enter_context(nc.sbuf_tensor("xh", [T2, PAIRS, C], F32))
            k.xT = fourth.enter_context(nc.sbuf_tensor("xT_f", [128, KC, N], F32))
            k.rows = fourth.enter_context(nc.sbuf_tensor("rows_f", [128, NR], F32))
            k.gates = fourth.enter_context(nc.sbuf_tensor("gates", [T2, PAIRS, E], F32))
            rl = fourth.enter_context(nc.semaphore("rows_loaded"))
            with nc.Block() as block:
                @block.sync
                def _(sp):
                    sp.dma_start(k.rows[:, R_GB:R_GB + E], d["rows"][:, R_GB:R_GB + E].to_broadcast([128, E])).then_inc(rl, 16)
                    sp.wait_ge(rl, 16)
            normalise_phase(nc, k, "ffn")
            gate_phase(nc, k)
            expert_phase(nc, k)


def _per_head(w):
    return w.reshape(w.shape[0], KC, 128, D).transpose(2, 0, 1, 3)


def _chunk(w, h0):
    return w[:, h0:h0 + 4].transpose(0, 2, 1, 3).reshape(128, KC, CH)


def _rope():
    inv = 1.0 / np.float32(10000.0) ** (np.arange(0, D, 2, dtype=np.float32) / np.float32(D))
    f = (np.arange(S, dtype=np.float32)[:, None] * inv[None, :].astype(np.float32)).astype(np.float32)
    cos, sin = np.cos(f).astype(np.float32), np.sin(f).astype(np.float32)
    cos = np.tile(np.repeat(cos, 2, axis=1), (2, 1))
    sin = np.tile(np.concatenate([sin, -sin], axis=1), (2, 1))
    return cos, sin


def _masks():
    b = np.arange(T2) // S
    same = b[:, None] == b[None, :]
    causal = same & (np.arange(T2)[:, None] >= np.arange(T2)[None, :])
    return (causal * np.float32(1.0 / np.float32(np.sqrt(D)))).astype(np.float32), np.where(same, 0.0, NEG).astype(np.float32)


def kernel(**inputs):
    import concourse.bacc as _bacc
    from concourse.bass_utils import run_bass_kernel_spmd as _run

    f = {n: np.asarray(a) for n, a in inputs.items()}
    at = {n[len("L0_attn_"):]: a for n, a in f.items() if n.startswith("L0_attn_")}
    xa = {n[len("L0_xattn_"):]: a for n, a in f.items() if n.startswith("L0_xattn_")}
    ff = {n[len("L0_ffn_"):]: a for n, a in f.items() if n.startswith("L0_ffn_")}

    q, kk, v = (_per_head(at[n]) for n in ("W_Q", "W_K", "W_V"))
    attn_w = np.stack([np.stack([_chunk(w, 8 * h + 4 * c) for w in (q, kk, v) for c in range(2)]) for h in range(2)])

    def heads(w):
        return _per_head(w.reshape(-1, D, C).transpose(0, 2, 1))

    wq, wk, wqx, wv = (heads(xa[n]) for n in ("wq", "wk", "wqx", "wv"))
    xattn_w = np.stack([np.stack([_chunk(wq, 8 * h), _chunk(wq, 8 * h + 4), _chunk(wk, 4 * h),
                                  _chunk(wqx, 8 * h), _chunk(wqx, 8 * h + 4), _chunk(wv, 4 * h)]) for h in range(2)])
    kvx = heads(xa["w_kv_x"]).transpose(0, 2, 1, 3)

    def col(a):
        return a.reshape(-1, 128).T

    def one(a):
        return np.broadcast_to(a.reshape(1, 1), (128, 1))

    vec = np.concatenate(
        [col(xa["ln_w"]), col(xa["ln_b"]), col(xa["q_in_scale"]), col(xa["k_in_scale"]), col(xa["qx_in_scale"]),
         col(xa["v_in_scale"]), col(ff["norm_w"])]
        + [col(xa[n]) for n in ("qln_w", "qln_b", "kln_w", "kln_b", "qxln_w", "qxln_b", "kxln_w", "kxln_b")]
        + [one(xa[n]) for n in ("wq_scale", "wk_scale", "wqx_scale", "wv_scale", "proj_w_scale", "proj_in_scale")]
        + [col(xa["proj_smooth"])], axis=1)
    rows = np.concatenate([at[n][8 * h:8 * h + 8].reshape(-1) for h in range(2) for n in ("b_Q", "b_K", "b_V")]
                          + [at["b_O"], ff["gate_b"]]).reshape(1, -1)
    cos, sin = _rope()
    cmask, bmask = _masks()
    ctx = f["ctx_2048"]
    w1 = ff["w1"].reshape(E, I, 2, C).transpose(0, 3, 2, 1).reshape(E, KC, 128, 2 * I).transpose(0, 2, 1, 3)
    b1 = ff["b1"].reshape(E, I // 128, 128, 2).transpose(0, 2, 1, 3).reshape(E, 128, 2 * (I // 128))
    w2 = ff["w2"].transpose(0, 2, 1).reshape(E, I // 128, 128, C).transpose(0, 2, 1, 3)
    arrays = {
        "x": f["x"], "attn_w": attn_w, "attn_wo": at["W_O"].transpose(1, 0, 2), "xattn_w": xattn_w,
        "ctx": ctx.reshape(B, NT_C, TT_C, C).transpose(0, 2, 1, 3),
        "ctxT": ctx.transpose(0, 2, 1).reshape(B, KC, 128, SC),
        "ctx_wk": kvx[:, :, 0:G].reshape(128, KC, G * D), "ctx_wv": kvx[:, :, G:2 * G].reshape(128, KC, G * D),
        "proj_w": xa["wproj"].T.reshape(2 * NH, 128, C).transpose(1, 0, 2),
        "gate_w": ff["gate_w"].T.reshape(KC, 128, E).transpose(1, 0, 2), "b2": ff["b2"],
        "w1": w1, "w2": w2, "b1": b1, "vec": vec, "rows": rows, "cos": cos, "sin": sin, "cmask": cmask, "bmask": bmask,
    }
    arrays = {n: np.ascontiguousarray(a) for n, a in arrays.items()}
    nc = _bacc.Bacc("TRN2", target_bir_lowering=False, num_devices=1)
    d = {n: nc.dram_tensor(n + "_dram", a.shape, mybir.dt.from_np(a.dtype), kind="ExternalInput").ap()
         for n, a in arrays.items()}
    out = nc.dram_tensor("out_dram", (B, S, C), F32, kind="ExternalOutput").ap()
    decoder_layer(nc, d, out)
    r = _run(nc, [{n + "_dram": a for n, a in arrays.items()}], core_ids=[0])
    return r.results[0]["out_dram"]
```
